# Optimizing a Trainium2 kernel written in Bass

```python
import numpy as np
import jax
import jax.numpy as jnp

def _softmax(x, axis=-1):
    return jax.nn.softmax(x, axis=axis)

def _gelu(x):
    return jax.nn.gelu(x, approximate=True)

def _silu(x):
    return jax.nn.silu(x)

def _sigmoid(x):
    return jax.nn.sigmoid(x)

def _layernorm(x, axis=-1, eps=1e-05):
    m = jnp.mean(x, axis=axis, keepdims=True)
    v = jnp.var(x, axis=axis, keepdims=True)
    return (x - m) / jnp.sqrt(v + eps)

def _scatter_add(tgt, idx, src, axis=0):
    return tgt.at[idx].add(src)

def _segment_sum(src, seg, n):
    return jax.ops.segment_sum(src, seg, n)
kernel_name = 'mk_cond_seq_d4_seqx_r4_11be6b'

def setup_inputs(seed: int=0):
    np.random.seed(seed)
    _w = jnp.asarray

    def _rec_inputs():
        import jax
        import jax.numpy as jnp
        _rk = jax.random.key(seed)
        x = -0.0003482 + 1 * jax.random.normal(jax.random.fold_in(_rk, 1), (16, 256, 288), jnp.float32)
        _lenS = 256 - jax.random.randint(jax.random.fold_in(_rk, 7), (16,), 0, max(1, 256 // 4) + 1, jnp.int32)
        _lenS2 = 256 - jax.random.randint(jax.random.fold_in(_rk, 8), (16,), 0, max(1, 256 // 4) + 1, jnp.int32)
        cond_1152 = 0.00257642 + 1.0011 * jax.random.normal(jax.random.fold_in(_rk, 11), (16, 288), jnp.float32)
        return (x, cond_1152)
    x, cond_1152 = _rec_inputs()

    def _L0_cond_setup():
        import jax, jax.numpy as jnp
        import numpy as np
        from jax.scipy.linalg import expm
        N, D, COND_DIM = (288, 64, 288)
        B, T = (16, 256)

        def _rotation(cond, W, b):
            v = jax.nn.silu(cond) @ W.T + b
            iu, ju = jnp.triu_indices(D, k=1)
            A = jnp.zeros((cond.shape[0], D, D), dtype=v.dtype)
            A = A.at[:, iu, ju].set(v).at[:, ju, iu].set(-v)
            return expm(A)
        key = jax.random.key(seed)
        k1, k2, k3, k4, k5 = jax.random.split(key, 5)
        x = jax.random.normal(k1, (B, T, N), dtype=jnp.float32)
        cond = jax.random.normal(k2, (B, COND_DIM), dtype=jnp.float32)
        P = jax.random.normal(k3, (N, D), dtype=jnp.float32)
        n_skew = D * (D - 1) // 2
        bound = 1.0 / np.sqrt(COND_DIM)
        W = jax.random.uniform(k4, (n_skew, COND_DIM), minval=-bound, maxval=bound, dtype=jnp.float32)
        b = jax.random.uniform(k5, (n_skew,), minval=-bound, maxval=bound, dtype=jnp.float32)
        return {'x': x, 'cond': cond, 'P': P, 'W': W, 'b': b}
    _L0_cond_all = _L0_cond_setup()
    _L0_cond_in = {k: v for k, v in _L0_cond_all.items() if k in ('P', 'W', 'b')}
    del _L0_cond_all

    def _L1_cond_setup():
        import jax, jax.numpy as jnp
        import numpy as np
        B, L, C = (8, 256, 288)
        H = 16
        D = C // H
        FF = int(C * 4.0)
        EPS = 1e-06

        def _layernorm(x):
            mu = jnp.mean(x, axis=-1, keepdims=True)
            var = jnp.mean(jnp.square(x - mu), axis=-1, keepdims=True)
            return (x - mu) * jax.lax.rsqrt(var + EPS)

        def _modulate(x, shift, scale):
            return x * (1.0 + scale) + shift

        def _attention(h, W_qkv, b_qkv, W_proj, b_proj):
            b, l, c = h.shape
            qkv = h @ W_qkv + b_qkv
            qkv = qkv.reshape(b, l, 3, H, D)
            q, k, v = (qkv[:, :, 0], qkv[:, :, 1], qkv[:, :, 2])
            scale = D ** (-0.5)
            scores = jnp.einsum('blhd,bmhd->bhlm', q * scale, k)
            attn = jax.nn.softmax(scores, axis=-1)
            o = jnp.einsum('bhlm,bmhd->blhd', attn, v).reshape(b, l, c)
            return o @ W_proj + b_proj
        key = jax.random.key(seed)
        ks = jax.random.split(key, 12)
        s = 0.02
        return {'x': jax.random.normal(ks[0], (B, L, C), jnp.float32), 'c': jax.random.normal(ks[1], (B, 1, C), jnp.float32), 'W_qkv': jax.random.normal(ks[2], (C, 3 * C), jnp.float32) * s, 'b_qkv': jnp.zeros((3 * C,), jnp.float32), 'W_proj': jax.random.normal(ks[3], (C, C), jnp.float32) * s, 'b_proj': jnp.zeros((C,), jnp.float32), 'W_fc1': jax.random.normal(ks[4], (C, FF), jnp.float32) * s, 'b_fc1': jnp.zeros((FF,), jnp.float32), 'W_fc2': jax.random.normal(ks[5], (FF, C), jnp.float32) * s, 'b_fc2': jnp.zeros((C,), jnp.float32), 'W_ada': jax.random.normal(ks[6], (C, 6 * C), jnp.float32) * s, 'b_ada': jnp.zeros((6 * C,), jnp.float32)}
    _L1_cond_all = _L1_cond_setup()
    _L1_cond_in = {k: v for k, v in _L1_cond_all.items() if k in ('W_qkv', 'b_qkv', 'W_proj', 'b_proj', 'W_fc1', 'b_fc1', 'W_fc2', 'b_fc2', 'W_ada', 'b_ada')}
    del _L1_cond_all

    def _L2_cond_setup():
        import math
        import jax, jax.numpy as jnp
        import numpy as np
        B, T, D = (8, 256, 288)
        H = 16
        E = 4
        EPS = 1e-06

        def _layer_norm(x):
            mu = jnp.mean(x, axis=-1, keepdims=True)
            var = jnp.mean(jnp.square(x - mu), axis=-1, keepdims=True)
            return (x - mu) * jax.lax.rsqrt(var + EPS)

        def _modulate(x, shift, scale):
            return x * (1.0 + scale) + shift

        def _attention(y, qkv_w, qkv_b, out_w, out_b):
            b, t, d = y.shape
            hd = d // H
            qkv = y @ qkv_w + qkv_b
            q, k, v = jnp.split(qkv, 3, axis=-1)
            q = q.reshape(b, t, H, hd).transpose(0, 2, 1, 3)
            k = k.reshape(b, t, H, hd).transpose(0, 2, 1, 3)
            v = v.reshape(b, t, H, hd).transpose(0, 2, 1, 3)
            scores = jnp.einsum('bhqd,bhkd->bhqk', q, k) / math.sqrt(hd)
            attn = jax.nn.softmax(scores, axis=-1)
            out = jnp.einsum('bhqk,bhkd->bhqd', attn, v)
            out = out.transpose(0, 2, 1, 3).reshape(b, t, d)
            return out @ out_w + out_b
        key = jax.random.key(seed)
        ks = jax.random.split(key, 12)
        std = 0.02
        return {'x': jax.random.normal(ks[0], (B, T, D), dtype=jnp.float32), 'c': jax.random.normal(ks[1], (B, D), dtype=jnp.float32), 'qkv_w': jax.random.normal(ks[2], (D, 3 * D), dtype=jnp.float32) * std, 'qkv_b': jnp.zeros((3 * D,), dtype=jnp.float32), 'out_w': jax.random.normal(ks[3], (D, D), dtype=jnp.float32) * std, 'out_b': jnp.zeros((D,), dtype=jnp.float32), 'w1': jax.random.normal(ks[4], (D, E * D), dtype=jnp.float32) * std, 'b1': jnp.zeros((E * D,), dtype=jnp.float32), 'w2': jax.random.normal(ks[5], (E * D, D), dtype=jnp.float32) * std, 'b2': jnp.zeros((D,), dtype=jnp.float32), 'ada_w': jax.random.normal(ks[6], (D, 6 * D), dtype=jnp.float32) * std, 'ada_b': jnp.zeros((6 * D,), dtype=jnp.float32)}
    _L2_cond_all = _L2_cond_setup()
    _L2_cond_in = {k: v for k, v in _L2_cond_all.items() if k in ('qkv_w', 'qkv_b', 'out_w', 'out_b', 'w1', 'b1', 'w2', 'b2', 'ada_w', 'ada_b')}
    del _L2_cond_all

    def _L3_cond_setup():
        import jax, jax.numpy as jnp
        import numpy as np
        B, N, D = (8, 256, 288)
        H = 16
        HD = D // H
        HID = 4 * D
        EPS = 1e-06

        def _ln(x):
            mu = jnp.mean(x, axis=-1, keepdims=True)
            var = jnp.mean(jnp.square(x - mu), axis=-1, keepdims=True)
            return (x - mu) * jax.lax.rsqrt(var + EPS)

        def _modulate(x, shift, scale):
            return x * (1.0 + scale[:, None, :]) + shift[:, None, :]

        def _attn(x, w_qkv, b_qkv, w_proj, b_proj):
            b, n, d = x.shape
            qkv = (x @ w_qkv + b_qkv).reshape(b, n, 3, H, HD)
            q = qkv[:, :, 0].transpose(0, 2, 1, 3)
            k = qkv[:, :, 1].transpose(0, 2, 1, 3)
            v = qkv[:, :, 2].transpose(0, 2, 1, 3)
            scores = jnp.einsum('bhnd,bhmd->bhnm', q, k) * HD ** (-0.5)
            attn = jax.nn.softmax(scores, axis=-1)
            out = jnp.einsum('bhnm,bhmd->bhnd', attn, v)
            out = out.transpose(0, 2, 1, 3).reshape(b, n, d)
            return out @ w_proj + b_proj
        key = jax.random.key(seed)
        ks = jax.random.split(key, 12)
        s = 0.02
        return {'x': jax.random.normal(ks[0], (B, N, D), jnp.float32), 't_emb': jax.random.normal(ks[1], (B, D), jnp.float32), 'w_qkv': jax.random.normal(ks[2], (D, 3 * D), jnp.float32) * s, 'b_qkv': jax.random.normal(ks[3], (3 * D,), jnp.float32) * s, 'w_proj': jax.random.normal(ks[4], (D, D), jnp.float32) * s, 'b_proj': jax.random.normal(ks[5], (D,), jnp.float32) * s, 'w_fc1': jax.random.normal(ks[6], (D, HID), jnp.float32) * s, 'b_fc1': jax.random.normal(ks[7], (HID,), jnp.float32) * s, 'w_fc2': jax.random.normal(ks[8], (HID, D), jnp.float32) * s, 'b_fc2': jax.random.normal(ks[9], (D,), jnp.float32) * s, 'w_ada': jax.random.normal(ks[10], (D, 6 * D), jnp.float32) * s, 'b_ada': jax.random.normal(ks[11], (6 * D,), jnp.float32) * s}
    _L3_cond_all = _L3_cond_setup()
    _L3_cond_in = {k: v for k, v in _L3_cond_all.items() if k in ('w_qkv', 'b_qkv', 'w_proj', 'b_proj', 'w_fc1', 'b_fc1', 'w_fc2', 'b_fc2', 'w_ada', 'b_ada')}
    del _L3_cond_all
    return {'x': x, 'cond_1152': cond_1152, 'L0_cond_P': _L0_cond_in['P'], 'L0_cond_W': _L0_cond_in['W'], 'L0_cond_b': _L0_cond_in['b'], 'L1_cond_W_qkv': _L1_cond_in['W_qkv'], 'L1_cond_b_qkv': _L1_cond_in['b_qkv'], 'L1_cond_W_proj': _L1_cond_in['W_proj'], 'L1_cond_b_proj': _L1_cond_in['b_proj'], 'L1_cond_W_fc1': _L1_cond_in['W_fc1'], 'L1_cond_b_fc1': _L1_cond_in['b_fc1'], 'L1_cond_W_fc2': _L1_cond_in['W_fc2'], 'L1_cond_b_fc2': _L1_cond_in['b_fc2'], 'L1_cond_W_ada': _L1_cond_in['W_ada'], 'L1_cond_b_ada': _L1_cond_in['b_ada'], 'L2_cond_qkv_w': _L2_cond_in['qkv_w'], 'L2_cond_qkv_b': _L2_cond_in['qkv_b'], 'L2_cond_out_w': _L2_cond_in['out_w'], 'L2_cond_out_b': _L2_cond_in['out_b'], 'L2_cond_w1': _L2_cond_in['w1'], 'L2_cond_b1': _L2_cond_in['b1'], 'L2_cond_w2': _L2_cond_in['w2'], 'L2_cond_b2': _L2_cond_in['b2'], 'L2_cond_ada_w': _L2_cond_in['ada_w'], 'L2_cond_ada_b': _L2_cond_in['ada_b'], 'L3_cond_w_qkv': _L3_cond_in['w_qkv'], 'L3_cond_b_qkv': _L3_cond_in['b_qkv'], 'L3_cond_w_proj': _L3_cond_in['w_proj'], 'L3_cond_b_proj': _L3_cond_in['b_proj'], 'L3_cond_w_fc1': _L3_cond_in['w_fc1'], 'L3_cond_b_fc1': _L3_cond_in['b_fc1'], 'L3_cond_w_fc2': _L3_cond_in['w_fc2'], 'L3_cond_b_fc2': _L3_cond_in['b_fc2'], 'L3_cond_w_ada': _L3_cond_in['w_ada'], 'L3_cond_b_ada': _L3_cond_in['b_ada']}

def reference(x, cond_1152, L0_cond_P, L0_cond_W, L0_cond_b, L1_cond_W_qkv, L1_cond_b_qkv, L1_cond_W_proj, L1_cond_b_proj, L1_cond_W_fc1, L1_cond_b_fc1, L1_cond_W_fc2, L1_cond_b_fc2, L1_cond_W_ada, L1_cond_b_ada, L2_cond_qkv_w, L2_cond_qkv_b, L2_cond_out_w, L2_cond_out_b, L2_cond_w1, L2_cond_b1, L2_cond_w2, L2_cond_b2, L2_cond_ada_w, L2_cond_ada_b, L3_cond_w_qkv, L3_cond_b_qkv, L3_cond_w_proj, L3_cond_b_proj, L3_cond_w_fc1, L3_cond_b_fc1, L3_cond_w_fc2, L3_cond_b_fc2, L3_cond_w_ada, L3_cond_b_ada):
    import jax
    import jax.numpy as jnp

    def _L0_cond_ref(x, cond, P, W, b):
        import jax, jax.numpy as jnp
        import numpy as np
        from jax.scipy.linalg import expm
        N, D, COND_DIM = (288, 64, 288)
        B, T = (16, 256)

        def _rotation(cond, W, b):
            v = jax.nn.silu(cond) @ W.T + b
            iu, ju = jnp.triu_indices(D, k=1)
            A = jnp.zeros((cond.shape[0], D, D), dtype=v.dtype)
            A = A.at[:, iu, ju].set(v).at[:, ju, iu].set(-v)
            return expm(A)
        U, _ = jnp.linalg.qr(P)
        R = _rotation(cond, W, b)
        z = jnp.einsum('btn,nd->btd', x, U)
        z_rot = jnp.einsum('btd,bde->bte', z, R)
        x_rot = x + jnp.einsum('btd,nd->btn', z_rot - z, U)
        return x_rot

    def _L1_cond_ref(x, c, W_qkv, b_qkv, W_proj, b_proj, W_fc1, b_fc1, W_fc2, b_fc2, W_ada, b_ada):
        import jax, jax.numpy as jnp
        import numpy as np
        B, L, C = (8, 256, 288)
        H = 16
        D = C // H
        FF = int(C * 4.0)
        EPS = 1e-06

        def _layernorm(x):
            mu = jnp.mean(x, axis=-1, keepdims=True)
            var = jnp.mean(jnp.square(x - mu), axis=-1, keepdims=True)
            return (x - mu) * jax.lax.rsqrt(var + EPS)

        def _modulate(x, shift, scale):
            return x * (1.0 + scale) + shift

        def _attention(h, W_qkv, b_qkv, W_proj, b_proj):
            b, l, c = h.shape
            qkv = h @ W_qkv + b_qkv
            qkv = qkv.reshape(b, l, 3, H, D)
            q, k, v = (qkv[:, :, 0], qkv[:, :, 1], qkv[:, :, 2])
            scale = D ** (-0.5)
            scores = jnp.einsum('blhd,bmhd->bhlm', q * scale, k)
            attn = jax.nn.softmax(scores, axis=-1)
            o = jnp.einsum('bhlm,bmhd->blhd', attn, v).reshape(b, l, c)
            return o @ W_proj + b_proj
        ada = jax.nn.silu(c) @ W_ada + b_ada
        shift_msa, scale_msa, gate_msa, shift_mlp, scale_mlp, gate_mlp = jnp.split(ada, 6, axis=-1)
        h = _modulate(_layernorm(x), shift_msa, scale_msa)
        x = x + gate_msa * _attention(h, W_qkv, b_qkv, W_proj, b_proj)
        h = _modulate(_layernorm(x), shift_mlp, scale_mlp)
        mlp = jax.nn.gelu(h @ W_fc1 + b_fc1, approximate=True) @ W_fc2 + b_fc2
        x = x + gate_mlp * mlp
        return x

    def _L2_cond_ref(x, c, qkv_w, qkv_b, out_w, out_b, w1, b1, w2, b2, ada_w, ada_b):
        import math
        import jax, jax.numpy as jnp
        import numpy as np
        B, T, D = (8, 256, 288)
        H = 16
        E = 4
        EPS = 1e-06

        def _layer_norm(x):
            mu = jnp.mean(x, axis=-1, keepdims=True)
            var = jnp.mean(jnp.square(x - mu), axis=-1, keepdims=True)
            return (x - mu) * jax.lax.rsqrt(var + EPS)

        def _modulate(x, shift, scale):
            return x * (1.0 + scale) + shift

        def _attention(y, qkv_w, qkv_b, out_w, out_b):
            b, t, d = y.shape
            hd = d // H
            qkv = y @ qkv_w + qkv_b
            q, k, v = jnp.split(qkv, 3, axis=-1)
            q = q.reshape(b, t, H, hd).transpose(0, 2, 1, 3)
            k = k.reshape(b, t, H, hd).transpose(0, 2, 1, 3)
            v = v.reshape(b, t, H, hd).transpose(0, 2, 1, 3)
            scores = jnp.einsum('bhqd,bhkd->bhqk', q, k) / math.sqrt(hd)
            attn = jax.nn.softmax(scores, axis=-1)
            out = jnp.einsum('bhqk,bhkd->bhqd', attn, v)
            out = out.transpose(0, 2, 1, 3).reshape(b, t, d)
            return out @ out_w + out_b
        mods = (jax.nn.silu(c) @ ada_w + ada_b)[:, None, :]
        m0, m1, m2, m3, m4, m5 = jnp.split(mods, 6, axis=-1)
        y = _modulate(_layer_norm(x), m0, m1)
        x = x + m2 * _attention(y, qkv_w, qkv_b, out_w, out_b)
        y = _modulate(_layer_norm(x), m3, m4)
        y = jax.nn.gelu(y @ w1 + b1, approximate=True)
        x = x + m5 * (y @ w2 + b2)
        return x

    def _L3_cond_ref(x, t_emb, w_qkv, b_qkv, w_proj, b_proj, w_fc1, b_fc1, w_fc2, b_fc2, w_ada, b_ada):
        import jax, jax.numpy as jnp
        import numpy as np
        B, N, D = (8, 256, 288)
        H = 16
        HD = D // H
        HID = 4 * D
        EPS = 1e-06

        def _ln(x):
            mu = jnp.mean(x, axis=-1, keepdims=True)
            var = jnp.mean(jnp.square(x - mu), axis=-1, keepdims=True)
            return (x - mu) * jax.lax.rsqrt(var + EPS)

        def _modulate(x, shift, scale):
            return x * (1.0 + scale[:, None, :]) + shift[:, None, :]

        def _attn(x, w_qkv, b_qkv, w_proj, b_proj):
            b, n, d = x.shape
            qkv = (x @ w_qkv + b_qkv).reshape(b, n, 3, H, HD)
            q = qkv[:, :, 0].transpose(0, 2, 1, 3)
            k = qkv[:, :, 1].transpose(0, 2, 1, 3)
            v = qkv[:, :, 2].transpose(0, 2, 1, 3)
            scores = jnp.einsum('bhnd,bhmd->bhnm', q, k) * HD ** (-0.5)
            attn = jax.nn.softmax(scores, axis=-1)
            out = jnp.einsum('bhnm,bhmd->bhnd', attn, v)
            out = out.transpose(0, 2, 1, 3).reshape(b, n, d)
            return out @ w_proj + b_proj
        ada = jax.nn.silu(t_emb) @ w_ada + b_ada
        shift_a, scale_a, gate_a, shift_f, scale_f, gate_f = jnp.split(ada, 6, axis=-1)
        x = x + gate_a[:, None, :] * _attn(_modulate(_ln(x), shift_a, scale_a), w_qkv, b_qkv, w_proj, b_proj)
        h = _modulate(_ln(x), shift_f, scale_f)
        h = jax.nn.gelu(h @ w_fc1 + b_fc1, approximate=True) @ w_fc2 + b_fc2
        return x + gate_f[:, None, :] * h
    x = _L0_cond_ref(x, cond_1152, L0_cond_P, L0_cond_W, L0_cond_b)
    x = _L1_cond_ref(x, cond_1152[:, None, :], L1_cond_W_qkv, L1_cond_b_qkv, L1_cond_W_proj, L1_cond_b_proj, L1_cond_W_fc1, L1_cond_b_fc1, L1_cond_W_fc2, L1_cond_b_fc2, L1_cond_W_ada, L1_cond_b_ada)
    x = _L2_cond_ref(x, cond_1152, L2_cond_qkv_w, L2_cond_qkv_b, L2_cond_out_w, L2_cond_out_b, L2_cond_w1, L2_cond_b1, L2_cond_w2, L2_cond_b2, L2_cond_ada_w, L2_cond_ada_b)
    x = _L3_cond_ref(x, cond_1152, L3_cond_w_qkv, L3_cond_b_qkv, L3_cond_w_proj, L3_cond_b_proj, L3_cond_w_fc1, L3_cond_b_fc1, L3_cond_w_fc2, L3_cond_b_fc2, L3_cond_w_ada, L3_cond_b_ada)
    return x

_drawn_inputs = setup_inputs


def setup_inputs(seed=0):
    import zlib

    import numpy as np

    out = dict(_drawn_inputs(seed))
    spreads = {'L1_cond_b_qkv': (0.0, 0.8),
     'L1_cond_b_proj': (0.0, 0.354),
     'L1_cond_b_fc1': (0.0, 0.8),
     'L1_cond_b_fc2': (0.0, 0.364),
     'L1_cond_b_ada': (0.0, 0.379),
     'L2_cond_qkv_b': (0.0, 0.8),
     'L2_cond_out_b': (0.0, 0.356),
     'L2_cond_b1': (0.0, 0.8),
     'L2_cond_b2': (0.0, 0.371),
     'L2_cond_ada_b': (0.0, 0.375)}
    factors = {'L1_cond_W_qkv': 8.0,
     'L1_cond_W_proj': 5.486,
     'L2_cond_qkv_w': 8.0,
     'L2_cond_out_w': 6.164,
     'L3_cond_w_qkv': 8.0,
     'L3_cond_b_qkv': 8.0,
     'L3_cond_w_proj': 8.0,
     'L3_cond_b_proj': 46.444,
     'L3_cond_b_fc1': 64.0,
     'L3_cond_b_fc2': 44.997,
     'L3_cond_b_ada': 8.0,
     'L3_cond_w_fc1': 7.054,
     'L3_cond_w_fc2': 6.225}
    for name, (base, spread) in spreads.items():
        noise = np.random.default_rng([zlib.crc32(name.encode()), seed]).standard_normal(out[name].shape)
        drawn = base * np.exp(spread * noise) if base else spread * noise
        out[name] = jnp.asarray(drawn.astype(out[name].dtype))
    for name, factor in factors.items():
        out[name] = (out[name] * factor).astype(out[name].dtype)
    return out
```

```python
from contextlib import ExitStack

import concourse.bass as bass
from concourse import mybir

F32 = mybir.dt.float32
F32R = mybir.dt.float32r
ALU = mybir.AluOpType
ACT = mybir.ActivationFunctionType
AX = mybir.AxisListType

P = 128
B, T, C = 16, 256, 288
R = 64
L = 3
H = 16
HD = C // H
KC, NCH = 96, 3
FF = 4 * C
NPAIR = B // 2
SQUARINGS = 12
EPS = 1e-6
MOD_COLUMNS = [k * C + c * KC for k in (0, 3, 1, 4) for c in range(NCH)]
GATE_COLUMNS = [2 * C, 5 * C]
NG = H // 4
NF = FF // P
QK_ROWS, QK_TILES = 7 * HD, 5
QK_USES, UP_USES = 3, 5
SCALE = float(HD) ** -0.5


def rotation_setup(nc, dram, keep):
    mods, u_twice, g_rot = keep["mods"], keep["u_twice"], keep["g_rot"]
    ident = keep["ident"]
    with ExitStack() as ctx:
        def sb(name, shape, dt=F32):
            return ctx.enter_context(nc.sbuf_tensor(name, shape, dt))

        def sem(name):
            return ctx.enter_context(nc.semaphore(name))

        cond = sb("cond", [KC, NCH, B])
        silu_c = sb("silu_c", [KC + 1, NCH, B])
        w_ada = sb("w_ada", [KC + 1, NCH, 6 * C])
        gates = sb("gates", [B, 2 * C])
        w_rot = sb("w_rot", [KC + 1, NCH, R * R])
        v_rot = sb("v_rot", [B, R * R])
        a_raw = sb("a_rows", [P, NPAIR, R])
        skew_mask = sb("skew_mask", [P, R])
        half_id = sb("half_id", [P, P])
        a_pos = sb("a_pos", [P, NPAIR, P])
        a_neg = sb("a_neg", [P, NPAIR, P])
        a_sq = sb("a_sq", [P, NPAIR, P])
        poly = sb("poly", [P, 2, NPAIR, P])
        e_mat = sb("e_mat", [P, NPAIR, P])
        f_mat = sb("f_mat", [P, NPAIR, P])
        p_t = sb("p_t", [R, C])
        p_nat = sb("p_nat", [KC, NCH, R])
        ones = sb("ones", [R, P])
        pivot = sb("pivot", [R, P])
        state = sb("state", [R, 3 * R])
        col = sb("col", [R, 12])
        c_row = sb("c_row", [1, R, R])
        beta_row = sb("beta_row", [1, R])
        c_mat = sb("c_mat", [R, R])
        beta_col = sb("beta_col", [R, 2])
        c_t = sb("c_t", [R, 2, R])
        u_t = sb("u_t", [P, C])
        ps = [ctx.enter_context(nc.psum_tensor(f"ps{i}", [P, 2, 512], F32)) for i in range(4)]

        s_cond = sem("s_cond")
        s_const = sem("s_const")
        s_p = sem("s_p")
        s_wada = sem("s_wada")
        s_wrot = sem("s_wrot")
        s_silu = sem("s_silu")
        s_ada_ps = sem("s_ada_ps")
        s_ada_out = sem("s_ada_out")
        s_gates = sem("s_gates")
        s_gates_st = sem("s_gates_st")
        s_rot_ps = sem("s_rot_ps")
        s_rot_out = sem("s_rot_out")
        s_v_st = sem("s_v_st")
        s_a_ld = sem("s_a_ld")
        s_chain = sem("s_chain")
        s_exp_ps = sem("s_exp_ps")
        s_exp_sb = sem("s_exp_sb")
        s_g0 = sem("s_g0")
        s_qr_init = sem("s_qr_init")
        s_ones = sem("s_ones")
        s_pivot = sem("s_pivot")
        s_row_ps = sem("s_row_ps")
        s_sqrt = sem("s_sqrt")
        s_beta = sem("s_beta")
        s_qr = sem("s_qr")
        s_save = sem("s_save")
        s_fold = sem("s_fold")
        s_u_ps = sem("s_u_ps")
        s_u_sb = sem("s_u_sb")
        s_gr_ps = sem("s_gr_ps")
        s_gr_sb = sem("s_gr_sb")
        block = ctx.enter_context(nc.Block())
        QR_OPS = 9

        @block.sync
        def _(sp):
            sp.dma_start(cond[:, :, :], dram["cond_t"]).then_inc(s_cond, 16)
            sp.dma_start(ident[:, :], dram["ident"]).then_inc(s_const, 16)
            sp.dma_start(skew_mask[:, :], dram["skew_mask"]).then_inc(s_const, 16)
            sp.dma_start(half_id[:, :], dram["half_ident"]).then_inc(s_const, 16)
            sp.dma_start(p_t[:, :], dram["p_t"]).then_inc(s_p, 16)
            sp.dma_start(p_nat[:, :, :], dram["p_nat"]).then_inc(s_p, 16)
            sp.dma_start(w_rot[:, :, :], dram["w_rot"]).then_inc(s_wrot, 16)
            sp.wait_ge(s_rot_out, 8)
            sp.dma_start(dram["v_scratch"], v_rot[:, :]).then_inc(s_v_st, 16)
            sp.wait_ge(s_v_st, 16)
            a_view = dram["v_scratch"].rearrange("(n two) (i j) -> two i n j", two=2, i=R)
            for half in range(2):
                sp.dma_start(a_raw[half * R:(half + 1) * R, :, :], a_view[half]).then_inc(s_a_ld, 16)
            sp.wait_ge(s_save, 2 * R + 1)
            sp.dma_start(c_mat[:, :], c_row[0:1, :, :]).then_inc(s_fold, 16)
            sp.dma_start(beta_col[:, 0:1], beta_row[0:1, :]).then_inc(s_fold, 16)

        @block.scalar
        def _(act):
            act.wait_ge(s_cond, 16)
            nc.scalar.activation(silu_c[0:KC, :, :], cond[:, :, :], ACT.Silu).then_inc(s_silu, 1)
            for n in range(8):
                act.wait_ge(s_rot_ps, n + 1)
                nc.scalar.activation(v_rot[:, n * 512:(n + 1) * 512], ps[2][0:B, n % 2, :],
                                     ACT.Copy).then_inc(s_rot_out, 1)
            act.wait_ge(s_const, 48)
            act.wait_ge(s_ones, 1)
            nc.scalar.activation(beta_row[0:1, :], ones[0:1, 0:R], ACT.Sqrt).then_inc(s_save, 1)
            act.wait_ge(s_save, 1)
            with act.Fori(0, R) as j:
                nc.scalar.activation(pivot[:, :], ones[:, :], ACT.Copy,
                                     scale=ident[0:R, bass.ds(j, 1)]).then_inc(s_pivot, 1)
                act.wait_ge(s_row_ps, 2 * j + 1)
                nc.scalar.activation(col[:, 0:1], ps[1][0:R, 0, bass.ds(j + R, 1)], ACT.Sqrt,
                                     scale=4.0).then_inc(s_sqrt, 1)
                nc.scalar.activation(c_row[0:1, bass.ds(j, 1), :], ps[1][0:1, 0:1, 2 * R:3 * R],
                                     ACT.Copy).then_inc(s_save, 1)
                act.wait_ge(s_beta, j + 1)
                nc.scalar.activation(beta_row[0:1, bass.ds(j, 1)], col[0:1, 1:2],
                                     ACT.Copy).then_inc(s_save, 1)

        @block.tensor
        def _(pe):
            mm = nc.tensor.matmul
            pe.wait_ge(s_silu, 3)
            with pe.Fori(0, L) as l:
                pe.wait_ge(s_wada, 16 * l + 16)
                for n in range(12):
                    src = MOD_COLUMNS[n]
                    for c in range(NCH):
                        k = KC + (c == NCH - 1)
                        last = mm(ps[0][0:KC, 0, n * B:(n + 1) * B], w_ada[0:k, c, src:src + KC],
                                  silu_c[0:k, c, :], start=c == 0, stop=c == NCH - 1)
                last.then_inc(s_ada_ps, 1)
                for n, src in enumerate(GATE_COLUMNS):
                    for c in range(NCH):
                        k = KC + (c == NCH - 1)
                        last = mm(ps[1][0:B, n, 0:C], silu_c[0:k, c, :], w_ada[0:k, c, src:src + C],
                                  start=c == 0, stop=c == NCH - 1)
                last.then_inc(s_ada_ps, 1)
                pe.wait_ge(s_ada_out, 3 * l + 3)
            pe.wait_ge(s_wrot, 16)
            for n in range(8):
                if n >= 2:
                    pe.wait_ge(s_rot_out, n - 1)
                for c in range(NCH):
                    k = KC + (c == NCH - 1)
                    last = mm(ps[2][0:B, n % 2, :], silu_c[0:k, c, :],
                              w_rot[0:k, c, n * 512:(n + 1) * 512], start=c == 0, stop=c == NCH - 1)
                last.then_inc(s_rot_ps, 1)

            def product(out, lhs, rhs):
                for n in range(NPAIR):
                    last = mm(out[:, n // 4, (n % 4) * P:(n % 4 + 1) * P], lhs[:, n, :], rhs[:, n, :],
                              start=True, stop=True)
                return last

            pe.wait_ge(s_exp_sb, 1)
            product(ps[0], a_neg, a_pos).then_inc(s_exp_ps, 1)
            pe.wait_ge(s_exp_sb, 3)
            product(ps[1], a_sq, poly[:, 0, :, :]).then_inc(s_exp_ps, 1)
            product(ps[2], a_sq, poly[:, 1, :, :]).then_inc(s_exp_ps, 1)
            with pe.Fori(0, SQUARINGS) as r:
                pe.wait_ge(s_exp_sb, 2 * r + 5)
                product(ps[0], f_mat, e_mat).then_inc(s_exp_ps, 1)
                product(ps[1], e_mat, f_mat).then_inc(s_exp_ps, 1)
            pe.wait_ge(s_p, 32)
            for c in range(NCH):
                last = mm(ps[2][0:R, 0, 0:R], p_nat[:, c, :], p_nat[:, c, :], start=c == 0, stop=c == NCH - 1)
            last.then_inc(s_g0, 1)
            pe.wait_ge(s_qr_init, 3)
            pe.wait_ge(s_exp_sb, 2 * SQUARINGS + 5)
            with pe.Fori(0, R) as j:
                pe.wait_ge(s_pivot, j + 1)
                mm(ps[1][:, 0, 0:3 * R], pivot[:, :], state[:, :], start=True, stop=True)\
                    .then_inc(s_row_ps, 1)
                mm(ps[0][:, 0, 0:3 * R], pivot[:, :], state[:, :], start=True, stop=True)\
                    .then_inc(s_row_ps, 1)
                pe.wait_ge(s_qr, QR_OPS * j + QR_OPS)
                pe.wait_ge(s_save, 2 * j + 3)
            pe.wait_ge(s_u_sb, 1)
            nc.tensor.transpose(ps[0][0:R, 0, 0:R], c_mat[:, :], ident[0:R, 0:R]).then_inc(s_u_ps, 1)
            pe.wait_ge(s_u_sb, 3)
            for c in range(NCH):
                last = mm(ps[1][0:KC, 0, c * R:(c + 1) * R], p_t[:, c * KC:(c + 1) * KC], c_t[:, 0, :],
                          start=True, stop=True)
            mm(ps[1][:, 1, 0:C], c_t[:, :, :], p_t[:, :], start=True, stop=True).then_inc(s_u_ps, 1)
            pe.wait_ge(s_u_sb, 6)
            for n in range(NPAIR):
                if n >= 2:
                    pe.wait_ge(s_gr_sb, n - 1)
                mm(ps[2][:, n % 2, 0:C], f_mat[:, n, :], u_t[:, :], start=True, stop=True)\
                    .then_inc(s_gr_ps, 1)

        @block.gpsimd
        def _(pool):
            with pool.Fori(0, L) as l:
                pool.dma_start(w_ada[:, :, :], dram["w_ada"][l]).then_inc(s_wada, 16)
                pool.wait_ge(s_gates, l + 1)
                pool.dma_start(dram["gate_scratch"][l], gates[:, :]).then_inc(s_gates_st, 16)
                pool.wait_ge(s_gates_st, 16 * l + 16)

        @block.vector
        def _(dve):
            nc.vector.memset(silu_c[KC:KC + 1, :, :], 1.0).then_inc(s_silu, 2)
            nc.vector.memset(ones[:, :], 1.0).then_inc(s_ones, 1)
            nc.vector.memset(a_pos[:, :, :], 0.0).then_inc(s_chain, 1)
            with dve.Fori(0, L) as l:
                dve.wait_ge(s_ada_ps, 2 * l + 1)
                mp = ps[0][0:KC, 0, 0:12 * B].rearrange("p (n b) -> p n b", b=B)
                nc.vector.tensor_copy(mods[:, 0:6, bass.ds(l * B, B)], mp[:, 0:6, :]).then_inc(s_ada_out, 1)
                nc.vector.tensor_scalar(mods[:, 6:12, bass.ds(l * B, B)], mp[:, 6:12, :], 1.0, None,
                                        ALU.add).then_inc(s_ada_out, 1)
                dve.wait_ge(s_ada_ps, 2 * l + 2)
                nc.vector.tensor_copy(gates[:, :].rearrange("b (n c) -> b n c", n=2), ps[1][0:B, :, 0:C])\
                    .then_inc(s_gates, 1)
                dve.wait_ge(s_gates, l + 1)
                dve.wait_ge(s_gates_st, 16 * l + 16)
                nc.vector.tensor_copy(col[:, 8:9], ones[:, 0:1]).then_inc(s_ada_out, 1)
            dve.wait_ge(s_a_ld, 32)
            dve.wait_ge(s_const, 48)
            dve.wait_ge(s_chain, 1)
            for half in range(2):
                h = slice(half * R, (half + 1) * R)
                nc.vector.tensor_tensor(a_pos[h, :, h], a_raw[h, :, :],
                                        skew_mask[h, :].unsqueeze(1).to_broadcast([R, NPAIR, R]),
                                        ALU.mult).then_inc(s_chain, 1)
            dve.wait_ge(s_chain, 3)
            nc.vector.tensor_scalar(a_neg[:, :, :], a_pos[:, :, :], -1.0, None, ALU.mult).then_inc(s_exp_sb, 1)
            half_b = half_id[:, :].unsqueeze(1).to_broadcast([P, NPAIR, P])
            for n, sign in enumerate((1.0, -1.0)):
                nc.vector.scalar_tensor_tensor(out=poly[:, n, :, :], in0=a_pos[:, :, :], scalar=sign / 6,
                                               in1=half_b, op0=ALU.mult, op1=ALU.add).then_inc(s_chain, 1)
            dve.wait_ge(s_exp_ps, 1)
            sq = ps[0][:, :, :].rearrange("p h (n c) -> p (h n) c", c=P)
            nc.vector.tensor_copy(a_sq[:, :, :], sq).then_inc(s_chain, 1)
            dve.wait_ge(s_chain, 6)
            for n in range(2):
                nc.vector.scalar_tensor_tensor(out=poly[:, n, :, :], in0=a_sq[:, :, :], scalar=1.0 / 24,
                                               in1=poly[:, n, :, :], op0=ALU.mult, op1=ALU.add)\
                    .then_inc(s_exp_sb, 1)
            for n, (m, src) in enumerate(((e_mat, a_pos), (f_mat, a_neg))):
                dve.wait_ge(s_exp_ps, n + 2)
                nc.vector.tensor_tensor(m[:, :, :], ps[n + 1][:, :, :].rearrange("p h (n c) -> p (h n) c", c=P),
                                        src[:, :, :], ALU.add).then_inc(s_exp_sb, 1)
            with dve.Fori(0, SQUARINGS) as r:
                dve.wait_ge(s_exp_ps, 2 * r + 5)
                dve.wait_ge(s_exp_sb, 2 * r + 5)
                for n, m in enumerate((e_mat, f_mat)):
                    nc.vector.scalar_tensor_tensor(
                        out=m[:, :, :], in0=m[:, :, :], scalar=2.0,
                        in1=ps[n][:, :, :].rearrange("p h (n c) -> p (h n) c", c=P),
                        op0=ALU.mult, op1=ALU.add).then_inc(s_exp_sb, 1)
            dve.wait_ge(s_p, 32)
            nc.vector.tensor_copy(state[:, 0:R], p_t[:, 0:R]).then_inc(s_qr_init, 1)
            dve.wait_ge(s_g0, 1)
            nc.vector.tensor_copy(state[:, R:2 * R], ps[2][0:R, 0, 0:R]).then_inc(s_qr_init, 1)
            nc.vector.tensor_copy(state[:, 2 * R:3 * R], ident[0:R, 0:R]).then_inc(s_qr_init, 1)
            dve.wait_ge(s_qr_init, 3)
            with dve.Fori(0, R) as j:
                row = ps[0][0:R, 0, :]
                alpha, g = row[:, bass.ds(j, 1)], row[:, bass.ds(j + R, 1)]
                t_j, g_j = state[:, bass.ds(j, 1)], state[:, bass.ds(j + R, 1)]

                def step(k, ins):
                    ins.then_inc(s_qr, 1)
                    dve.wait_ge(s_qr, QR_OPS * j + k)

                dve.wait_ge(s_row_ps, 2 * j + 2)
                nc.vector.reciprocal(col[:, 2:3], g).then_inc(s_qr, 1)
                step(2, nc.vector.tensor_scalar(col[:, 3:4], alpha, 0.0, 0.5, ALU.is_lt, ALU.subtract))
                step(3, nc.vector.tensor_scalar(col[:, 4:5], g_j, col[:, 2:3], -1.0, ALU.mult, ALU.mult))
                dve.wait_ge(s_sqrt, j + 1)
                step(4, nc.vector.tensor_tensor(col[:, 1:2], col[:, 0:1], col[:, 3:4], ALU.mult))
                step(5, nc.vector.scalar_tensor_tensor(out=col[:, 5:6], in0=col[:, 1:2], scalar=alpha,
                                                       in1=col[:, 1:2], op0=ALU.subtract, op1=ALU.mult))
                nc.vector.scalar_tensor_tensor(out=col[:, 6:7], in0=t_j, scalar=col[:, 1:2], in1=g_j,
                                               op0=ALU.mult, op1=ALU.subtract).then_inc(s_beta, 1)
                step(6, nc.vector.reciprocal(col[:, 7:8], col[:, 5:6]))
                dve.wait_ge(s_beta, j + 1)
                step(7, nc.vector.tensor_tensor(col[:, 8:9], col[:, 6:7], col[:, 7:8], ALU.mult))
                nc.vector.scalar_tensor_tensor(out=state[:, 0:R], in0=row[:, 0:R], scalar=col[:, 8:9],
                                               in1=state[:, 0:R], op0=ALU.mult, op1=ALU.add).then_inc(s_qr, 1)
                step(9, nc.vector.scalar_tensor_tensor(out=state[:, R:3 * R], in0=row[:, R:3 * R],
                                                       scalar=col[:, 4:5], in1=state[:, R:3 * R],
                                                       op0=ALU.mult, op1=ALU.add))
            dve.wait_ge(s_fold, 32)
            nc.vector.reciprocal(beta_col[:, 1:2], beta_col[:, 0:1]).then_inc(s_chain, 1)
            dve.wait_ge(s_chain, 7)
            nc.vector.tensor_scalar(c_mat[:, :], c_mat[:, :], beta_col[:, 1:2], None, ALU.mult)\
                .then_inc(s_u_sb, 1)
            dve.wait_ge(s_u_ps, 1)
            for n in range(2):
                nc.vector.tensor_copy(c_t[:, n, :], ps[0][0:R, 0, 0:R]).then_inc(s_u_sb, 1)
            dve.wait_ge(s_u_ps, 2)
            u_ps = ps[1][0:KC, 0, 0:NCH * R].rearrange("p (c r) -> p c r", r=R)
            for n in range(2):
                nc.vector.tensor_copy(u_twice[:, :, n * R:(n + 1) * R], u_ps).then_inc(s_u_sb, 1)
            nc.vector.tensor_copy(u_t[:, :], ps[1][:, 1, 0:C]).then_inc(s_u_sb, 1)
            for n in range(NPAIR):
                dve.wait_ge(s_gr_ps, n + 1)
                nc.vector.tensor_copy(g_rot[:, n, :], ps[2][:, n % 2, 0:C]).then_inc(s_gr_sb, 1)


def apply_rotation(nc, dram, keep):
    ident, u_twice, g_rot = keep["ident"], keep["u_twice"], keep["g_rot"]
    with ExitStack() as ctx:
        def sb(name, shape, dt=F32):
            return ctx.enter_context(nc.sbuf_tensor(name, shape, dt))

        def sem(name):
            return ctx.enter_context(nc.semaphore(name))

        x_in = sb("r_x", [P, 2, 2, C])
        x_t = sb("r_xt", [KC, 2, NCH, T])
        z_t = sb("r_zt", [P, 2, T])
        g_now = sb("r_g", [P, C])
        x_out = sb("r_out", [P, 2, 2, C])
        xt_ps = ctx.enter_context(nc.psum_tensor("xt_ps", [P, 2, 512], F32))
        z_ps = ctx.enter_context(nc.psum_tensor("z_ps", [P, 512], F32))
        d_ps = ctx.enter_context(nc.psum_tensor("d_ps", [P, 2, 512], F32))
        s_x = [sem("r_x0"), sem("r_x1")]
        s_xt_ps = sem("r_xt_ps")
        s_xt = sem("r_xt")
        s_z_ps = sem("r_z_ps")
        s_z = sem("r_z")
        s_g = sem("r_g")
        s_d_ps = sem("r_d_ps")
        s_out = sem("r_out")
        s_st = [sem("r_st0"), sem("r_st1")]
        block = ctx.enter_context(nc.Block())

        @block.gpsimd
        def _(pool):
            for h in range(2):
                pool.dma_start(x_in[:, h, :, :], dram["x"][h]).then_inc(s_x[h], 16)
            with pool.Fori(0, NPAIR - 1) as n:
                for h in range(2):
                    pool.wait_ge(s_out, 4 * n + 2 * h + 2)
                    pool.dma_start(x_in[:, h, :, :], dram["x"][2 * n + h + 2]).then_inc(s_x[h], 16)

        @block.scalar
        def _(act):
            with act.Fori(0, NPAIR) as n:
                for h in range(2):
                    act.wait_ge(s_xt_ps, 2 * n + h + 1)
                    nc.scalar.activation(x_t[:, h, 0:2, :], xt_ps[0:KC, 0, :].rearrange("p (c t) -> p c t", t=T),
                                         ACT.Copy).then_inc(s_xt, 1)
                    nc.scalar.activation(x_t[:, h, 2, :], xt_ps[0:KC, 1, 0:T], ACT.Copy).then_inc(s_xt, 1)
                    act.wait_ge(s_z_ps, 2 * n + h + 1)
                    nc.scalar.activation(z_t[:, h, :], z_ps[:, 0:T], ACT.Copy).then_inc(s_z, 1)
                for h in range(2):
                    act.wait_ge(s_out, 4 * n + 2 * h + 2)
                    act.dma_start(dram["out"][2 * n + h], x_out[:, h, :, :]).then_inc(s_st[h], 16)
            for h in range(2):
                act.wait_ge(s_st[h], 16 * NPAIR + 16)

        @block.tensor
        def _(pe):
            with pe.Fori(0, NPAIR) as n:
                for h in range(2):
                    pe.wait_ge(s_x[h], 16 * n + 16)
                    if h:
                        pe.wait_ge(s_xt, 4 * n + 2)
                    for c in range(NCH):
                        for t in range(2):
                            last = nc.tensor.transpose(xt_ps[0:KC, c // 2, (c % 2) * T + t * P:(c % 2) * T + (t + 1) * P],
                                                       x_in[:, h, t, c * KC:(c + 1) * KC], ident[:, :])
                    last.then_inc(s_xt_ps, 1)
                    pe.wait_ge(s_xt, 4 * n + 2 * h + 2)
                    if h:
                        pe.wait_ge(s_z, 2 * n + 1)
                    for c in range(NCH):
                        last = nc.tensor.matmul(z_ps[:, 0:T], u_twice[:, c, :], x_t[:, h, c, :],
                                                start=c == 0, stop=c == NCH - 1)
                    last.then_inc(s_z_ps, 1)
                pe.wait_ge(s_g, n + 1)
                for h in range(2):
                    pe.wait_ge(s_z, 2 * n + h + 1)
                    for t in range(2):
                        if h:
                            pe.wait_ge(s_out, 4 * n + t + 1)
                        nc.tensor.matmul(d_ps[:, t, 0:C], z_t[h * R:(h + 1) * R, h, t * P:(t + 1) * P],
                                         g_now[h * R:(h + 1) * R, :], start=True, stop=True).then_inc(s_d_ps, 1)
                pe.wait_ge(s_out, 4 * n + 4)

        @block.vector
        def _(dve):
            for h in range(2):
                dve.sem_inc(s_st[h], 16)
            with dve.Fori(0, NPAIR) as n:
                nc.vector.tensor_copy(g_now[:, :].unsqueeze(1), g_rot[:, bass.ds(n, 1), :]).then_inc(s_g, 1)
                for h in range(2):
                    for t in range(2):
                        dve.wait_ge(s_d_ps, 4 * n + 2 * h + t + 1)
                        if t == 0:
                            dve.wait_ge(s_st[h], 16 * n + 16)
                        nc.vector.tensor_tensor(x_out[:, h, t, :], d_ps[:, t, 0:C], x_in[:, h, t, :],
                                                ALU.add).then_inc(s_out, 1)


def layers(nc, dram, keep):
    ident, mods = keep["ident"], keep["mods"]
    with ExitStack() as ctx:
        def sb(name, shape, dt=F32):
            return ctx.enter_context(nc.sbuf_tensor(name, shape, dt))

        def sem(name):
            return ctx.enter_context(nc.semaphore(name))

        w_in = [sb(f"w_in{i}", [KC + 1, NCH, 3 * C], F32R) for i in range(2)]
        w_out = [sb(f"w_out{i}", [P, NG, C], F32R) for i in range(2)]
        w_up = [sb(f"w_up{i}", [KC + 1, NCH, FF], F32R) for i in range(2)]
        w_down = [sb(f"w_down{i}", [P, NF, C], F32R) for i in range(2)]
        b_down = [sb(f"b_down{i}", [1, C], F32R) for i in range(2)]
        staging = sb("staging", [P, 2, 3 * C])
        sel = sb("sel", [P, P])
        one_row = sb("one_row", [1, P], F32R)
        x_in = sb("x_in", [P, 2, C])
        x_mid = sb("x_mid", [P, 2, C])
        x_one = sb("x_one", [P, 2, C])
        x_out = sb("x_out", [P, 2, C])
        gated = sb("gated", [P, 2, C])
        gate_a = sb("gate_a", [P, C])
        gate_f = sb("gate_f", [P, C])
        stats = sb("stats", [P, 2, 6])
        mean_var = sb("mean_var", [P, 2, 2])
        rstd = sb("rstd", [P, 2, 2])
        minus_half = sb("minus_half", [P, 2])
        x_hat = sb("x_hat", [P, 2, C])
        h_full = sb("h_full", [KC, NCH, T])
        h_att = [sb(f"h_att{i}", [KC + 1, NCH, T], F32R) for i in range(2)]
        h_mlp = [sb(f"h_mlp{i}", [KC + 1, NCH, T], F32R) for i in range(2)]
        qk = [sb(f"qk{i}", [QK_ROWS, QK_TILES, T], F32R) for i in range(2)]
        q_stack = sb("q_stack", [P, H // 2, T], F32R)
        k_stack = sb("k_stack", [P, H // 2, T], F32R)
        v_sb = sb("v_sb", [P, 2, H, 32])
        maxima = sb("maxima", [P, 2, 2, H // 2])
        neg_max = sb("neg_max", [H, T], F32R)
        probs = sb("probs", [P, 3, 2, 2, T])
        o_full = sb("o_full", [P, 2, 512])
        inv_sum = sb("inv_sum", [P, 2, 512])
        o_att = [sb(f"o_att{i}", [P, 2, 512], F32R) for i in range(2)]
        g_full = sb("g_full", [P, 2, 512])
        hidden = [sb(f"hidden{i}", [P, NF, T], F32R) for i in range(2)]

        scores = [ctx.enter_context(nc.psum_tensor(f"scores{i}", [P, 2, 2, T], F32)) for i in range(2)]
        pv_ps = ctx.enter_context(nc.psum_tensor("pv_ps", [P, 512], F32))
        sum_ps = ctx.enter_context(nc.psum_tensor("sum_ps", [P, 512], F32))
        att_ps = ctx.enter_context(nc.psum_tensor("att_ps", [P, 512], F32))
        mlp_ps = ctx.enter_context(nc.psum_tensor("mlp_ps", [P, 512], F32))
        qk_bank = (att_ps, mlp_ps, att_ps)
        token_bank = (mlp_ps, sum_ps)
        up_bank = (mlp_ps, sum_ps)
        spread_bank = (sum_ps, pv_ps)

        s_init = sem("s_init")
        s_sel = sem("s_sel")
        s_kinit = sem("s_kinit")
        s_half = sem("s_half")
        s_stage = [sem("s_stage0"), sem("s_stage1")]
        s_w_high = sem("s_w_high")
        s_w_low = sem("s_w_low")
        s_xin = sem("s_xin")
        s_xmid = sem("s_xmid")
        s_gate_a = sem("s_gate_a")
        s_gate_f = sem("s_gate_f")
        s_stats = [sem("s_stats_a"), sem("s_stats_m")]
        s_var = [sem("s_var_a"), sem("s_var_m")]
        s_rstd = [sem("s_rstd_a"), sem("s_rstd_m")]
        s_pow = [sem("s_pow_a"), sem("s_pow_m")]
        s_xhat_a = sem("s_xhat_a")
        s_xhat_m = sem("s_xhat_m")
        s_tr_a = sem("s_tr_a")
        s_tr_m = sem("s_tr_m")
        s_h_a = sem("s_h_a")
        s_h_m = sem("s_h_m")
        s_hhi_a = sem("s_hhi_a")
        s_hhi_m = sem("s_hhi_m")
        s_hlo_a = sem("s_hlo_a")
        s_hlo_m = sem("s_hlo_m")
        s_qk_ps = sem("s_qk_ps")
        s_qk_hi = sem("s_qk_hi")
        s_qk_lo = sem("s_qk_lo")
        s_qk_st = sem("s_qk_st")
        s_stack = sem("s_stack")
        s_v_ps = sem("s_v_ps")
        s_v = sem("s_v")
        s_score = sem("s_score")
        s_max = sem("s_max")
        s_max_ps = sem("s_max_ps")
        s_neg = sem("s_neg")
        s_neg_st = sem("s_neg_st")
        s_st = sem("s_st")
        s_exp = sem("s_exp")
        s_pv = sem("s_pv")
        s_o_full = sem("s_o_full")
        s_sum = sem("s_sum")
        s_inv = sem("s_inv")
        s_o = sem("s_o")
        s_o_hi = sem("s_o_hi")
        s_o_lo = sem("s_o_lo")
        s_proj = sem("s_proj")
        s_proj_gated = sem("s_proj_gated")
        s_x_one = sem("s_x_one")
        s_up = sem("s_up")
        s_gelu = sem("s_gelu")
        s_g_lo = sem("s_g_lo")
        s_down = sem("s_down")
        s_down_gated = sem("s_down_gated")
        s_x_out = sem("s_x_out")
        s_x_st = sem("s_x_st")
        s_tick = [sem("s_tick_sp"), sem("s_tick_pool"), sem("s_tick_dve")]

        block = ctx.enter_context(nc.Block())

        PRE_EXP, PRE_PV, G_PRE, PRE2, PRE = 2, 2, 2, 2, 1
        TRS = 2

        pieces = [(w_in, (slice(0, KC + 1), c, slice(0, 3 * C)), "w_in", KC + 1, 3 * C) for c in range(NCH)]
        pieces += [(w_out, (slice(0, P), slice(2 * n, 2 * n + 2), slice(0, C)), "w_out", P, 2 * C) for n in range(2)]
        pieces += [(w_up, (slice(0, KC + 1), c, slice(n * 576, (n + 1) * 576)), "w_up", KC + 1, 576)
                   for c in range(NCH) for n in range(2)]
        pieces += [(w_down, (slice(0, P), slice(3 * n, 3 * n + 3), slice(0, C)), "w_down", P, 3 * C) for n in range(3)]
        pieces += [(b_down, (slice(0, 1), slice(0, C)), "b_down", 1, C)]
        NP = len(pieces)
        OF = {name: range(a, b) for name, a, b in (("w_in", 0, 3), ("w_out", 3, 5), ("w_up", 5, 11), ("w_down", 11, 15))}

        def staged(n, view):
            _, _, _, rows, cols = pieces[n]
            part = staging[0:rows, n % 2, 0:cols]
            return part.rearrange("p (a c) -> p a c", c=C) if len(view) == 3 and isinstance(view[1], slice) else part

        def whole_run(engine, prologue, half_step, epilogue):
            prologue()
            half_step(0, 0)
            with engine.Fori(0, L - 1) as l:
                half_step(l, 1)
                with engine.Fori(2, B - 2) as b:
                    half_step(l, b)
                half_step(l, B - 2)
                half_step(l, B - 1)
                half_step(l + 1, 0)
            half_step(L - 1, 1)
            with engine.Fori(2, B - 2) as b:
                half_step(L - 1, b)
            half_step(L - 1, B - 2)
            half_step(L - 1, B - 1)
            epilogue()

        def neighbours(l, b):
            start = isinstance(l, int) and isinstance(b, int) and l == 0 and b == 0
            final = isinstance(l, int) and isinstance(b, int) and l == L - 1
            return not start, not (final and b >= B - 1), not (final and b >= B - 2)

        def at(b, n):
            return isinstance(b, int) and b == n

        @block.sync
        def _(sp):
            def hold(semaphore, value):
                sp.wait_ge(semaphore, value)
                sp.sem_inc(s_tick[0], 1)

            sp.sem_inc(s_x_st, 16 * B)
            sp.sem_inc(s_qk_st, 16)
            sp.sem_inc(s_stack, 16)
            sp.wait_ge(s_kinit, 1)
            sp.dma_start(sel[:, :], dram["sel"]).then_inc(s_sel, 16)
            sp.dma_start(x_in[:, :, :], dram["out"][0]).then_inc(s_xin, 16)
            qk_rows = dram["qk_scratch"].rearrange("s a b c d t -> s (a b c d) t")
            gate_rows = dram["gate_scratch"].rearrange("l b c -> (l b) c")
            FULL = QK_ROWS * (QK_TILES - 1)

            def load_x_in(it, b):
                hold(s_xhat_a, 2 * it)
                hold(s_x_st, 16 * it + 16)
                sp.dma_start(x_in[:, :, :], dram["out"][b]).then_inc(s_xin, 16)

            def stacks(it):
                for i, made in enumerate((s_qk_hi, s_qk_lo)):
                    hold(made, 3 * it + 3)
                    if i == 0:
                        hold(s_stack, 192 * it + 16)
                    sp.dma_start(qk_rows[i, 0:FULL, :].rearrange("(m p) t -> p m t", p=QK_ROWS),
                                 qk[i][:, 0:QK_TILES - 1, :].bitcast(F32)).then_inc(s_qk_st, 16)
                    sp.dma_start(qk_rows[i, FULL:2 * C, :],
                                 qk[i][0:2 * C - FULL, QK_TILES - 1, :].bitcast(F32)).then_inc(s_qk_st, 16)
                hold(s_qk_st, 64 * it + 80)
                hold(s_st, 8 * it + PRE)
                for n, (stack, order) in enumerate(((q_stack, (0, 1, 0)), (k_stack, (0, 0, 1)))):
                    for par in range(2):
                        for j, part in enumerate(order):
                            row = R * par + HD * j
                            sp.dma_start(stack[row:row + HD, :, :].bitcast(F32),
                                         dram["qk_scratch"][part, n, :, par].rearrange("b d t -> d b t"))\
                              .then_inc(s_stack, 16)

            def negated_maxima(it):
                hold(s_neg, it + 1 + PRE)
                for par in range(2):
                    row = R * par + 3 * HD
                    sp.dma_start(q_stack[row:row + 1, :, :].bitcast(F32),
                                 neg_max[par * 8:par * 8 + 8, :].bitcast(F32)).then_inc(s_neg_st, 16)

            def store(it, b):
                hold(s_x_out, 2 * it + 2 + PRE2)
                sp.dma_start(dram["out"][b], x_out[:, :, :]).then_inc(s_x_st, 16)

            def gate(it, tile, which, signal, free, count):
                hold(free, count)
                row = gate_rows[bass.ds(it, 1), which * C:(which + 1) * C]
                sp.dma_start(tile[:, :], row.rearrange("a c -> (a c)").partition_broadcast(P)).then_inc(signal, 16)

            def prologue():
                load_x_in(1, 1)
                stacks(0)

            def half_step(l, b):
                it = l * B + b
                before, after, after_next = neighbours(l, b)
                negated_maxima(it)
                hold(s_x_one, 2 * it + PRE)
                sp.dma_start(x_mid[:, :, :], dram["out"][b]).then_inc(s_xmid, 16)
                gate(it, gate_a, 0, s_gate_a, s_proj_gated, 2 * it + PRE)
                if after_next:
                    load_x_in(it + 2, (b + 2) % B if isinstance(b, int) else b + 2)
                if after:
                    stacks(it + 1)
                gate(it, gate_f, 1, s_gate_f, s_down_gated, 2 * it + PRE2)
                if before:
                    store(it - 1, (b - 1) % B if isinstance(b, int) else b - 1)

            def epilogue():
                store(L * B - 1, B - 1)

            whole_run(sp, prologue, half_step, epilogue)
            sp.wait_ge(s_x_st, 16 * B * (L + 1))

        @block.gpsimd
        def _(pool):
            tt = nc.gpsimd.tensor_tensor
            nc.gpsimd.memset(minus_half[:, :], -0.5).then_inc(s_half, 1)
            for sm in (s_x_one, s_o_lo, s_hlo_m):
                pool.sem_inc(sm, PRE)
            pool.sem_inc(s_x_out, PRE2)
            pool.sem_inc(s_g_lo, G_PRE)
            pool.wait_ge(s_half, 1)

            def inverse_deviation(order, it):
                pool.wait_ge(s_var[order], 2 * it + 2)
                pool.sem_inc(s_tick[1], 1)
                nc.gpsimd.tensor_scalar(rstd[:, 0, :], mean_var[:, :, 1], EPS, None, ALU.add).then_inc(s_pow[order], 1)
                pool.wait_ge(s_pow[order], it + 1)
                tt(rstd[:, 1, :], rstd[:, 0, :], minus_half[:, :], ALU.pow).then_inc(s_rstd[order], 1)

            def low(out, full, high, signal):
                tt(out, full, high.bitcast(F32), ALU.subtract).then_inc(signal, 1)

            def stage(l, n):
                _, view, name, rows, cols = pieces[n]
                src = dram[name][bass.ds(l, 1)]
                if name == "b_down":
                    pool.dma_start(staging[0:1, n % 2, 0:C], src).then_inc(s_stage[n % 2], 16)
                else:
                    src = src.rearrange("l p a c -> (l p) a c")[view]
                    pool.dma_start(staged(n, view), src).then_inc(s_stage[n % 2], 16)

            def low_weights(name, l, last_layer=False):
                for n in OF[name]:
                    pair, view = pieces[n][0:2]
                    pool.wait_ge(s_w_high, NP * l + n + 1)
                    low(pair[1][view], staged(n, view), pair[0][view], s_w_low)
                    follower = (l, n + 2) if n + 2 < NP else (l + 1, n % 2)
                    if n + 2 < NP or not last_layer:
                        pool.wait_ge(s_w_low, NP * l + n + 1)
                        stage(*follower)

            def attention_low(it):
                pool.wait_ge(s_hhi_a, it + 1)
                low(h_att[1][0:KC, :, :], h_full[:, :, :], h_att[0][0:KC, :, :], s_hlo_a)

            def prologue():
                stage(0, 0)
                stage(0, 1)
                low_weights("w_in", 0)
                inverse_deviation(0, 0)
                attention_low(0)
                inverse_deviation(0, 1)
                low_weights("w_out", 0)
                attention_low(1)

            def half_step(l, b):
                it = l * B + b
                before, after, after_next = neighbours(l, b)
                if before:
                    add_attention(it - 1)
                    inverse_deviation(1, it - 1)
                if at(b, 1):
                    low_weights("w_up", l)
                if after_next:
                    inverse_deviation(0, it + 2)
                if before:
                    mlp_low(it - 1)
                if at(b, 1):
                    low_weights("w_down", l, last_layer=isinstance(l, int) and l == L - 1)
                for half in range(2):
                    pool.wait_ge(s_o_hi, 2 * it + half + 1)
                    low(o_att[1][:, half, :], o_full[:, half, :], o_att[0][:, half, :], s_o_lo)
                if before:
                    hidden_low(it - 1)
                if after_next:
                    attention_low(it + 2)
                if at(b, B - 2) and after_next:
                    low_weights("w_in", l + 1)
                if at(b, 0) and before:
                    low_weights("w_out", l)
                if before:
                    add_mlp(it - 1)

            def add_attention(it):
                pool.wait_ge(s_xmid, 16 * it + 16)
                for t in range(2):
                    pool.wait_ge(s_proj_gated, 2 * it + t + 1 + PRE)
                    tt(x_one[:, t, :], x_mid[:, t, :], gated[:, t, :], ALU.add).then_inc(s_x_one, 1)

            def mlp_low(it):
                pool.wait_ge(s_hhi_m, it + 1)
                low(h_mlp[1][0:KC, :, :], h_full[:, :, :], h_mlp[0][0:KC, :, :], s_hlo_m)

            def hidden_low(it):
                for n in range(UP_USES):
                    tiles = slice(2 * n, min(2 * n + 2, NF))
                    width = (tiles.stop - tiles.start) * T
                    pool.wait_ge(s_gelu, 2 * (UP_USES * it + n + 1))
                    low(hidden[1][:, tiles, :].rearrange("p a t -> p (a t)"), g_full[:, n % 2, 0:width],
                        hidden[0][:, tiles, :].rearrange("p a t -> p (a t)"), s_g_lo)

            def add_mlp(it):
                for t in range(2):
                    pool.wait_ge(s_down_gated, 2 * it + t + 1 + PRE2)
                    if t == 0:
                        pool.wait_ge(s_x_st, 16 * it + 16 * B)
                    tt(x_out[:, t, :], x_one[:, t, :], gated[:, t, :], ALU.add).then_inc(s_x_out, 1)

            def epilogue():
                it = L * B - 1
                add_attention(it)
                inverse_deviation(1, it)
                mlp_low(it)
                hidden_low(it)
                add_mlp(it)

            whole_run(pool, prologue, half_step, epilogue)

        @block.scalar
        def _(act):
            act.sem_inc(s_exp, PRE_EXP)
            act.sem_inc(s_neg, PRE)
            act.sem_inc(s_neg_st, 16)
            act.sem_inc(s_v, PRE)
            act.sem_inc(s_o_full, PRE)
            act.wait_ge(s_init, 6)
            evict = nc.scalar.activation

            def high_weights(name, l, which=None):
                for n in OF[name] if which is None else [OF[name][k] for k in which]:
                    pair, view = pieces[n][0:2]
                    act.wait_ge(s_stage[n % 2], 16 * (l * ((NP + 1 - n % 2) // 2) + n // 2 + 1))
                    evict(pair[0][view], staged(n, view), ACT.Copy).then_inc(s_w_high, 1)

            def modulate(it, order, chunks):
                bank = (att_ps, mlp_ps)[order]
                for c in chunks:
                    act.wait_ge((s_tr_a, s_tr_m)[order], TRS * it + c // 2 + 1 + (PRE if order else 0))
                    mod = [mods[:, base + 3 * order + c, bass.ds(it, 1)] for base in (6, 0)]
                    evict(h_full[:, c, :], bank[0:KC, (c % 2) * T:(c % 2 + 1) * T], ACT.Identity, scale=mod[0],
                          bias=mod[1]).then_inc((s_h_a, s_h_m)[order], 1)

            def attention_modulate(it, chunks, a_before, m_before):
                if 0 in chunks:
                    if a_before is not None:
                        act.wait_ge(s_hlo_a, a_before)
                    if m_before is not None:
                        act.wait_ge(s_hlo_m, m_before + PRE)
                modulate(it, 0, chunks)

            def qk_high(it, n):
                act.wait_ge(s_qk_ps, QK_USES * it + n + 1)
                if n == 0:
                    act.wait_ge(s_qk_st, 64 * it + 16)
                tiles = slice(2 * n, min(2 * n + 2, QK_TILES))
                rows = QK_ROWS if tiles.stop < QK_TILES else 2 * C - QK_ROWS * (QK_TILES - 1)
                width = (tiles.stop - tiles.start) * T
                evict(qk[0][0:rows, tiles, :].rearrange("p a t -> p (a t)"), qk_bank[n][0:rows, 0:width], ACT.Copy)\
                    .then_inc(s_qk_hi, 1)

            def v_evict(it, kt):
                act.wait_ge(s_v_ps, 2 * it + kt + 1 + PRE)
                if kt == 0:
                    act.wait_ge(s_pv, NG * it + PRE_PV)
                evict(v_sb[:, kt, :, 0:HD], att_ps[:, 0:C].rearrange("p (h d) -> p h d", d=HD), ACT.Copy)\
                    .then_inc(s_v, 1)

            def negate_maxima(it):
                act.wait_ge(s_max_ps, it + 1 + PRE)
                act.wait_ge(s_neg_st, 32 * it + 16)
                evict(neg_max[:, :], att_ps[0:H, 0:T], ACT.Copy, scale=-1.0).then_inc(s_neg, 1)

            def exponentials(it, u):
                act.wait_ge(s_st, 8 * it + u + 1 + PRE)
                if u >= 3:
                    act.wait_ge(s_pv, NG * it + (u - 3) // 2 + 1 + PRE_PV)
                else:
                    act.wait_ge(s_pv, NG * it + PRE_PV)
                evict(probs[:, u % 3, :, :, :], scores[u % 2][:, :, :, :], ACT.Exp, scale=SCALE)\
                    .then_inc(s_exp, 1)

            def copy_o(it, half):
                act.wait_ge(s_pv, NG * it + 2 * half + 2 + PRE_PV)
                act.wait_ge(s_o_lo, 2 * it + PRE)
                evict(o_full[:, half, :], pv_ps[:, :], ACT.Copy).then_inc(s_o_full, 1)

            def gelu(it, n):
                act.wait_ge(s_up, UP_USES * it + n + 1 + PRE)
                act.wait_ge(s_g_lo, UP_USES * it + max(n - 1, 0) + G_PRE)
                if n == 0:
                    act.wait_ge(s_down, 2 * it + PRE)
                tiles = slice(2 * n, min(2 * n + 2, NF))
                width = (tiles.stop - tiles.start) * T
                bank = up_bank[n % 2]
                evict(g_full[:, n % 2, 0:width], bank[:, 0:width], ACT.Gelu_apprx_tanh).then_inc(s_gelu, 1)
                evict(hidden[0][:, tiles, :].rearrange("p a t -> p (a t)"), bank[:, 0:width], ACT.Gelu_apprx_tanh)\
                    .then_inc(s_gelu, 1)

            def prologue():
                high_weights("w_in", 0)
                attention_modulate(0, (0, 1, 2), None, None)
                for n in range(QK_USES):
                    qk_high(0, n)
                for kt in range(2):
                    v_evict(0, kt)
                attention_modulate(1, (0, 1, 2), 1, None)
                high_weights("w_out", 0)

            def half_step(l, b):
                it = l * B + b
                before, after, after_next = neighbours(l, b)
                negate_maxima(it)
                for n in range(3):
                    if after:
                        qk_high(it + 1, n)
                    if n < 2:
                        exponentials(it, n)
                    if n == 1 and at(b, 1):
                        high_weights("w_up", l, (0, 1))
                for u in range(2, 5):
                    exponentials(it, u)
                    if at(b, 1):
                        high_weights("w_up", l, (u,))
                if before:
                    act.wait_ge(s_hlo_a, it + 2 if after else it + 1)
                    modulate(it - 1, 1, (0, 1))
                exponentials(it, 5)
                if at(b, 1):
                    high_weights("w_up", l, (5,))
                copy_o(it, 0)
                exponentials(it, 6)
                if before:
                    modulate(it - 1, 1, (2,))
                exponentials(it, 7)
                copy_o(it, 1)
                if after:
                    v_evict(it + 1, 0)
                    v_evict(it + 1, 1)
                if at(b, 1):
                    act.wait_ge(s_down, 2 * it - 2 + PRE)
                    high_weights("w_down", l)
                if before:
                    for n in range(UP_USES):
                        gelu(it - 1, n)
                if after_next:
                    attention_modulate(it + 2, (0, 1, 2), None if before else it + 2, it if before else None)
                if at(b, B - 2) and after_next:
                    high_weights("w_in", l + 1)
                if at(b, 0) and before:
                    act.wait_ge(s_proj, 2 * it + PRE)
                    high_weights("w_out", l)

            def epilogue():
                it = L * B - 1
                modulate(it, 1, (0, 1, 2))
                for n in range(UP_USES):
                    gelu(it, n)

            whole_run(act, prologue, half_step, epilogue)

        @block.tensor
        def _(pe):
            mm = nc.tensor.matmul
            pe.sem_inc(s_st, PRE)
            pe.sem_inc(s_down, PRE)
            pe.sem_inc(s_pv, PRE_PV)
            for sm in (s_v_ps, s_up, s_max_ps, s_proj):
                pe.sem_inc(sm, PRE)
            pe.sem_inc(s_tr_m, PRE)
            pe.wait_ge(s_sel, 16)
            pe.wait_ge(s_init, 6)

            def split(out, high, low_part, weights, steps, start=True, stop=True):
                n, total = 0, 3 * len(steps)
                for s in steps:
                    a, c = s
                    for left, w in ((high, 0), (high, 1), (low_part, 0)):
                        last = mm(out, a(left), c(weights[w]), start=start and n == 0, stop=stop and n == total - 1)
                        n += 1
                return last

            def rows(c):
                return KC + (c == NCH - 1)

            def transposes(it, bank, chunks, done):
                for c in chunks:
                    for t in range(2):
                        last = nc.tensor.transpose(bank[0:KC, (c % 2) * T + t * P:(c % 2) * T + (t + 1) * P],
                                                   x_hat[:, t, c * KC:(c + 1) * KC], ident[:, :])
                last.then_inc(done, 1)

            def attention_transposes(it, use, v_before=True):
                if use == 0:
                    pe.wait_ge(s_xhat_a, 2 * it + 2)
                    if v_before:
                        pe.wait_ge(s_v, 2 * it + PRE)
                    transposes(it, att_ps, (0, 1), s_tr_a)
                else:
                    pe.wait_ge(s_h_a, NCH * it + 2)
                    transposes(it, att_ps, (2,), s_tr_a)

            def mlp_transposes(it, use, qk_between):
                if use == 0:
                    pe.wait_ge(s_xhat_m, 2 * it + 2)
                    if qk_between:
                        pe.wait_ge(s_qk_lo, QK_USES * (it + 2) + 2)
                    else:
                        pe.wait_ge(s_proj_gated, 2 * it + 2 + PRE)
                    transposes(it, mlp_ps, (0, 1), s_tr_m)
                else:
                    pe.wait_ge(s_h_m, NCH * it + 2)
                    transposes(it, mlp_ps, (2,), s_tr_m)

            def qk_tiles(it, n, m_between=True):
                if n == 0:
                    pe.wait_ge(s_hlo_a, it + 1)
                    pe.wait_ge(s_neg, it + PRE)
                    pe.wait_ge(s_h_a, NCH * it + NCH)
                elif n == 1:
                    if m_between:
                        pe.wait_ge(s_proj_gated, 2 * it - 3 + PRE)
                    else:
                        pe.wait_ge(s_qk_lo, QK_USES * it + 0) if not at(it, 0) else None
                else:
                    pe.wait_ge(s_qk_lo, QK_USES * it + 1)
                for m in range(2 * n, min(2 * n + 2, QK_TILES)):
                    cols = slice(m * QK_ROWS, min((m + 1) * QK_ROWS, 2 * C))
                    count = 0
                    for c in range(NCH):
                        for w, h in ((0, 0), (0, 1), (1, 0)):
                            last = mm(qk_bank[n][0:cols.stop - cols.start, (m % 2) * T:(m % 2 + 1) * T],
                                      w_in[w][0:rows(c), c, cols], h_att[h][0:rows(c), c, :],
                                      start=count == 0, stop=count == 8)
                            count += 1
                last.then_inc(s_qk_ps, 1)

            def values(it, kt):
                if kt == 0:
                    pe.wait_ge(s_qk_lo, QK_USES * it + QK_USES)
                else:
                    pe.wait_ge(s_v, 2 * it + 1 + PRE)
                split(att_ps[:, 0:C], h_att[0], h_att[1], w_in,
                      [(lambda h, c=c: h[0:rows(c), c, kt * P:(kt + 1) * P],
                        lambda w, c=c: w[0:rows(c), c, 2 * C:3 * C]) for c in range(NCH)]).then_inc(s_v_ps, 1)

            def score_unit(it, u):
                if u == 0:
                    pe.wait_ge(s_stack, 192 * it + 192 + 16)
                if u < 2:
                    pe.wait_ge(s_exp, 8 * it - 1 + u + PRE_EXP)
                else:
                    pe.wait_ge(s_max, 8 * it + u - 1)
                for par in range(2):
                    r = slice(R * par, R * par + 3 * HD)
                    for qt in range(2):
                        last = mm(scores[u % 2][:, par, qt, :], q_stack[r, u, qt * P:(qt + 1) * P],
                                  k_stack[r, u, :], start=True, stop=True)
                last.then_inc(s_score, 1)

            def maxima_transposes(it, after):
                pe.wait_ge(s_max, 8 * it + 8)
                pe.wait_ge(s_h_a, NCH * (it + 2 if after else it + 1))
                pe.wait_ge(s_v, 2 * it + 2 + PRE)
                for qt in range(2):
                    last = nc.tensor.transpose(att_ps[0:H, qt * P:(qt + 1) * P],
                                               maxima[:, qt, :, :].rearrange("p a b -> p (a b)"), ident[:, :])
                last.then_inc(s_max_ps, 1)

            def shifted_unit(it, u):
                if u == 0:
                    pe.wait_ge(s_neg_st, 32 * it + 32 + 16)
                if u >= 2:
                    pe.wait_ge(s_exp, 8 * it + u - 1 + PRE_EXP)
                for par in range(2):
                    r = slice(R * par, R * par + 3 * HD + 1)
                    for kt in range(2):
                        last = mm(scores[u % 2][:, par, kt, :], k_stack[r, u, kt * P:(kt + 1) * P],
                                  q_stack[r, u, :], start=True, stop=True)
                last.then_inc(s_st, 1)

            def weighted_values(it, g):
                pe.wait_ge(s_exp, 8 * it + 2 * g + 2 + PRE_EXP)
                if g == 0:
                    pe.wait_ge(s_v, 2 * it + 2 + PRE)
                if g < 2:
                    pe.wait_ge(s_inv, 2 * it + PRE)
                else:
                    pe.wait_ge(s_o_full, 2 * it + 1 + PRE)
                for kt in range(2):
                    for i in range(4):
                        u = 2 * g + i // 2
                        last = mm(pv_ps[32 * i:32 * i + 32, (g % 2) * T:(g % 2 + 1) * T], v_sb[:, kt, 4 * g + i, :],
                                  probs[:, u % 3, i % 2, kt, :], start=kt == 0, stop=kt == 1, tile_position=(0, 32 * i))
                last.then_inc(s_pv, 1)

            def spread_sums(it, half):
                pe.wait_ge(s_o_full, 2 * it + half + 1 + PRE)
                if half == 0:
                    pe.wait_ge(s_proj_gated, 2 * it + PRE)
                mm(spread_bank[half][:, :], sel[:, :], o_full[:, half, :], start=True, stop=True).then_inc(s_sum, 1)

            def projection(it, t):
                if t == 0:
                    pe.wait_ge(s_o_lo, 2 * it + 2 + PRE)
                pe.wait_ge(s_down_gated, 2 * it - 1 + t + PRE2)
                split(token_bank[t][:, 0:C], o_att[0], o_att[1], w_out,
                      [(lambda o, g=g: o[:, g // 2, (g % 2) * T + t * P:(g % 2) * T + (t + 1) * P],
                        lambda w, g=g: w[:, g, :]) for g in range(NG)]).then_inc(s_proj, 1)

            def up(it, n):
                if n == 0:
                    pe.wait_ge(s_hlo_m, it + 1 + PRE)
                    pe.wait_ge(s_h_m, NCH * it + NCH)
                elif n == 1:
                    pe.wait_ge(s_inv, 2 * it + 3 + PRE) if not at(it, L * B - 1) else None
                else:
                    pe.wait_ge(s_gelu, 2 * (UP_USES * it + n - 1))
                for m in range(2 * n, min(2 * n + 2, NF)):
                    count = 0
                    for c in range(NCH):
                        for w, h in ((0, 0), (0, 1), (1, 0)):
                            last = mm(up_bank[n % 2][:, (m % 2) * T:(m % 2 + 1) * T],
                                      w_up[w][0:rows(c), c, m * P:(m + 1) * P],
                                      h_mlp[h][0:rows(c), c, :], start=count == 0, stop=count == 8)
                            count += 1
                last.then_inc(s_up, 1)

            def down(it, t, part):
                tiles = range(0, 6) if part == 0 else range(6, NF)
                if part == 0:
                    pe.wait_ge(s_gelu, 2 * (UP_USES * it + UP_USES))
                    pe.wait_ge(s_g_lo, UP_USES * it + 3 + G_PRE)
                    for w in range(2):
                        mm(token_bank[t][:, 0:C], one_row[:, :], b_down[w][:, :], start=w == 0, stop=False)
                else:
                    pe.wait_ge(s_g_lo, UP_USES * it + UP_USES + G_PRE)
                last = split(token_bank[t][:, 0:C], hidden[0], hidden[1], w_down,
                             [(lambda h, m=m: h[:, m, t * P:(t + 1) * P], lambda w, m=m: w[:, m, :]) for m in tiles],
                             start=False, stop=part == 1)
                if part == 1:
                    last.then_inc(s_down, 1)

            def weights_ready(name, l):
                pe.wait_ge(s_w_low, NP * l + OF[name].stop)

            def prologue():
                weights_ready("w_in", 0)
                attention_transposes(0, 0, v_before=False)
                attention_transposes(0, 1)
                for n in range(QK_USES):
                    qk_tiles(0, n, m_between=False)
                values(0, 0)
                values(0, 1)
                attention_transposes(1, 0)
                attention_transposes(1, 1)
                for u in range(8):
                    score_unit(0, u)

            def half_step(l, b):
                it = l * B + b
                before, after, after_next = neighbours(l, b)
                if before:
                    if at(b, 1):
                        weights_ready("w_out", l)
                    projection(it - 1, 0)
                maxima_transposes(it, after)
                if before:
                    projection(it - 1, 1)
                if after and at(b, B - 1):
                    weights_ready("w_in", l + 1)
                for n in range(3):
                    if after:
                        qk_tiles(it + 1, n, m_between=before)
                    shifted_unit(it, n)
                shifted_unit(it, 3)
                weighted_values(it, 0)
                shifted_unit(it, 4)
                shifted_unit(it, 5)
                weighted_values(it, 1)
                if before:
                    mlp_transposes(it - 1, 0, after)
                shifted_unit(it, 6)
                if after:
                    values(it + 1, 0)
                shifted_unit(it, 7)
                if before:
                    mlp_transposes(it - 1, 1, after)
                weighted_values(it, 2)
                spread_sums(it, 0)
                weighted_values(it, 3)
                m = it - 1
                if before:
                    if at(b, 1):
                        weights_ready("w_up", l)
                    up(m, 0)
                spread_sums(it, 1)
                if after:
                    values(it + 1, 1)
                work = []
                if before:
                    work = [lambda: None, lambda: up(m, 1), lambda: up(m, 2), lambda: up(m, 3), lambda: up(m, 4)]
                for n, w in enumerate(work):
                    w()
                    if n >= 1 and after:
                        score_unit(it + 1, n - 1)
                if after and not before:
                    for u in range(4):
                        score_unit(it + 1, u)
                if before and at(b, 1):
                    weights_ready("w_down", l)
                if after_next:
                    attention_transposes(it + 2, 0)
                if after:
                    score_unit(it + 1, 4)
                if before:
                    down(m, 0, 0)
                if after:
                    score_unit(it + 1, 5)
                if after_next:
                    attention_transposes(it + 2, 1)
                if before:
                    down(m, 0, 1)
                if after:
                    score_unit(it + 1, 6)
                if before:
                    down(m, 1, 0)
                if after:
                    score_unit(it + 1, 7)
                if before:
                    down(m, 1, 1)

            def epilogue():
                it = L * B - 1
                projection(it, 0)
                projection(it, 1)
                mlp_transposes(it, 0, False)
                mlp_transposes(it, 1, False)
                for n in range(UP_USES):
                    up(it, n)
                for t in range(2):
                    down(it, t, 0)
                    down(it, t, 1)

            whole_run(pe, prologue, half_step, epilogue)

        @block.vector
        def _(dve):
            tt = nc.vector.tensor_tensor
            nc.vector.memset(one_row[:, :].bitcast(F32), 1.0).then_inc(s_init, 1)
            nc.vector.memset(h_att[0][:, :, :].bitcast(F32), 1.0).then_inc(s_init, 1)
            nc.vector.memset(h_att[1][:, :, :].bitcast(F32), 0.0).then_inc(s_init, 1)
            nc.vector.memset(h_mlp[0][:, :, :].bitcast(F32), 1.0).then_inc(s_init, 1)
            nc.vector.memset(h_mlp[1][:, :, :].bitcast(F32), 0.0).then_inc(s_init, 1)
            nc.vector.memset(v_sb[:, :, :, :], 1.0).then_inc(s_init, 1)
            nc.vector.memset(k_stack[:, :, :].bitcast(F32), 1.0).then_inc(s_kinit, 1)
            for sm in (s_proj_gated, s_inv):
                dve.sem_inc(sm, PRE)
            dve.sem_inc(s_down_gated, PRE2)

            def norm(order, it, x_tile, ready, done):
                for t in range(2):
                    if ready:
                        ready(t)
                    nc.vector.bn_stats(out=stats[:, t, :], in_=x_tile[:, t, :]).then_inc(s_stats[order], 1)
                for t in range(2):
                    dve.wait_ge(s_stats[order], 2 * it + t + 1)
                    dve.sem_inc(s_tick[2], 1)
                    nc.vector.bn_aggr(out=mean_var[:, t, :], in_=stats[:, t, :]).then_inc(s_var[order], 1)

            def x_hats(order, it, x_tile, done):
                dve.wait_ge(s_var[order], 2 * it + 2)
                dve.wait_ge(s_rstd[order], it + 1)
                for t in range(2):
                    nc.vector.tensor_scalar(x_hat[:, t, :], x_tile[:, t, :], mean_var[:, t, 0:1], rstd[:, 1, t:t + 1],
                                            ALU.subtract, ALU.mult).then_inc(done, 1)

            def attention_norm(it):
                def ready(t):
                    if t == 0:
                        dve.wait_ge(s_xin, 16 * it + 16)
                norm(0, it, x_in, ready, s_xhat_a)

            def attention_high(it):
                dve.wait_ge(s_h_a, NCH * it + NCH)
                dve.wait_ge(s_v_ps, 2 * it + PRE)
                nc.vector.tensor_copy(h_att[0][0:KC, :, :], h_full[:, :, :]).then_inc(s_hhi_a, 1)

            def qk_low(it, n):
                dve.wait_ge(s_qk_hi, QK_USES * it + n + 1)
                tiles = slice(2 * n, min(2 * n + 2, QK_TILES))
                rows = QK_ROWS if tiles.stop < QK_TILES else 2 * C - QK_ROWS * (QK_TILES - 1)
                width = (tiles.stop - tiles.start) * T
                tt(qk[1][0:rows, tiles, :].rearrange("p a t -> p (a t)"), qk_bank[n][0:rows, 0:width],
                   qk[0][0:rows, tiles, :].rearrange("p a t -> p (a t)").bitcast(F32), ALU.subtract)\
                    .then_inc(s_qk_lo, 1)

            def unit_max(it, u):
                dve.wait_ge(s_score, 8 * it + u + 1)
                if u == 0:
                    dve.wait_ge(s_max_ps, it + PRE)
                nc.vector.tensor_reduce(out=maxima[:, :, :, u].rearrange("p q r -> p r q"), in_=scores[u % 2][:, :, :, :],
                                        axis=AX.X, op=ALU.max).then_inc(s_max, 1)

            def inverse_sums(it, half):
                dve.wait_ge(s_sum, 2 * it + half + 1)
                nc.vector.reciprocal(inv_sum[:, half, :], spread_bank[half][:, :]).then_inc(s_inv, 1)

            def normalise(it, half):
                dve.wait_ge(s_inv, 2 * it + half + 1 + PRE)
                tt(o_full[:, half, :], o_full[:, half, :], inv_sum[:, half, :], ALU.mult).then_inc(s_o, 1)
                dve.wait_ge(s_o, 2 * it + half + 1)
                dve.wait_ge(s_proj, 2 * it + PRE)
                nc.vector.tensor_copy(o_att[0][:, half, :], o_full[:, half, :]).then_inc(s_o_hi, 1)

            def gate_projection(it):
                dve.wait_ge(s_gate_a, 16 * it + 16)
                for t in range(2):
                    dve.wait_ge(s_proj, 2 * it + t + 1 + PRE)
                    dve.wait_ge(s_x_out, 2 * it - 1 + t + PRE2)
                    tt(gated[:, t, :], token_bank[t][:, 0:C], gate_a[:, :], ALU.mult).then_inc(s_proj_gated, 1)

            def mlp_norm(it):
                norm(1, it, x_one, lambda t: dve.wait_ge(s_x_one, 2 * it + t + 1 + PRE), s_xhat_m)

            def mlp_high(it):
                dve.wait_ge(s_h_m, NCH * it + NCH)
                dve.wait_ge(s_up, UP_USES * it + PRE)
                nc.vector.tensor_copy(h_mlp[0][0:KC, :, :], h_full[:, :, :]).then_inc(s_hhi_m, 1)

            def gate_down(it, t):
                if t == 0:
                    dve.wait_ge(s_gate_f, 16 * it + 16)
                dve.wait_ge(s_down, 2 * it + t + 1 + PRE)
                tt(gated[:, t, :], token_bank[t][:, 0:C], gate_f[:, :], ALU.mult).then_inc(s_down_gated, 1)

            def prologue():
                attention_norm(0)
                x_hats(0, 0, x_in, s_xhat_a)
                attention_high(0)
                for n in range(QK_USES):
                    qk_low(0, n)
                attention_norm(1)
                dve.wait_ge(s_tr_a, TRS)
                x_hats(0, 1, x_in, s_xhat_a)
                attention_high(1)
                for u in range(8):
                    unit_max(0, u)

            def half_step(l, b):
                it = l * B + b
                before, after, after_next = neighbours(l, b)
                if before:
                    gate_projection(it - 1)
                    mlp_norm(it - 1)
                if after:
                    qk_low(it + 1, 0)
                if before:
                    dve.wait_ge(s_tr_a, TRS * (it + 2 if after else it + 1))
                    x_hats(1, it - 1, x_one, s_xhat_m)
                if after:
                    qk_low(it + 1, 1)
                    qk_low(it + 1, 2)
                if after_next:
                    attention_norm(it + 2)
                if before:
                    mlp_high(it - 1)
                if after_next:
                    dve.wait_ge(s_tr_a, TRS * (it + 2))
                    dve.wait_ge(s_tr_m, TRS * it + PRE)
                    x_hats(0, it + 2, x_in, s_xhat_a)
                inverse_sums(it, 0)
                inverse_sums(it, 1)
                normalise(it, 0)
                normalise(it, 1)
                for u in range(8):
                    if u == 7 and after_next:
                        attention_high(it + 2)
                    if u == 7 and before:
                        gate_down(it - 1, 0)
                    if after:
                        unit_max(it + 1, u)
                if before:
                    gate_down(it - 1, 1)

            def epilogue():
                it = L * B - 1
                gate_projection(it)
                mlp_norm(it)
                dve.wait_ge(s_tr_a, TRS * (it + 1))
                x_hats(1, it, x_one, s_xhat_m)
                mlp_high(it)
                gate_down(it, 0)
                gate_down(it, 1)

            whole_run(dve, prologue, half_step, epilogue)


def _in_chunks(np, weight, bias):
    n = weight.shape[1]
    out = np.zeros((KC + 1, NCH, n), weight.dtype)
    out[0:KC] = weight.reshape(NCH, KC, n).transpose(1, 0, 2)
    out[KC, NCH - 1] = bias
    return out


def _by_head(np, weight, bias):
    out = np.zeros((P, NG, C), weight.dtype)
    for g in range(NG):
        for i in range(4):
            out[32 * i:32 * i + HD, g] = weight[(4 * g + i) * HD:(4 * g + i + 1) * HD]
    out[HD, 0] = bias
    return out


_LAYERS = [
    dict(qkv=("L1_cond_W_qkv", "L1_cond_b_qkv"), out=("L1_cond_W_proj", "L1_cond_b_proj"),
         up=("L1_cond_W_fc1", "L1_cond_b_fc1"), down=("L1_cond_W_fc2", "L1_cond_b_fc2"),
         ada=("L1_cond_W_ada", "L1_cond_b_ada")),
    dict(qkv=("L2_cond_qkv_w", "L2_cond_qkv_b"), out=("L2_cond_out_w", "L2_cond_out_b"),
         up=("L2_cond_w1", "L2_cond_b1"), down=("L2_cond_w2", "L2_cond_b2"),
         ada=("L2_cond_ada_w", "L2_cond_ada_b")),
    dict(qkv=("L3_cond_w_qkv", "L3_cond_b_qkv"), out=("L3_cond_w_proj", "L3_cond_b_proj"),
         up=("L3_cond_w_fc1", "L3_cond_b_fc1"), down=("L3_cond_w_fc2", "L3_cond_b_fc2"),
         ada=("L3_cond_w_ada", "L3_cond_b_ada")),
]


def _layout(np, inputs):
    a = {k: np.asarray(v) for k, v in inputs.items()}
    f = np.float32
    upper = np.triu_indices(R, k=1)
    index = np.zeros((R, R), np.int64)
    index[upper] = np.arange(len(upper[0]))
    index = index + index.T
    signs = (np.triu(np.ones((R, R)), 1) - np.tril(np.ones((R, R)), -1)) * 2.0 ** -SQUARINGS
    selector = np.zeros((P, P), f)
    for i in range(4):
        selector[32 * i + HD, 32 * i:32 * i + 32] = 1.0
    pick = lambda key, lay: np.stack([lay(np, a[w[key][0]], a[w[key][1]]) for w in _LAYERS])
    return {
        "x": a["x"].reshape(B, 2, P, C).transpose(0, 2, 1, 3),
        "cond_t": a["cond_1152"].T.reshape(NCH, KC, B).transpose(1, 0, 2),
        "p_t": a["L0_cond_P"].T,
        "p_nat": a["L0_cond_P"].reshape(NCH, KC, R).transpose(1, 0, 2),
        "w_rot": _in_chunks(np, a["L0_cond_W"].T[:, index.reshape(-1)], a["L0_cond_b"][index.reshape(-1)]),
        "w_ada": pick("ada", _in_chunks),
        "w_in": pick("qkv", _in_chunks),
        "w_out": pick("out", _by_head),
        "w_up": pick("up", _in_chunks),
        "w_down": np.stack([a[w["down"][0]].reshape(NF, P, C).transpose(1, 0, 2) for w in _LAYERS]),
        "b_down": np.stack([a[w["down"][1]] for w in _LAYERS]),
        "ident": np.eye(P, dtype=f),
        "half_ident": 0.5 * np.eye(P, dtype=f),
        "skew_mask": np.concatenate([signs, signs]).astype(f),
        "sel": selector,
    }


def build(nc, dram):
    dram["v_scratch"] = nc.dram_tensor("v_scratch", (B, R * R), F32, kind="Internal").ap()
    dram["gate_scratch"] = nc.dram_tensor("gate_scratch", (L, B, 2 * C), F32, kind="Internal").ap()
    dram["qk_scratch"] = nc.dram_tensor("qk_scratch", (2, 2, H // 2, 2, HD, T), F32, kind="Internal").ap()
    with ExitStack() as ctx:
        def sb(name, shape):
            return ctx.enter_context(nc.sbuf_tensor(name, shape, F32))

        keep = {"ident": sb("ident", [P, P]), "mods": sb("mods", [KC, 12, L * B])}
        with ExitStack() as inner:
            for name, shape in (("u_twice", [KC, NCH, P]), ("g_rot", [P, NPAIR, C])):
                keep[name] = inner.enter_context(nc.sbuf_tensor(name, shape, F32))
            rotation_setup(nc, dram, keep)
            apply_rotation(nc, dram, keep)
        layers(nc, dram, keep)


def kernel(**inputs):
    import numpy as _np
    import concourse.bacc as _bacc
    from concourse import mybir as _mybir
    from concourse.bass_utils import run_bass_kernel_spmd as _run

    nc = _bacc.Bacc("TRN2", target_bir_lowering=False, num_devices=1)
    arrays, dram = {}, {}
    for name, a in _layout(_np, inputs).items():
        arrays[f"in_{name}"] = _np.ascontiguousarray(a)
        dram[name] = nc.dram_tensor(f"in_{name}", a.shape, _mybir.dt.from_np(a.dtype), kind="ExternalInput").ap()
    dram["out"] = nc.dram_tensor("out_x", (B, P, 2, C), F32, kind="ExternalOutput").ap()
    build(nc, dram)
    r = _run(nc, [arrays], core_ids=[0])
    got = _np.asarray(r.results[0]["out_x"])
    return got.transpose(0, 2, 1, 3).reshape(B, T, C)
```

```python
from contextlib import ExitStack

import concourse.bass as bass
from concourse import mybir

F32 = mybir.dt.float32
F32R = mybir.dt.float32r
ALU = mybir.AluOpType
ACT = mybir.ActivationFunctionType
AX = mybir.AxisListType

P = 128
B, T, C = 16, 256, 288
R = 64
L = 3
H = 16
HD = C // H
KC, NCH = 96, 3
FF = 4 * C
NPAIR = B // 2
SQUARINGS = 8
EPS = 1e-6
MOD_COLUMNS = [k * C + c * KC for k in (0, 3, 1, 4) for c in range(NCH)]
GATE_COLUMNS = [2 * C, 5 * C]
NG = H // 4
NF = FF // P
QK_ROWS, QK_TILES = 7 * HD, 5
QK_USES, UP_USES = 3, 5
SCALE = float(HD) ** -0.5


def rotation_setup(nc, dram, keep):
    mods, u_twice, g_rot = keep["mods"], keep["u_twice"], keep["g_rot"]
    ident = keep["ident"]
    with ExitStack() as ctx:
        def sb(name, shape, dt=F32):
            return ctx.enter_context(nc.sbuf_tensor(name, shape, dt))

        def sem(name):
            return ctx.enter_context(nc.semaphore(name))

        cond = sb("cond", [KC, NCH, B])
        silu_c = sb("silu_c", [KC + 1, NCH, B])
        w_ada = sb("w_ada", [KC + 1, L, NCH, 6 * C])
        gates = sb("gates", [B, L, 2 * C])
        w_rot = sb("w_rot", [KC + 1, NCH, R * R])
        v_rot = sb("v_rot", [B, R * R])
        a_raw = sb("a_rows", [P, NPAIR, R])
        skew_mask = sb("skew_mask", [P, R])
        a_pos = sb("a_pos", [P, NPAIR, P])
        a_neg = sb("a_neg", [P, NPAIR, P])
        a_sq = sb("a_sq", [P, NPAIR, P])
        a_4 = sb("a_4", [P, NPAIR, P])
        even = sb("even", [P, NPAIR, P])
        inner_odd = sb("inner_odd", [P, NPAIR, P])
        outer_odd = sb("outer_odd", [P, NPAIR, P])
        e_mat = sb("e_mat", [P, NPAIR, P])
        f_mat = sb("f_mat", [P, NPAIR, P])
        p_t = sb("p_t", [R, C])
        p_nat = sb("p_nat", [KC, NCH, R])
        ones = sb("ones", [R, P])
        lower = sb("lower", [R, 2, R])
        pivot = sb("pivot", [R, 2, P])
        top = sb("top", [R, R])
        gram = sb("gram", [R, 2 * R])
        col = sb("col", [R, 2, 8])
        root = sb("root", [R, 2, 2])
        beta_all = sb("beta_all", [R, R])
        beta_diag = sb("beta_diag", [R, R])
        beta_col = sb("beta_col", [R, 2])
        c_mat = sb("c_mat", [R, R])
        c_t = sb("c_t", [R, 2, R])
        u_t = sb("u_t", [P, C])
        qr_ps = ctx.enter_context(nc.psum_tensor("qr_ps", [P, 2, 512], F32))
        ps_a = ctx.enter_context(nc.psum_tensor("ps_a", [P, 2, 512], F32))
        ps_b = ctx.enter_context(nc.psum_tensor("ps_b", [P, 2, 512], F32))
        ada_ps = ctx.enter_context(nc.psum_tensor("ada_ps", [P, 2, 512], F32))

        s_cond = sem("s_cond")
        s_const = sem("s_const")
        s_p = sem("s_p")
        s_wada = [sem(f"s_wada{l}") for l in range(L)]
        s_wrot = [sem(f"s_wrot{n}") for n in range(4)]
        s_ones = sem("s_ones")
        s_silu = sem("s_silu")
        s_ada_ps = sem("s_ada_ps")
        s_ada_out = sem("s_ada_out")
        s_gates = sem("s_gates")
        s_gates_st = sem("s_gates_st")
        s_rot_ps = sem("s_rot_ps")
        s_rot_out = sem("s_rot_out")
        s_v_st = sem("s_v_st")
        s_a_ld = sem("s_a_ld")
        s_chain = sem("s_chain")
        s_exp_ps = sem("s_exp_ps")
        s_exp_sb = sem("s_exp_sb")
        s_sq_ps = sem("s_sq_ps")
        s_sq = sem("s_sq")
        s_g0 = sem("s_g0")
        s_qr_init = sem("s_qr_init")
        s_pivot = sem("s_pivot")
        s_row_g = sem("s_row_g")
        s_row_t = sem("s_row_t")
        s_pivot_g = sem("s_pivot_g")
        s_root = sem("s_root")
        s_gram = sem("s_gram")
        s_top = sem("s_top")
        s_beta = sem("s_beta")
        s_u_ps = sem("s_u_ps")
        s_u_sb = sem("s_u_sb")
        s_gr_ps = sem("s_gr_ps")
        s_gr_sb = sem("s_gr_sb")
        block = ctx.enter_context(nc.Block())
        EARLY, GROUP, PER_ROUND = R - 6 * SQUARINGS, 8, 6
        SQUARED = ((0,), (1, 2), (3,), (4,), (5, 6), (7,))

        def elimination(engine, step, square=None):
            with engine.Fori(0, EARLY // GROUP) as r:
                for k in range(GROUP):
                    step(r * GROUP + k, k % 2, lambda n: None, ())
            yield
            with engine.Fori(0, SQUARINGS) as r:
                for k in range(PER_ROUND):
                    step(r * PER_ROUND + (EARLY + k), k % 2, (lambda n: square(r, n)) if square else None, SQUARED[k])
            yield

        @block.sync
        def _(sp):
            sp.dma_start(p_t[:, :], dram["p_t"]).then_inc(s_p, 16)
            sp.dma_start(p_nat[:, :, :], dram["p_nat"]).then_inc(s_p, 16)
            sp.dma_start(ident[:, :], dram["ident"]).then_inc(s_const, 16)
            sp.dma_start(lower[:, :, :], dram["lower"]).then_inc(s_const, 16)
            sp.dma_start(skew_mask[:, :], dram["skew_mask"]).then_inc(s_const, 16)
            sp.dma_start(cond[:, :, :], dram["cond_t"]).then_inc(s_cond, 16)
            for n in range(4):
                part = slice(n * 1024, (n + 1) * 1024)
                sp.dma_start(w_rot[:, :, part], dram["w_rot"][:, :, part]).then_inc(s_wrot[n], 16)
            for l in range(L):
                sp.dma_start(w_ada[:, l, :, :], dram["w_ada"][l]).then_inc(s_wada[l], 16)
            sp.wait_ge(s_rot_out, 8)
            sp.dma_start(dram["v_scratch"], v_rot[:, :]).then_inc(s_v_st, 16)
            sp.wait_ge(s_v_st, 16)
            a_view = dram["v_scratch"].rearrange("(n two) (i j) -> two i n j", two=2, i=R)
            for half in range(2):
                sp.dma_start(a_raw[half * R:(half + 1) * R, :, :], a_view[half]).then_inc(s_a_ld, 16)
            sp.wait_ge(s_gates, 2 * L)
            sp.dma_start(dram["gate_scratch"].rearrange("l b c -> b l c"), gates[:, :, :]).then_inc(s_gates_st, 16)
            sp.wait_ge(s_gates_st, 16)

        @block.scalar
        def _(act):
            act.wait_ge(s_cond, 16)
            nc.scalar.activation(silu_c[0:KC, :, :], cond[:, :, :], ACT.Silu).then_inc(s_silu, 1)
            act.wait_ge(s_ones, 1)
            nc.scalar.activation(root[0:1, 0, 0:1], ones[0:1, 0:1], ACT.Sqrt).then_inc(s_root, 1)
            act.wait_ge(s_const, 48)
            for j in range(2):
                nc.scalar.activation(pivot[:, j, :], ones[:, :], ACT.Copy, scale=ident[0:R, j:j + 1])\
                    .then_inc(s_pivot, 1)

            def step(j, parity, square, pairs):
                act.wait_ge(s_pivot_g, j + 1)
                for n, scale in enumerate((1.0, 4.0)):
                    nc.scalar.activation(root[:, parity, n:n + 1], col[:, parity, 0:1], ACT.Sqrt,
                                         scale=scale).then_inc(s_root, 1)
                act.wait_ge(s_row_t, j + 1)
                nc.scalar.activation(pivot[:, parity, :], ones[:, :], ACT.Copy,
                                     scale=ident[0:R, bass.ds(j + 2, 1)]).then_inc(s_pivot, 1)

            steps = elimination(act, step)
            next(steps)
            for n in range(8):
                act.wait_ge(s_rot_ps, n + 1)
                nc.scalar.activation(v_rot[:, n * 512:(n + 1) * 512], ps_b[0:B, n % 2, :],
                                     ACT.Copy).then_inc(s_rot_out, 1)
            next(steps)

        @block.tensor
        def _(pe):
            mm = nc.tensor.matmul
            pe.wait_ge(s_p, 32)
            for c in range(NCH):
                last = mm(ps_a[0:R, 0, 0:R], p_nat[:, c, :], p_nat[:, c, :], start=c == 0, stop=c == NCH - 1)
            last.then_inc(s_g0, 1)
            pe.wait_ge(s_qr_init, 3)

            def step(j, parity, square, pairs):
                pe.wait_ge(s_pivot, j + 1)
                pe.wait_ge(s_gram, 3 * j + 1)
                mm(qr_ps[:, 0, 0:2 * R], pivot[:, parity, :], gram[:, :], start=True, stop=True).then_inc(s_row_g, 1)
                pe.wait_ge(s_top, 7 * j + 1)
                mm(qr_ps[:, 1, 0:R], pivot[:, parity, :], top[:, :], start=True, stop=True).then_inc(s_row_t, 1)
                for n in pairs:
                    square(n)

            def square(r, n):
                pe.wait_ge(s_sq, 2 * NPAIR * r + 2 * n + 14)
                bank = ps_a[:, n % 2, :]
                mm(bank[:, 0:P], f_mat[:, n, :], e_mat[:, n, :], start=True, stop=True)
                mm(bank[:, P:2 * P], e_mat[:, n, :], f_mat[:, n, :], start=True, stop=True).then_inc(s_sq_ps, 1)

            steps = elimination(pe, step, square)
            next(steps)
            pe.wait_ge(s_silu, 3)
            for n in range(8):
                pe.wait_ge(s_wrot[n // 2], 16)
                if n >= 2:
                    pe.wait_ge(s_rot_out, n - 1)
                for c in range(NCH):
                    k = KC + (c == NCH - 1)
                    last = mm(ps_b[0:B, n % 2, :], silu_c[0:k, c, :],
                              w_rot[0:k, c, n * 512:(n + 1) * 512], start=c == 0, stop=c == NCH - 1)
                last.then_inc(s_rot_ps, 1)

            def modulation(l, outputs):
                if 0 in outputs:
                    pe.wait_ge(s_wada[l], 16)
                    if l:
                        pe.wait_ge(s_ada_out, 2 * l)
                        pe.wait_ge(s_gates, 2 * l)
                for n in outputs:
                    src = MOD_COLUMNS[n]
                    for c in range(NCH):
                        k = KC + (c == NCH - 1)
                        mm(ada_ps[0:KC, 0, n * B:(n + 1) * B], w_ada[0:k, l, c, src:src + KC],
                           silu_c[0:k, c, :], start=c == 0, stop=c == NCH - 1)

            def gate_rows(l):
                for n, src in enumerate(GATE_COLUMNS):
                    for c in range(NCH):
                        k = KC + (c == NCH - 1)
                        last = mm(ada_ps[0:B, n, 192:192 + C], silu_c[0:k, c, :], w_ada[0:k, l, c, src:src + C],
                                  start=c == 0, stop=c == NCH - 1)
                last.then_inc(s_ada_ps, 1)

            modulation(0, range(12))
            gate_rows(0)

            def product(out, lhs, rhs):
                for n in range(NPAIR):
                    last = mm(out[:, n // 4, (n % 4) * P:(n % 4 + 1) * P], lhs[:, n, :], rhs[:, n, :],
                              start=True, stop=True)
                last.then_inc(s_exp_ps, 1)

            pe.wait_ge(s_exp_sb, 1)
            product(ps_a, a_neg, a_pos)
            modulation(1, range(0, 4))
            pe.wait_ge(s_exp_sb, 2)
            product(ps_b, a_sq, a_sq)
            modulation(1, range(4, 8))
            pe.wait_ge(s_exp_sb, 4)
            product(ps_a, a_4, inner_odd)
            pe.wait_ge(s_exp_sb, 5)
            product(ps_b, a_4, even)
            modulation(1, range(8, 12))
            pe.wait_ge(s_exp_sb, 6)
            product(ps_a, a_neg, outer_odd)
            gate_rows(1)
            modulation(2, range(12))
            gate_rows(2)
            next(steps)
            pe.wait_ge(s_u_sb, 1)
            nc.tensor.transpose(qr_ps[0:R, 0, 0:R], c_mat[:, :], ident[0:R, 0:R]).then_inc(s_u_ps, 1)
            pe.wait_ge(s_u_sb, 3)
            for c in range(NCH):
                last = mm(ps_a[0:KC, 0, c * R:(c + 1) * R], p_t[:, c * KC:(c + 1) * KC], c_t[:, 0, :],
                          start=True, stop=True)
            mm(ps_a[:, 1, 0:C], c_t[:, :, :], p_t[:, :], start=True, stop=True).then_inc(s_u_ps, 1)
            pe.wait_ge(s_u_sb, 6)
            for n in range(NPAIR):
                if n >= 2:
                    pe.wait_ge(s_gr_sb, n - 1)
                mm(ps_b[:, n % 2, 0:C], f_mat[:, n, :], u_t[:, :], start=True, stop=True)\
                    .then_inc(s_gr_ps, 1)

        @block.vector
        def _(dve):
            V = nc.vector
            V.memset(ones[:, :], 1.0).then_inc(s_ones, 1)
            V.memset(silu_c[KC:KC + 1, :, :], 1.0).then_inc(s_silu, 2)
            V.memset(a_pos[:, :, :], 0.0).then_inc(s_chain, 1)
            dve.wait_ge(s_p, 32)
            V.tensor_copy(top[:, :], p_t[:, 0:R]).then_inc(s_qr_init, 1)
            dve.wait_ge(s_const, 48)
            V.tensor_copy(gram[:, R:2 * R], ident[0:R, 0:R]).then_inc(s_qr_init, 1)
            dve.wait_ge(s_g0, 1)
            V.tensor_copy(gram[:, 0:R], ps_a[0:R, 0, 0:R]).then_inc(s_qr_init, 1)
            dve.sem_inc(s_gram, 1)
            dve.sem_inc(s_top, 1)
            dve.wait_ge(s_qr_init, 3)

            def step(j, parity, square, pairs):
                g, t = qr_ps[0:R, 0, :], qr_ps[0:R, 1, :]
                c = [col[:, parity, n:n + 1] for n in range(8)]
                norm, twice = root[:, parity, 0:1], root[:, parity, 1:2]
                beta = beta_all[:, bass.ds(j, 1)]
                fill = list(pairs)

                def beside():
                    if fill:
                        square(fill.pop(0))

                dve.wait_ge(s_row_g, j + 1)
                V.reciprocal(c[1], g[:, bass.ds(j, 1)]).then_inc(s_gram, 1)
                V.tensor_copy(c[0], g[:, bass.ds(j, 1)]).then_inc(s_pivot_g, 1)
                dve.wait_ge(s_gram, 3 * j + 2)
                V.tensor_scalar(c[2], gram[:, bass.ds(j, 1)], c[1], lower[:, 1, bass.ds(j, 1)],
                                ALU.mult, ALU.mult).then_inc(s_gram, 1)
                dve.wait_ge(s_gram, 3 * j + 3)
                V.scalar_tensor_tensor(out=gram[:, :], in0=g[:, 0:2 * R], scalar=c[2], in1=gram[:, :],
                                       op0=ALU.mult, op1=ALU.add).then_inc(s_gram, 1)
                dve.wait_ge(s_row_t, j + 1)
                dve.wait_ge(s_root, 2 * j + 3)
                alpha = t[:, bass.ds(j, 1)]
                V.tensor_scalar(c[3], alpha, 0.0, twice, ALU.is_lt, ALU.mult).then_inc(s_top, 1)
                dve.wait_ge(s_top, 7 * j + 2)
                V.tensor_scalar(c[5], c[3], norm, alpha, ALU.subtract, ALU.subtract).then_inc(s_top, 1)
                V.tensor_scalar(beta, c[3], norm, None, ALU.subtract).then_inc(s_top, 1)
                beside()
                dve.wait_ge(s_top, 7 * j + 3)
                V.reciprocal(c[6], c[5]).then_inc(s_top, 1)
                dve.wait_ge(s_top, 7 * j + 4)
                V.scalar_tensor_tensor(out=c[4], in0=c[2], scalar=beta, in1=top[:, bass.ds(j, 1)],
                                       op0=ALU.mult, op1=ALU.add).then_inc(s_top, 1)
                beside()
                dve.wait_ge(s_top, 7 * j + 6)
                V.tensor_scalar(c[7], c[4], c[6], lower[:, 0, bass.ds(j, 1)], ALU.mult, ALU.mult).then_inc(s_top, 1)
                dve.wait_ge(s_top, 7 * j + 7)
                V.scalar_tensor_tensor(out=top[:, :], in0=t[:, 0:R], scalar=c[7], in1=top[:, :],
                                       op0=ALU.mult, op1=ALU.add).then_inc(s_top, 1)

            def square(r, n):
                dve.wait_ge(s_sq_ps, NPAIR * r + n + 1)
                for m, part in ((e_mat, slice(0, P)), (f_mat, slice(P, 2 * P))):
                    V.scalar_tensor_tensor(out=m[:, n, :], in0=m[:, n, :], scalar=2.0, in1=ps_a[:, n % 2, part],
                                           op0=ALU.mult, op1=ALU.add).then_inc(s_sq, 1)

            steps = elimination(dve, step, square)
            next(steps)

            def modulation_out(l):
                dve.wait_ge(s_ada_ps, l + 1)
                mp = ada_ps[0:KC, 0, 0:12 * B].rearrange("p (n b) -> p n b", b=B)
                V.tensor_copy(mods[:, 0:6, l * B:(l + 1) * B], mp[:, 0:6, :]).then_inc(s_ada_out, 1)
                V.tensor_scalar(mods[:, 6:12, l * B:(l + 1) * B], mp[:, 6:12, :], 1.0, None,
                                ALU.add).then_inc(s_ada_out, 1)
                for n in range(2):
                    V.tensor_copy(gates[:, l, n * C:(n + 1) * C], ada_ps[0:B, n, 192:192 + C]).then_inc(s_gates, 1)

            modulation_out(0)
            dve.wait_ge(s_a_ld, 32)
            dve.wait_ge(s_chain, 1)
            for half in range(2):
                h = slice(half * R, (half + 1) * R)
                V.tensor_tensor(a_pos[h, :, h], a_raw[h, :, :],
                                skew_mask[h, :].unsqueeze(1).to_broadcast([R, NPAIR, R]),
                                ALU.mult).then_inc(s_chain, 1)
            dve.wait_ge(s_chain, 3)
            V.tensor_scalar(a_neg[:, :, :], a_pos[:, :, :], -1.0, None, ALU.mult).then_inc(s_exp_sb, 1)
            unit = ident[:, :].unsqueeze(1).to_broadcast([P, NPAIR, P])

            def blocks(ps):
                return ps[:, :, :].rearrange("p h (n c) -> p (h n) c", c=P)

            def scaled_sum(out, in0, scalar, in1, op=ALU.add):
                return V.scalar_tensor_tensor(out=out[:, :, :], in0=in0, scalar=scalar, in1=in1, op0=ALU.mult, op1=op)

            dve.wait_ge(s_exp_ps, 1)
            V.tensor_copy(a_sq[:, :, :], blocks(ps_a)).then_inc(s_exp_sb, 1)
            dve.wait_ge(s_exp_sb, 2)
            scaled_sum(inner_odd, a_sq[:, :, :], 1 / 42, unit).then_inc(s_exp_sb, 1)
            scaled_sum(even, a_sq[:, :, :], 1 / 30, unit).then_inc(s_chain, 1)
            dve.wait_ge(s_exp_ps, 2)
            V.tensor_copy(a_4[:, :, :], blocks(ps_b)).then_inc(s_exp_sb, 1)
            dve.wait_ge(s_exp_sb, 4)
            dve.wait_ge(s_chain, 4)
            scaled_sum(even, a_4[:, :, :], 1 / 1680, even[:, :, :]).then_inc(s_exp_sb, 1)
            scaled_sum(outer_odd, a_sq[:, :, :], 1 / 6, unit).then_inc(s_chain, 1)
            dve.wait_ge(s_exp_ps, 3)
            dve.wait_ge(s_chain, 5)
            scaled_sum(outer_odd, blocks(ps_a), 1 / 120, outer_odd[:, :, :]).then_inc(s_exp_sb, 1)
            dve.wait_ge(s_exp_ps, 4)
            scaled_sum(even, blocks(ps_b), 1 / 12, a_sq[:, :, :]).then_inc(s_chain, 1)
            dve.wait_ge(s_exp_ps, 5)
            dve.wait_ge(s_chain, 6)
            scaled_sum(e_mat, even[:, :, :], 0.5, blocks(ps_a)).then_inc(s_chain, 1)
            scaled_sum(f_mat, even[:, :, :], 0.5, blocks(ps_a), ALU.subtract).then_inc(s_sq, 2 * NPAIR)
            modulation_out(1)
            modulation_out(2)
            dve.wait_ge(s_chain, 7)
            next(steps)
            dve.wait_ge(s_top, 7 * R + 1)
            V.tensor_tensor(beta_diag[:, :], beta_all[:, :], ident[0:R, 0:R], ALU.mult).then_inc(s_beta, 1)
            dve.wait_ge(s_beta, 1)
            V.tensor_reduce(out=beta_col[:, 0:1], in_=beta_diag[:, :], axis=AX.X, op=ALU.add).then_inc(s_beta, 1)
            dve.wait_ge(s_beta, 2)
            V.reciprocal(beta_col[:, 1:2], beta_col[:, 0:1]).then_inc(s_beta, 1)
            dve.wait_ge(s_beta, 3)
            dve.wait_ge(s_gram, 3 * R + 1)
            V.tensor_scalar(c_mat[:, :], gram[:, R:2 * R], beta_col[:, 1:2], None, ALU.mult).then_inc(s_u_sb, 1)
            dve.wait_ge(s_u_ps, 1)
            for n in range(2):
                V.tensor_copy(c_t[:, n, :], qr_ps[0:R, 0, 0:R]).then_inc(s_u_sb, 1)
            dve.wait_ge(s_u_ps, 2)
            u_ps = ps_a[0:KC, 0, 0:NCH * R].rearrange("p (c r) -> p c r", r=R)
            for n in range(2):
                V.tensor_copy(u_twice[:, :, n * R:(n + 1) * R], u_ps).then_inc(s_u_sb, 1)
            V.tensor_copy(u_t[:, :], ps_a[:, 1, 0:C]).then_inc(s_u_sb, 1)
            for n in range(NPAIR):
                dve.wait_ge(s_gr_ps, n + 1)
                V.tensor_copy(g_rot[:, n, :], ps_b[:, n % 2, 0:C]).then_inc(s_gr_sb, 1)


def apply_rotation(nc, dram, keep):
    ident, u_twice, g_rot = keep["ident"], keep["u_twice"], keep["g_rot"]
    with ExitStack() as ctx:
        def sb(name, shape, dt=F32):
            return ctx.enter_context(nc.sbuf_tensor(name, shape, dt))

        def sem(name):
            return ctx.enter_context(nc.semaphore(name))

        AHEAD = 4
        x_in = sb("r_x", [P, AHEAD, 2, C])
        x_t = sb("r_xt", [KC, 2, NCH, T])
        z_t = sb("r_zt", [P, 2, T])
        g_now = sb("r_g", [P, 2, C])
        x_out = sb("r_out", [P, 2, 2, C])
        xt_ps = [ctx.enter_context(nc.psum_tensor(f"xt_ps{i}", [P, 2, 512], F32)) for i in range(2)]
        z_ps = ctx.enter_context(nc.psum_tensor("z_ps", [P, 2, 512], F32))
        d_ps = ctx.enter_context(nc.psum_tensor("d_ps", [P, 2, 512], F32))
        s_x = [sem(f"r_x{n}") for n in range(AHEAD)]
        s_xt_ps = sem("r_xt_ps")
        s_xt = sem("r_xt")
        s_z_ps = sem("r_z_ps")
        s_z = sem("r_z")
        s_g = sem("r_g")
        s_d_ps = sem("r_d_ps")
        s_out = sem("r_out")
        s_st = [sem("r_st0"), sem("r_st1")]
        s_tick = sem("r_tick")
        block = ctx.enter_context(nc.Block())
        PRE_D, PRE_OUT, PRE_Z = 2, 2, 1

        def batches(engine, step):
            with engine.Fori(0, B // AHEAD - 1) as m:
                for k in range(AHEAD):
                    step(m, k)
            for k in range(AHEAD):
                step(B // AHEAD - 1, k)

        def follows(m, k, n):
            return not isinstance(m, int) or AHEAD * m + k + n < B

        @block.sync
        def _(sp):
            for k in range(AHEAD):
                sp.dma_start(x_in[:, k, :, :], dram["x"][k]).then_inc(s_x[k], 16)

            def step(m, k):
                sp.wait_ge(s_out, 2 * (AHEAD * m + k) + 2 + PRE_OUT)
                sp.sem_inc(s_tick, 1)
                sp.dma_start(dram["out"][AHEAD * m + k], x_out[:, k % 2, :, :]).then_inc(s_st[k % 2], 16)
                if follows(m, k, AHEAD):
                    sp.dma_start(x_in[:, k, :, :], dram["x"][AHEAD * m + (k + AHEAD)]).then_inc(s_x[k], 16)

            batches(sp, step)
            for h in range(2):
                sp.wait_ge(s_st[h], 16 * (B // 2) + 16)

        @block.scalar
        def _(act):
            def copy_xt(i, k):
                act.wait_ge(s_xt_ps, i + 1)
                bank = xt_ps[k % 2]
                nc.scalar.activation(x_t[:, k % 2, 0:2, :], bank[0:KC, 0, :].rearrange("p (c t) -> p c t", t=T),
                                     ACT.Copy).then_inc(s_xt, 1)
                nc.scalar.activation(x_t[:, k % 2, 2, :], bank[0:KC, 1, 0:T], ACT.Copy).then_inc(s_xt, 1)

            def copy_z(i, k):
                act.wait_ge(s_z_ps, i + 1)
                nc.scalar.activation(z_t[:, k % 2, :], z_ps[:, k % 2, 0:T], ACT.Copy).then_inc(s_z, 1)

            act.sem_inc(s_z, PRE_Z)
            copy_xt(0, 0)
            copy_xt(1, 1)
            copy_z(0, 0)

            def step(m, k):
                i = AHEAD * m + k
                if follows(m, k, 2):
                    act.wait_ge(s_z_ps, i + 1)
                    copy_xt(i + 2, k)
                if follows(m, k, 1):
                    act.wait_ge(s_d_ps, 2 * i + PRE_D)
                    copy_z(i + 1, k + 1)

            batches(act, step)

        @block.tensor
        def _(pe):
            pe.sem_inc(s_d_ps, PRE_D)

            def transposes(m, k, ahead):
                slot, turn = (k + ahead) % AHEAD, (k + ahead) // AHEAD
                pe.wait_ge(s_x[slot], 16 * (m + turn) + 16)
                for c in range(NCH):
                    for t in range(2):
                        last = nc.tensor.transpose(
                            xt_ps[slot % 2][0:KC, c // 2, (c % 2) * T + t * P:(c % 2) * T + (t + 1) * P],
                            x_in[:, slot, t, c * KC:(c + 1) * KC], ident[:, :])
                last.then_inc(s_xt_ps, 1)

            def into_subspace(i, k):
                pe.wait_ge(s_xt, 2 * i + 2)
                for c in range(NCH):
                    last = nc.tensor.matmul(z_ps[:, k % 2, 0:T], u_twice[:, c, :], x_t[:, k % 2, c, :],
                                            start=c == 0, stop=c == NCH - 1)
                last.then_inc(s_z_ps, 1)

            transposes(0, 0, 0)
            transposes(0, 1, 0)
            into_subspace(0, 0)

            def step(m, k):
                i = AHEAD * m + k
                if follows(m, k, 2):
                    pe.wait_ge(s_xt, 2 * i + 2)
                    transposes(m, k, 2)
                if follows(m, k, 1):
                    pe.wait_ge(s_z, i + PRE_Z)
                    into_subspace(i + 1, k + 1)
                pe.wait_ge(s_z, i + 1 + PRE_Z)
                pe.wait_ge(s_g, 2 * m + k // 2 + 1)
                h = k % 2
                for t in range(2):
                    pe.wait_ge(s_out, 2 * i - 1 + t + PRE_OUT)
                    nc.tensor.matmul(d_ps[:, t, 0:C], z_t[h * R:(h + 1) * R, h, t * P:(t + 1) * P],
                                     g_now[h * R:(h + 1) * R, k // 2, :], start=True, stop=True).then_inc(s_d_ps, 1)

            batches(pe, step)

        @block.vector
        def _(dve):
            for h in range(2):
                dve.sem_inc(s_st[h], 16)
            dve.sem_inc(s_out, PRE_OUT)
            nc.vector.tensor_copy(g_now[:, 0, :], g_rot[:, 0, :]).then_inc(s_g, 1)

            def step(m, k):
                i = AHEAD * m + k
                if k % 2 == 0 and follows(m, k, 2):
                    nc.vector.tensor_copy(g_now[:, (k // 2 + 1) % 2, :].unsqueeze(1),
                                          g_rot[:, bass.ds(2 * m + k // 2 + 1, 1), :]).then_inc(s_g, 1)
                for t in range(2):
                    dve.wait_ge(s_d_ps, 2 * i + t + 1 + PRE_D)
                    if t == 0:
                        dve.wait_ge(s_st[k % 2], 16 * (2 * m + k // 2) + 16)
                    nc.vector.tensor_tensor(x_out[:, k % 2, t, :], d_ps[:, t, 0:C], x_in[:, k, t, :],
                                            ALU.add).then_inc(s_out, 1)

            batches(dve, step)


def layers(nc, dram, keep):
    ident, mods = keep["ident"], keep["mods"]
    with ExitStack() as ctx:
        def sb(name, shape, dt=F32):
            return ctx.enter_context(nc.sbuf_tensor(name, shape, dt))

        def sem(name):
            return ctx.enter_context(nc.semaphore(name))

        w_in = [sb(f"w_in{i}", [KC + 1, NCH, 3 * C], F32R) for i in range(2)]
        w_out = [sb(f"w_out{i}", [P, NG, C], F32R) for i in range(2)]
        w_up = [sb(f"w_up{i}", [KC + 1, NCH, FF], F32R) for i in range(2)]
        w_down = [sb(f"w_down{i}", [P, NF, C], F32R) for i in range(2)]
        b_down = [sb(f"b_down{i}", [1, C], F32R) for i in range(2)]
        staging = sb("staging", [P, 2, 3 * C])
        sel = sb("sel", [P, P])
        one_row = sb("one_row", [1, P], F32R)
        x_in = sb("x_in", [P, 2, C])
        x_mid = sb("x_mid", [P, 2, C])
        x_one = sb("x_one", [P, 2, C])
        x_out = sb("x_out", [P, 2, C])
        gated = sb("gated", [P, 2, C])
        gate_a = sb("gate_a", [P, C])
        gate_f = sb("gate_f", [P, C])
        stats = sb("stats", [P, 2, 6])
        mean_var = sb("mean_var", [P, 2, 2])
        rstd = sb("rstd", [P, 2, 2])
        minus_half = sb("minus_half", [P, 2])
        x_hat = sb("x_hat", [P, 2, C])
        h_full = sb("h_full", [KC, NCH, T])
        h_att = [sb(f"h_att{i}", [KC + 1, NCH, T], F32R) for i in range(2)]
        h_mlp = [sb(f"h_mlp{i}", [KC + 1, NCH, T], F32R) for i in range(2)]
        qk = [sb(f"qk{i}", [QK_ROWS, QK_TILES, T], F32R) for i in range(2)]
        q_stack = sb("q_stack", [P, H // 2, T], F32R)
        k_stack = sb("k_stack", [P, H // 2, T], F32R)
        v_sb = sb("v_sb", [P, 2, H, 32])
        maxima = sb("maxima", [P, 2, 2, H // 2])
        neg_max = sb("neg_max", [H, T], F32R)
        probs = sb("probs", [P, 3, 2, 2, T])
        o_full = sb("o_full", [P, 2, 512])
        inv_sum = sb("inv_sum", [P, 2, 512])
        o_att = [sb(f"o_att{i}", [P, 2, 512], F32R) for i in range(2)]
        g_full = sb("g_full", [P, 2, 512])
        hidden = [sb(f"hidden{i}", [P, NF, T], F32R) for i in range(2)]

        scores = [ctx.enter_context(nc.psum_tensor(f"scores{i}", [P, 2, 2, T], F32)) for i in range(2)]
        pv_ps = ctx.enter_context(nc.psum_tensor("pv_ps", [P, 512], F32))
        sum_ps = ctx.enter_context(nc.psum_tensor("sum_ps", [P, 512], F32))
        att_ps = ctx.enter_context(nc.psum_tensor("att_ps", [P, 512], F32))
        mlp_ps = ctx.enter_context(nc.psum_tensor("mlp_ps", [P, 512], F32))
        qk_bank = (att_ps, mlp_ps, att_ps)
        token_bank = (mlp_ps, sum_ps)
        up_bank = (mlp_ps, sum_ps)
        spread_bank = (sum_ps, pv_ps)

        s_init = sem("s_init")
        s_sel = sem("s_sel")
        s_kinit = sem("s_kinit")
        s_half = sem("s_half")
        s_stage = [sem("s_stage0"), sem("s_stage1")]
        s_w_high = sem("s_w_high")
        s_w_low = sem("s_w_low")
        s_xin = sem("s_xin")
        s_xmid = sem("s_xmid")
        s_gate_a = sem("s_gate_a")
        s_gate_f = sem("s_gate_f")
        s_stats = [sem("s_stats_a"), sem("s_stats_m")]
        s_var = [sem("s_var_a"), sem("s_var_m")]
        s_rstd = [sem("s_rstd_a"), sem("s_rstd_m")]
        s_pow = [sem("s_pow_a"), sem("s_pow_m")]
        s_xhat_a = sem("s_xhat_a")
        s_xhat_m = sem("s_xhat_m")
        s_tr_a = sem("s_tr_a")
        s_tr_m = sem("s_tr_m")
        s_h_a = sem("s_h_a")
        s_h_m = sem("s_h_m")
        s_hhi_a = sem("s_hhi_a")
        s_hhi_m = sem("s_hhi_m")
        s_hlo_a = sem("s_hlo_a")
        s_hlo_m = sem("s_hlo_m")
        s_qk_ps = sem("s_qk_ps")
        s_qk_hi = sem("s_qk_hi")
        s_qk_lo = sem("s_qk_lo")
        s_qk_st = sem("s_qk_st")
        s_stack = sem("s_stack")
        s_v_ps = sem("s_v_ps")
        s_v = sem("s_v")
        s_score = sem("s_score")
        s_max = sem("s_max")
        s_max_ps = sem("s_max_ps")
        s_neg = sem("s_neg")
        s_neg_st = sem("s_neg_st")
        s_st = sem("s_st")
        s_exp = sem("s_exp")
        s_pv = sem("s_pv")
        s_o_full = sem("s_o_full")
        s_sum = sem("s_sum")
        s_inv = sem("s_inv")
        s_o = sem("s_o")
        s_o_hi = sem("s_o_hi")
        s_o_lo = sem("s_o_lo")
        s_proj = sem("s_proj")
        s_proj_gated = sem("s_proj_gated")
        s_x_one = sem("s_x_one")
        s_up = sem("s_up")
        s_gelu = sem("s_gelu")
        s_g_lo = sem("s_g_lo")
        s_down = sem("s_down")
        s_down_gated = sem("s_down_gated")
        s_x_out = sem("s_x_out")
        s_x_st = sem("s_x_st")
        s_tick = [sem("s_tick_sp"), sem("s_tick_pool"), sem("s_tick_dve")]

        block = ctx.enter_context(nc.Block())

        PRE_EXP, PRE_PV, G_PRE, PRE2, PRE = 2, 2, 2, 2, 1
        TRS = 2

        pieces = [(w_in, (slice(0, KC + 1), c, slice(0, 3 * C)), "w_in", KC + 1, 3 * C) for c in range(NCH)]
        pieces += [(w_out, (slice(0, P), slice(2 * n, 2 * n + 2), slice(0, C)), "w_out", P, 2 * C) for n in range(2)]
        pieces += [(w_up, (slice(0, KC + 1), c, slice(n * 576, (n + 1) * 576)), "w_up", KC + 1, 576)
                   for c in range(NCH) for n in range(2)]
        pieces += [(w_down, (slice(0, P), slice(3 * n, 3 * n + 3), slice(0, C)), "w_down", P, 3 * C) for n in range(3)]
        pieces += [(b_down, (slice(0, 1), slice(0, C)), "b_down", 1, C)]
        NP = len(pieces)
        OF = {name: range(a, b) for name, a, b in (("w_in", 0, 3), ("w_out", 3, 5), ("w_up", 5, 11), ("w_down", 11, 15))}

        def staged(n, view):
            _, _, _, rows, cols = pieces[n]
            part = staging[0:rows, n % 2, 0:cols]
            return part.rearrange("p (a c) -> p a c", c=C) if len(view) == 3 and isinstance(view[1], slice) else part

        def whole_run(engine, prologue, half_step, epilogue):
            prologue()
            half_step(0, 0)
            with engine.Fori(0, L - 1) as l:
                half_step(l, 1)
                with engine.Fori(2, B - 2) as b:
                    half_step(l, b)
                half_step(l, B - 2)
                half_step(l, B - 1)
                half_step(l + 1, 0)
            half_step(L - 1, 1)
            with engine.Fori(2, B - 2) as b:
                half_step(L - 1, b)
            half_step(L - 1, B - 2)
            half_step(L - 1, B - 1)
            epilogue()

        def neighbours(l, b):
            start = isinstance(l, int) and isinstance(b, int) and l == 0 and b == 0
            final = isinstance(l, int) and isinstance(b, int) and l == L - 1
            return not start, not (final and b >= B - 1), not (final and b >= B - 2)

        def at(b, n):
            return isinstance(b, int) and b == n

        @block.sync
        def _(sp):
            def hold(semaphore, value):
                sp.wait_ge(semaphore, value)
                sp.sem_inc(s_tick[0], 1)

            sp.sem_inc(s_x_st, 16 * B)
            sp.sem_inc(s_qk_st, 16)
            sp.sem_inc(s_stack, 16)
            sp.wait_ge(s_kinit, 1)
            sp.dma_start(sel[:, :], dram["sel"]).then_inc(s_sel, 16)
            sp.dma_start(x_in[:, :, :], dram["out"][0]).then_inc(s_xin, 16)
            qk_rows = dram["qk_scratch"].rearrange("s a b c d t -> s (a b c d) t")
            gate_rows = dram["gate_scratch"].rearrange("l b c -> (l b) c")
            FULL = QK_ROWS * (QK_TILES - 1)

            def load_x_in(it, b):
                hold(s_xhat_a, 2 * it)
                hold(s_x_st, 16 * it + 16)
                sp.dma_start(x_in[:, :, :], dram["out"][b]).then_inc(s_xin, 16)

            def stacks(it):
                for i, made in enumerate((s_qk_hi, s_qk_lo)):
                    hold(made, 3 * it + 3)
                    if i == 0:
                        hold(s_stack, 192 * it + 16)
                    sp.dma_start(qk_rows[i, 0:FULL, :].rearrange("(m p) t -> p m t", p=QK_ROWS),
                                 qk[i][:, 0:QK_TILES - 1, :].bitcast(F32)).then_inc(s_qk_st, 16)
                    sp.dma_start(qk_rows[i, FULL:2 * C, :],
                                 qk[i][0:2 * C - FULL, QK_TILES - 1, :].bitcast(F32)).then_inc(s_qk_st, 16)
                hold(s_qk_st, 64 * it + 80)
                hold(s_st, 8 * it + PRE)
                for n, (stack, order) in enumerate(((q_stack, (0, 1, 0)), (k_stack, (0, 0, 1)))):
                    for par in range(2):
                        for j, part in enumerate(order):
                            row = R * par + HD * j
                            sp.dma_start(stack[row:row + HD, :, :].bitcast(F32),
                                         dram["qk_scratch"][part, n, :, par].rearrange("b d t -> d b t"))\
                              .then_inc(s_stack, 16)

            def negated_maxima(it):
                hold(s_neg, it + 1 + PRE)
                for par in range(2):
                    row = R * par + 3 * HD
                    sp.dma_start(q_stack[row:row + 1, :, :].bitcast(F32),
                                 neg_max[par * 8:par * 8 + 8, :].bitcast(F32)).then_inc(s_neg_st, 16)

            def store(it, b):
                hold(s_x_out, 2 * it + 2 + PRE2)
                sp.dma_start(dram["out"][b], x_out[:, :, :]).then_inc(s_x_st, 16)

            def gate(it, tile, which, signal, free, count):
                hold(free, count)
                row = gate_rows[bass.ds(it, 1), which * C:(which + 1) * C]
                sp.dma_start(tile[:, :], row.rearrange("a c -> (a c)").partition_broadcast(P)).then_inc(signal, 16)

            def prologue():
                load_x_in(1, 1)
                stacks(0)

            def half_step(l, b):
                it = l * B + b
                before, after, after_next = neighbours(l, b)
                negated_maxima(it)
                hold(s_x_one, 2 * it + PRE)
                sp.dma_start(x_mid[:, :, :], dram["out"][b]).then_inc(s_xmid, 16)
                gate(it, gate_a, 0, s_gate_a, s_proj_gated, 2 * it + PRE)
                if after_next:
                    load_x_in(it + 2, (b + 2) % B if isinstance(b, int) else b + 2)
                if after:
                    stacks(it + 1)
                gate(it, gate_f, 1, s_gate_f, s_down_gated, 2 * it + PRE2)
                if before:
                    store(it - 1, (b - 1) % B if isinstance(b, int) else b - 1)

            def epilogue():
                store(L * B - 1, B - 1)

            whole_run(sp, prologue, half_step, epilogue)
            sp.wait_ge(s_x_st, 16 * B * (L + 1))

        @block.gpsimd
        def _(pool):
            tt = nc.gpsimd.tensor_tensor
            nc.gpsimd.memset(minus_half[:, :], -0.5).then_inc(s_half, 1)
            for sm in (s_x_one, s_o_lo, s_hlo_m):
                pool.sem_inc(sm, PRE)
            pool.sem_inc(s_x_out, PRE2)
            pool.sem_inc(s_g_lo, G_PRE)
            pool.wait_ge(s_half, 1)

            def inverse_deviation(order, it):
                pool.wait_ge(s_var[order], 2 * it + 2)
                pool.sem_inc(s_tick[1], 1)
                nc.gpsimd.tensor_scalar(rstd[:, 0, :], mean_var[:, :, 1], EPS, None, ALU.add).then_inc(s_pow[order], 1)
                pool.wait_ge(s_pow[order], it + 1)
                tt(rstd[:, 1, :], rstd[:, 0, :], minus_half[:, :], ALU.pow).then_inc(s_rstd[order], 1)

            def low(out, full, high, signal):
                tt(out, full, high.bitcast(F32), ALU.subtract).then_inc(signal, 1)

            def stage(l, n):
                _, view, name, rows, cols = pieces[n]
                src = dram[name][bass.ds(l, 1)]
                if name == "b_down":
                    pool.dma_start(staging[0:1, n % 2, 0:C], src).then_inc(s_stage[n % 2], 16)
                else:
                    src = src.rearrange("l p a c -> (l p) a c")[view]
                    pool.dma_start(staged(n, view), src).then_inc(s_stage[n % 2], 16)

            def low_weights(name, l, last_layer=False):
                for n in OF[name]:
                    pair, view = pieces[n][0:2]
                    pool.wait_ge(s_w_high, NP * l + n + 1)
                    low(pair[1][view], staged(n, view), pair[0][view], s_w_low)
                    follower = (l, n + 2) if n + 2 < NP else (l + 1, n % 2)
                    if n + 2 < NP or not last_layer:
                        pool.wait_ge(s_w_low, NP * l + n + 1)
                        stage(*follower)

            def attention_low(it):
                pool.wait_ge(s_hhi_a, it + 1)
                low(h_att[1][0:KC, :, :], h_full[:, :, :], h_att[0][0:KC, :, :], s_hlo_a)

            def prologue():
                stage(0, 0)
                stage(0, 1)
                low_weights("w_in", 0)
                inverse_deviation(0, 0)
                attention_low(0)
                inverse_deviation(0, 1)
                low_weights("w_out", 0)
                attention_low(1)

            def half_step(l, b):
                it = l * B + b
                before, after, after_next = neighbours(l, b)
                if before:
                    add_attention(it - 1)
                    inverse_deviation(1, it - 1)
                if at(b, 1):
                    low_weights("w_up", l)
                if after_next:
                    inverse_deviation(0, it + 2)
                if before:
                    mlp_low(it - 1)
                if at(b, 1):
                    low_weights("w_down", l, last_layer=isinstance(l, int) and l == L - 1)
                for half in range(2):
                    pool.wait_ge(s_o_hi, 2 * it + half + 1)
                    low(o_att[1][:, half, :], o_full[:, half, :], o_att[0][:, half, :], s_o_lo)
                if before:
                    hidden_low(it - 1)
                if after_next:
                    attention_low(it + 2)
                if at(b, B - 2) and after_next:
                    low_weights("w_in", l + 1)
                if at(b, 0) and before:
                    low_weights("w_out", l)
                if before:
                    add_mlp(it - 1)

            def add_attention(it):
                pool.wait_ge(s_xmid, 16 * it + 16)
                for t in range(2):
                    pool.wait_ge(s_proj_gated, 2 * it + t + 1 + PRE)
                    tt(x_one[:, t, :], x_mid[:, t, :], gated[:, t, :], ALU.add).then_inc(s_x_one, 1)

            def mlp_low(it):
                pool.wait_ge(s_hhi_m, it + 1)
                low(h_mlp[1][0:KC, :, :], h_full[:, :, :], h_mlp[0][0:KC, :, :], s_hlo_m)

            def hidden_low(it):
                for n in range(UP_USES):
                    tiles = slice(2 * n, min(2 * n + 2, NF))
                    width = (tiles.stop - tiles.start) * T
                    pool.wait_ge(s_gelu, 2 * (UP_USES * it + n + 1))
                    low(hidden[1][:, tiles, :].rearrange("p a t -> p (a t)"), g_full[:, n % 2, 0:width],
                        hidden[0][:, tiles, :].rearrange("p a t -> p (a t)"), s_g_lo)

            def add_mlp(it):
                for t in range(2):
                    pool.wait_ge(s_down_gated, 2 * it + t + 1 + PRE2)
                    if t == 0:
                        pool.wait_ge(s_x_st, 16 * it + 16 * B)
                    tt(x_out[:, t, :], x_one[:, t, :], gated[:, t, :], ALU.add).then_inc(s_x_out, 1)

            def epilogue():
                it = L * B - 1
                add_attention(it)
                inverse_deviation(1, it)
                mlp_low(it)
                hidden_low(it)
                add_mlp(it)

            whole_run(pool, prologue, half_step, epilogue)

        @block.scalar
        def _(act):
            act.sem_inc(s_exp, PRE_EXP)
            act.sem_inc(s_neg, PRE)
            act.sem_inc(s_neg_st, 16)
            act.sem_inc(s_v, PRE)
            act.sem_inc(s_o_full, PRE)
            act.wait_ge(s_init, 6)
            evict = nc.scalar.activation

            def high_weights(name, l, which=None):
                for n in OF[name] if which is None else [OF[name][k] for k in which]:
                    pair, view = pieces[n][0:2]
                    act.wait_ge(s_stage[n % 2], 16 * (l * ((NP + 1 - n % 2) // 2) + n // 2 + 1))
                    evict(pair[0][view], staged(n, view), ACT.Copy).then_inc(s_w_high, 1)

            def modulate(it, order, chunks):
                bank = (att_ps, mlp_ps)[order]
                for c in chunks:
                    act.wait_ge((s_tr_a, s_tr_m)[order], TRS * it + c // 2 + 1 + (PRE if order else 0))
                    mod = [mods[:, base + 3 * order + c, bass.ds(it, 1)] for base in (6, 0)]
                    evict(h_full[:, c, :], bank[0:KC, (c % 2) * T:(c % 2 + 1) * T], ACT.Identity, scale=mod[0],
                          bias=mod[1]).then_inc((s_h_a, s_h_m)[order], 1)

            def attention_modulate(it, chunks, a_before, m_before):
                if 0 in chunks:
                    if a_before is not None:
                        act.wait_ge(s_hlo_a, a_before)
                    if m_before is not None:
                        act.wait_ge(s_hlo_m, m_before + PRE)
                modulate(it, 0, chunks)

            def qk_high(it, n):
                act.wait_ge(s_qk_ps, QK_USES * it + n + 1)
                if n == 0:
                    act.wait_ge(s_qk_st, 64 * it + 16)
                tiles = slice(2 * n, min(2 * n + 2, QK_TILES))
                rows = QK_ROWS if tiles.stop < QK_TILES else 2 * C - QK_ROWS * (QK_TILES - 1)
                width = (tiles.stop - tiles.start) * T
                evict(qk[0][0:rows, tiles, :].rearrange("p a t -> p (a t)"), qk_bank[n][0:rows, 0:width], ACT.Copy)\
                    .then_inc(s_qk_hi, 1)

            def v_evict(it, kt):
                act.wait_ge(s_v_ps, 2 * it + kt + 1 + PRE)
                if kt == 0:
                    act.wait_ge(s_pv, NG * it + PRE_PV)
                evict(v_sb[:, kt, :, 0:HD], att_ps[:, 0:C].rearrange("p (h d) -> p h d", d=HD), ACT.Copy)\
                    .then_inc(s_v, 1)

            def negate_maxima(it):
                act.wait_ge(s_max_ps, it + 1 + PRE)
                act.wait_ge(s_neg_st, 32 * it + 16)
                evict(neg_max[:, :], att_ps[0:H, 0:T], ACT.Copy, scale=-1.0).then_inc(s_neg, 1)

            def exponentials(it, u):
                act.wait_ge(s_st, 8 * it + u + 1 + PRE)
                if u >= 3:
                    act.wait_ge(s_pv, NG * it + (u - 3) // 2 + 1 + PRE_PV)
                else:
                    act.wait_ge(s_pv, NG * it + PRE_PV)
                evict(probs[:, u % 3, :, :, :], scores[u % 2][:, :, :, :], ACT.Exp, scale=SCALE)\
                    .then_inc(s_exp, 1)

            def copy_o(it, half):
                act.wait_ge(s_pv, NG * it + 2 * half + 2 + PRE_PV)
                act.wait_ge(s_o_lo, 2 * it + PRE)
                evict(o_full[:, half, :], pv_ps[:, :], ACT.Copy).then_inc(s_o_full, 1)

            def gelu(it, n):
                act.wait_ge(s_up, UP_USES * it + n + 1 + PRE)
                act.wait_ge(s_g_lo, UP_USES * it + max(n - 1, 0) + G_PRE)
                if n == 0:
                    act.wait_ge(s_down, 2 * it + PRE)
                tiles = slice(2 * n, min(2 * n + 2, NF))
                width = (tiles.stop - tiles.start) * T
                bank = up_bank[n % 2]
                evict(g_full[:, n % 2, 0:width], bank[:, 0:width], ACT.Gelu_apprx_tanh).then_inc(s_gelu, 1)
                evict(hidden[0][:, tiles, :].rearrange("p a t -> p (a t)"), bank[:, 0:width], ACT.Gelu_apprx_tanh)\
                    .then_inc(s_gelu, 1)

            def prologue():
                high_weights("w_in", 0)
                attention_modulate(0, (0, 1, 2), None, None)
                for n in range(QK_USES):
                    qk_high(0, n)
                for kt in range(2):
                    v_evict(0, kt)
                attention_modulate(1, (0, 1, 2), 1, None)
                high_weights("w_out", 0)

            def half_step(l, b):
                it = l * B + b
                before, after, after_next = neighbours(l, b)
                negate_maxima(it)
                for n in range(3):
                    if after:
                        qk_high(it + 1, n)
                    if n < 2:
                        exponentials(it, n)
                    if n == 1 and at(b, 1):
                        high_weights("w_up", l, (0, 1))
                for u in range(2, 5):
                    exponentials(it, u)
                    if at(b, 1):
                        high_weights("w_up", l, (u,))
                if before:
                    act.wait_ge(s_hlo_a, it + 2 if after else it + 1)
                    modulate(it - 1, 1, (0, 1))
                exponentials(it, 5)
                if at(b, 1):
                    high_weights("w_up", l, (5,))
                copy_o(it, 0)
                exponentials(it, 6)
                if before:
                    modulate(it - 1, 1, (2,))
                exponentials(it, 7)
                copy_o(it, 1)
                if after:
                    v_evict(it + 1, 0)
                    v_evict(it + 1, 1)
                if at(b, 1):
                    act.wait_ge(s_down, 2 * it - 2 + PRE)
                    high_weights("w_down", l)
                if before:
                    for n in range(UP_USES):
                        gelu(it - 1, n)
                if after_next:
                    attention_modulate(it + 2, (0, 1, 2), None if before else it + 2, it if before else None)
                if at(b, B - 2) and after_next:
                    high_weights("w_in", l + 1)
                if at(b, 0) and before:
                    act.wait_ge(s_proj, 2 * it + PRE)
                    high_weights("w_out", l)

            def epilogue():
                it = L * B - 1
                modulate(it, 1, (0, 1, 2))
                for n in range(UP_USES):
                    gelu(it, n)

            whole_run(act, prologue, half_step, epilogue)

        @block.tensor
        def _(pe):
            mm = nc.tensor.matmul
            pe.sem_inc(s_st, PRE)
            pe.sem_inc(s_down, PRE)
            pe.sem_inc(s_pv, PRE_PV)
            for sm in (s_v_ps, s_up, s_max_ps, s_proj):
                pe.sem_inc(sm, PRE)
            pe.sem_inc(s_tr_m, PRE)
            pe.wait_ge(s_sel, 16)
            pe.wait_ge(s_init, 6)

            def split(out, high, low_part, weights, steps, start=True, stop=True):
                n, total = 0, 3 * len(steps)
                for s in steps:
                    a, c = s
                    for left, w in ((high, 0), (high, 1), (low_part, 0)):
                        last = mm(out, a(left), c(weights[w]), start=start and n == 0, stop=stop and n == total - 1)
                        n += 1
                return last

            def rows(c):
                return KC + (c == NCH - 1)

            def transposes(it, bank, chunks, done):
                for c in chunks:
                    for t in range(2):
                        last = nc.tensor.transpose(bank[0:KC, (c % 2) * T + t * P:(c % 2) * T + (t + 1) * P],
                                                   x_hat[:, t, c * KC:(c + 1) * KC], ident[:, :])
                last.then_inc(done, 1)

            def attention_transposes(it, use, v_before=True):
                if use == 0:
                    pe.wait_ge(s_xhat_a, 2 * it + 2)
                    if v_before:
                        pe.wait_ge(s_v, 2 * it + PRE)
                    transposes(it, att_ps, (0, 1), s_tr_a)
                else:
                    pe.wait_ge(s_h_a, NCH * it + 2)
                    transposes(it, att_ps, (2,), s_tr_a)

            def mlp_transposes(it, use, qk_between):
                if use == 0:
                    pe.wait_ge(s_xhat_m, 2 * it + 2)
                    if qk_between:
                        pe.wait_ge(s_qk_lo, QK_USES * (it + 2) + 2)
                    else:
                        pe.wait_ge(s_proj_gated, 2 * it + 2 + PRE)
                    transposes(it, mlp_ps, (0, 1), s_tr_m)
                else:
                    pe.wait_ge(s_h_m, NCH * it + 2)
                    transposes(it, mlp_ps, (2,), s_tr_m)

            def qk_tiles(it, n, m_between=True):
                if n == 0:
                    pe.wait_ge(s_hlo_a, it + 1)
                    pe.wait_ge(s_neg, it + PRE)
                    pe.wait_ge(s_h_a, NCH * it + NCH)
                elif n == 1:
                    if m_between:
                        pe.wait_ge(s_proj_gated, 2 * it - 3 + PRE)
                    else:
                        pe.wait_ge(s_qk_lo, QK_USES * it) if not at(it, 0) else None
                else:
                    pe.wait_ge(s_qk_lo, QK_USES * it + 1)
                for m in range(2 * n, min(2 * n + 2, QK_TILES)):
                    cols = slice(m * QK_ROWS, min((m + 1) * QK_ROWS, 2 * C))
                    count = 0
                    for c in range(NCH):
                        for w, h in ((0, 0), (0, 1), (1, 0)):
                            last = mm(qk_bank[n][0:cols.stop - cols.start, (m % 2) * T:(m % 2 + 1) * T],
                                      w_in[w][0:rows(c), c, cols], h_att[h][0:rows(c), c, :],
                                      start=count == 0, stop=count == 8)
                            count += 1
                last.then_inc(s_qk_ps, 1)

            def values(it, kt):
                if kt == 0:
                    pe.wait_ge(s_qk_lo, QK_USES * it + QK_USES)
                else:
                    pe.wait_ge(s_v, 2 * it + 1 + PRE)
                split(att_ps[:, 0:C], h_att[0], h_att[1], w_in,
                      [(lambda h, c=c: h[0:rows(c), c, kt * P:(kt + 1) * P],
                        lambda w, c=c: w[0:rows(c), c, 2 * C:3 * C]) for c in range(NCH)]).then_inc(s_v_ps, 1)

            def score_unit(it, u):
                if u == 0:
                    pe.wait_ge(s_stack, 192 * it + 192 + 16)
                if u < 2:
                    pe.wait_ge(s_exp, 8 * it - 1 + u + PRE_EXP)
                else:
                    pe.wait_ge(s_max, 8 * it + u - 1)
                for par in range(2):
                    r = slice(R * par, R * par + 3 * HD)
                    for qt in range(2):
                        last = mm(scores[u % 2][:, par, qt, :], q_stack[r, u, qt * P:(qt + 1) * P],
                                  k_stack[r, u, :], start=True, stop=True)
                last.then_inc(s_score, 1)

            def maxima_transposes(it, after):
                pe.wait_ge(s_max, 8 * it + 8)
                pe.wait_ge(s_h_a, NCH * (it + 2 if after else it + 1))
                pe.wait_ge(s_v, 2 * it + 2 + PRE)
                for qt in range(2):
                    last = nc.tensor.transpose(att_ps[0:H, qt * P:(qt + 1) * P],
                                               maxima[:, qt, :, :].rearrange("p a b -> p (a b)"), ident[:, :])
                last.then_inc(s_max_ps, 1)

            def shifted_unit(it, u):
                if u == 0:
                    pe.wait_ge(s_neg_st, 32 * it + 32 + 16)
                if u >= 2:
                    pe.wait_ge(s_exp, 8 * it + u - 1 + PRE_EXP)
                for par in range(2):
                    r = slice(R * par, R * par + 3 * HD + 1)
                    for kt in range(2):
                        last = mm(scores[u % 2][:, par, kt, :], k_stack[r, u, kt * P:(kt + 1) * P],
                                  q_stack[r, u, :], start=True, stop=True)
                last.then_inc(s_st, 1)

            def weighted_values(it, g):
                pe.wait_ge(s_exp, 8 * it + 2 * g + 2 + PRE_EXP)
                if g == 0:
                    pe.wait_ge(s_v, 2 * it + 2 + PRE)
                if g < 2:
                    pe.wait_ge(s_inv, 2 * it + PRE)
                else:
                    pe.wait_ge(s_o_full, 2 * it + 1 + PRE)
                for kt in range(2):
                    for i in range(4):
                        u = 2 * g + i // 2
                        last = mm(pv_ps[32 * i:32 * i + 32, (g % 2) * T:(g % 2 + 1) * T], v_sb[:, kt, 4 * g + i, :],
                                  probs[:, u % 3, i % 2, kt, :], start=kt == 0, stop=kt == 1, tile_position=(0, 32 * i))
                last.then_inc(s_pv, 1)

            def spread_sums(it, half):
                pe.wait_ge(s_o_full, 2 * it + half + 1 + PRE)
                if half == 0:
                    pe.wait_ge(s_proj_gated, 2 * it + PRE)
                mm(spread_bank[half][:, :], sel[:, :], o_full[:, half, :], start=True, stop=True).then_inc(s_sum, 1)

            def projection(it, t):
                if t == 0:
                    pe.wait_ge(s_o_lo, 2 * it + 2 + PRE)
                pe.wait_ge(s_down_gated, 2 * it - 1 + t + PRE2)
                split(token_bank[t][:, 0:C], o_att[0], o_att[1], w_out,
                      [(lambda o, g=g: o[:, g // 2, (g % 2) * T + t * P:(g % 2) * T + (t + 1) * P],
                        lambda w, g=g: w[:, g, :]) for g in range(NG)]).then_inc(s_proj, 1)

            def up(it, n):
                if n == 0:
                    pe.wait_ge(s_hlo_m, it + 1 + PRE)
                    pe.wait_ge(s_h_m, NCH * it + NCH)
                elif n == 1:
                    pe.wait_ge(s_inv, 2 * it + 3 + PRE) if not at(it, L * B - 1) else None
                else:
                    pe.wait_ge(s_gelu, 2 * (UP_USES * it + n - 1))
                for m in range(2 * n, min(2 * n + 2, NF)):
                    count = 0
                    for c in range(NCH):
                        for w, h in ((0, 0), (0, 1), (1, 0)):
                            last = mm(up_bank[n % 2][:, (m % 2) * T:(m % 2 + 1) * T],
                                      w_up[w][0:rows(c), c, m * P:(m + 1) * P],
                                      h_mlp[h][0:rows(c), c, :], start=count == 0, stop=count == 8)
                            count += 1
                last.then_inc(s_up, 1)

            def down(it, t, part):
                tiles = range(0, 6) if part == 0 else range(6, NF)
                if part == 0:
                    pe.wait_ge(s_gelu, 2 * (UP_USES * it + UP_USES))
                    pe.wait_ge(s_g_lo, UP_USES * it + 3 + G_PRE)
                    for w in range(2):
                        mm(token_bank[t][:, 0:C], one_row[:, :], b_down[w][:, :], start=w == 0, stop=False)
                else:
                    pe.wait_ge(s_g_lo, UP_USES * it + UP_USES + G_PRE)
                last = split(token_bank[t][:, 0:C], hidden[0], hidden[1], w_down,
                             [(lambda h, m=m: h[:, m, t * P:(t + 1) * P], lambda w, m=m: w[:, m, :]) for m in tiles],
                             start=False, stop=part == 1)
                if part == 1:
                    last.then_inc(s_down, 1)

            def weights_ready(name, l):
                pe.wait_ge(s_w_low, NP * l + OF[name].stop)

            def prologue():
                weights_ready("w_in", 0)
                attention_transposes(0, 0, v_before=False)
                attention_transposes(0, 1)
                for n in range(QK_USES):
                    qk_tiles(0, n, m_between=False)
                values(0, 0)
                values(0, 1)
                attention_transposes(1, 0)
                attention_transposes(1, 1)
                for u in range(8):
                    score_unit(0, u)

            def half_step(l, b):
                it = l * B + b
                before, after, after_next = neighbours(l, b)
                if before:
                    if at(b, 1):
                        weights_ready("w_out", l)
                    projection(it - 1, 0)
                maxima_transposes(it, after)
                if before:
                    projection(it - 1, 1)
                if after and at(b, B - 1):
                    weights_ready("w_in", l + 1)
                for n in range(3):
                    if after:
                        qk_tiles(it + 1, n, m_between=before)
                    shifted_unit(it, n)
                shifted_unit(it, 3)
                weighted_values(it, 0)
                shifted_unit(it, 4)
                shifted_unit(it, 5)
                weighted_values(it, 1)
                if before:
                    mlp_transposes(it - 1, 0, after)
                shifted_unit(it, 6)
                if after:
                    values(it + 1, 0)
                shifted_unit(it, 7)
                if before:
                    mlp_transposes(it - 1, 1, after)
                weighted_values(it, 2)
                spread_sums(it, 0)
                weighted_values(it, 3)
                m = it - 1
                if before:
                    if at(b, 1):
                        weights_ready("w_up", l)
                    up(m, 0)
                spread_sums(it, 1)
                if after:
                    values(it + 1, 1)
                work = []
                if before:
                    work = [lambda: None, lambda: up(m, 1), lambda: up(m, 2), lambda: up(m, 3), lambda: up(m, 4)]
                for n, w in enumerate(work):
                    w()
                    if n >= 1 and after:
                        score_unit(it + 1, n - 1)
                if after and not before:
                    for u in range(4):
                        score_unit(it + 1, u)
                if before and at(b, 1):
                    weights_ready("w_down", l)
                if after_next:
                    attention_transposes(it + 2, 0)
                if after:
                    score_unit(it + 1, 4)
                if before:
                    down(m, 0, 0)
                if after:
                    score_unit(it + 1, 5)
                if after_next:
                    attention_transposes(it + 2, 1)
                if before:
                    down(m, 0, 1)
                if after:
                    score_unit(it + 1, 6)
                if before:
                    down(m, 1, 0)
                if after:
                    score_unit(it + 1, 7)
                if before:
                    down(m, 1, 1)

            def epilogue():
                it = L * B - 1
                projection(it, 0)
                projection(it, 1)
                mlp_transposes(it, 0, False)
                mlp_transposes(it, 1, False)
                for n in range(UP_USES):
                    up(it, n)
                for t in range(2):
                    down(it, t, 0)
                    down(it, t, 1)

            whole_run(pe, prologue, half_step, epilogue)

        @block.vector
        def _(dve):
            tt = nc.vector.tensor_tensor
            nc.vector.memset(one_row[:, :].bitcast(F32), 1.0).then_inc(s_init, 1)
            nc.vector.memset(h_att[0][:, :, :].bitcast(F32), 1.0).then_inc(s_init, 1)
            nc.vector.memset(h_att[1][:, :, :].bitcast(F32), 0.0).then_inc(s_init, 1)
            nc.vector.memset(h_mlp[0][:, :, :].bitcast(F32), 1.0).then_inc(s_init, 1)
            nc.vector.memset(h_mlp[1][:, :, :].bitcast(F32), 0.0).then_inc(s_init, 1)
            nc.vector.memset(v_sb[:, :, :, :], 1.0).then_inc(s_init, 1)
            nc.vector.memset(k_stack[:, :, :].bitcast(F32), 1.0).then_inc(s_kinit, 1)
            for sm in (s_proj_gated, s_inv):
                dve.sem_inc(sm, PRE)
            dve.sem_inc(s_down_gated, PRE2)

            def norm(order, it, x_tile, ready, done):
                for t in range(2):
                    if ready:
                        ready(t)
                    nc.vector.bn_stats(out=stats[:, t, :], in_=x_tile[:, t, :]).then_inc(s_stats[order], 1)
                for t in range(2):
                    dve.wait_ge(s_stats[order], 2 * it + t + 1)
                    dve.sem_inc(s_tick[2], 1)
                    nc.vector.bn_aggr(out=mean_var[:, t, :], in_=stats[:, t, :]).then_inc(s_var[order], 1)

            def x_hats(order, it, x_tile, done):
                dve.wait_ge(s_var[order], 2 * it + 2)
                dve.wait_ge(s_rstd[order], it + 1)
                for t in range(2):
                    nc.vector.tensor_scalar(x_hat[:, t, :], x_tile[:, t, :], mean_var[:, t, 0:1], rstd[:, 1, t:t + 1],
                                            ALU.subtract, ALU.mult).then_inc(done, 1)

            def attention_norm(it):
                def ready(t):
                    if t == 0:
                        dve.wait_ge(s_xin, 16 * it + 16)
                norm(0, it, x_in, ready, s_xhat_a)

            def attention_high(it):
                dve.wait_ge(s_h_a, NCH * it + NCH)
                dve.wait_ge(s_v_ps, 2 * it + PRE)
                nc.vector.tensor_copy(h_att[0][0:KC, :, :], h_full[:, :, :]).then_inc(s_hhi_a, 1)

            def qk_low(it, n):
                dve.wait_ge(s_qk_hi, QK_USES * it + n + 1)
                tiles = slice(2 * n, min(2 * n + 2, QK_TILES))
                rows = QK_ROWS if tiles.stop < QK_TILES else 2 * C - QK_ROWS * (QK_TILES - 1)
                width = (tiles.stop - tiles.start) * T
                tt(qk[1][0:rows, tiles, :].rearrange("p a t -> p (a t)"), qk_bank[n][0:rows, 0:width],
                   qk[0][0:rows, tiles, :].rearrange("p a t -> p (a t)").bitcast(F32), ALU.subtract)\
                    .then_inc(s_qk_lo, 1)

            def unit_max(it, u):
                dve.wait_ge(s_score, 8 * it + u + 1)
                if u == 0:
                    dve.wait_ge(s_max_ps, it + PRE)
                nc.vector.tensor_reduce(out=maxima[:, :, :, u].rearrange("p q r -> p r q"), in_=scores[u % 2][:, :, :, :],
                                        axis=AX.X, op=ALU.max).then_inc(s_max, 1)

            def inverse_sums(it, half):
                dve.wait_ge(s_sum, 2 * it + half + 1)
                nc.vector.reciprocal(inv_sum[:, half, :], spread_bank[half][:, :]).then_inc(s_inv, 1)

            def normalise(it, half):
                dve.wait_ge(s_inv, 2 * it + half + 1 + PRE)
                tt(o_full[:, half, :], o_full[:, half, :], inv_sum[:, half, :], ALU.mult).then_inc(s_o, 1)
                dve.wait_ge(s_o, 2 * it + half + 1)
                dve.wait_ge(s_proj, 2 * it + PRE)
                nc.vector.tensor_copy(o_att[0][:, half, :], o_full[:, half, :]).then_inc(s_o_hi, 1)

            def gate_projection(it):
                dve.wait_ge(s_gate_a, 16 * it + 16)
                for t in range(2):
                    dve.wait_ge(s_proj, 2 * it + t + 1 + PRE)
                    dve.wait_ge(s_x_out, 2 * it - 1 + t + PRE2)
                    tt(gated[:, t, :], token_bank[t][:, 0:C], gate_a[:, :], ALU.mult).then_inc(s_proj_gated, 1)

            def mlp_norm(it):
                norm(1, it, x_one, lambda t: dve.wait_ge(s_x_one, 2 * it + t + 1 + PRE), s_xhat_m)

            def mlp_high(it):
                dve.wait_ge(s_h_m, NCH * it + NCH)
                dve.wait_ge(s_up, UP_USES * it + PRE)
                nc.vector.tensor_copy(h_mlp[0][0:KC, :, :], h_full[:, :, :]).then_inc(s_hhi_m, 1)

            def gate_down(it, t):
                if t == 0:
                    dve.wait_ge(s_gate_f, 16 * it + 16)
                dve.wait_ge(s_down, 2 * it + t + 1 + PRE)
                tt(gated[:, t, :], token_bank[t][:, 0:C], gate_f[:, :], ALU.mult).then_inc(s_down_gated, 1)

            def prologue():
                attention_norm(0)
                x_hats(0, 0, x_in, s_xhat_a)
                attention_high(0)
                for n in range(QK_USES):
                    qk_low(0, n)
                attention_norm(1)
                dve.wait_ge(s_tr_a, TRS)
                x_hats(0, 1, x_in, s_xhat_a)
                attention_high(1)
                for u in range(8):
                    unit_max(0, u)

            def half_step(l, b):
                it = l * B + b
                before, after, after_next = neighbours(l, b)
                if before:
                    gate_projection(it - 1)
                    mlp_norm(it - 1)
                if after:
                    qk_low(it + 1, 0)
                if before:
                    dve.wait_ge(s_tr_a, TRS * (it + 2 if after else it + 1))
                    x_hats(1, it - 1, x_one, s_xhat_m)
                if after:
                    qk_low(it + 1, 1)
                    qk_low(it + 1, 2)
                if after_next:
                    attention_norm(it + 2)
                if before:
                    mlp_high(it - 1)
                if after_next:
                    dve.wait_ge(s_tr_a, TRS * (it + 2))
                    dve.wait_ge(s_tr_m, TRS * it + PRE)
                    x_hats(0, it + 2, x_in, s_xhat_a)
                inverse_sums(it, 0)
                inverse_sums(it, 1)
                normalise(it, 0)
                normalise(it, 1)
                for u in range(8):
                    if u == 7 and after_next:
                        attention_high(it + 2)
                    if u == 7 and before:
                        gate_down(it - 1, 0)
                    if after:
                        unit_max(it + 1, u)
                if before:
                    gate_down(it - 1, 1)

            def epilogue():
                it = L * B - 1
                gate_projection(it)
                mlp_norm(it)
                dve.wait_ge(s_tr_a, TRS * (it + 1))
                x_hats(1, it, x_one, s_xhat_m)
                mlp_high(it)
                gate_down(it, 0)
                gate_down(it, 1)

            whole_run(dve, prologue, half_step, epilogue)


def _in_chunks(np, weight, bias):
    n = weight.shape[1]
    out = np.zeros((KC + 1, NCH, n), weight.dtype)
    out[0:KC] = weight.reshape(NCH, KC, n).transpose(1, 0, 2)
    out[KC, NCH - 1] = bias
    return out


def _by_head(np, weight, bias):
    out = np.zeros((P, NG, C), weight.dtype)
    for g in range(NG):
        for i in range(4):
            out[32 * i:32 * i + HD, g] = weight[(4 * g + i) * HD:(4 * g + i + 1) * HD]
    out[HD, 0] = bias
    return out


_LAYERS = [
    dict(qkv=("L1_cond_W_qkv", "L1_cond_b_qkv"), out=("L1_cond_W_proj", "L1_cond_b_proj"),
         up=("L1_cond_W_fc1", "L1_cond_b_fc1"), down=("L1_cond_W_fc2", "L1_cond_b_fc2"),
         ada=("L1_cond_W_ada", "L1_cond_b_ada")),
    dict(qkv=("L2_cond_qkv_w", "L2_cond_qkv_b"), out=("L2_cond_out_w", "L2_cond_out_b"),
         up=("L2_cond_w1", "L2_cond_b1"), down=("L2_cond_w2", "L2_cond_b2"),
         ada=("L2_cond_ada_w", "L2_cond_ada_b")),
    dict(qkv=("L3_cond_w_qkv", "L3_cond_b_qkv"), out=("L3_cond_w_proj", "L3_cond_b_proj"),
         up=("L3_cond_w_fc1", "L3_cond_b_fc1"), down=("L3_cond_w_fc2", "L3_cond_b_fc2"),
         ada=("L3_cond_w_ada", "L3_cond_b_ada")),
]


def _layout(np, inputs):
    a = {k: np.asarray(v) for k, v in inputs.items()}
    f = np.float32
    upper = np.triu_indices(R, k=1)
    index = np.zeros((R, R), np.int64)
    index[upper] = np.arange(len(upper[0]))
    index = index + index.T
    signs = (np.triu(np.ones((R, R)), 1) - np.tril(np.ones((R, R)), -1)) * 2.0 ** -SQUARINGS
    selector = np.zeros((P, P), f)
    for i in range(4):
        selector[32 * i + HD, 32 * i:32 * i + 32] = 1.0
    pick = lambda key, lay: np.stack([lay(np, a[w[key][0]], a[w[key][1]]) for w in _LAYERS])
    return {
        "x": a["x"].reshape(B, 2, P, C).transpose(0, 2, 1, 3),
        "cond_t": a["cond_1152"].T.reshape(NCH, KC, B).transpose(1, 0, 2),
        "p_t": a["L0_cond_P"].T,
        "p_nat": a["L0_cond_P"].reshape(NCH, KC, R).transpose(1, 0, 2),
        "w_rot": _in_chunks(np, a["L0_cond_W"].T[:, index.reshape(-1)], a["L0_cond_b"][index.reshape(-1)]),
        "w_ada": pick("ada", _in_chunks),
        "w_in": pick("qkv", _in_chunks),
        "w_out": pick("out", _by_head),
        "w_up": pick("up", _in_chunks),
        "w_down": np.stack([a[w["down"][0]].reshape(NF, P, C).transpose(1, 0, 2) for w in _LAYERS]),
        "b_down": np.stack([a[w["down"][1]] for w in _LAYERS]),
        "ident": np.eye(P, dtype=f),
        "lower": np.stack([np.tril(np.ones((R, R), f), -1), -np.tril(np.ones((R, R), f), -1)], axis=1),
        "skew_mask": np.concatenate([signs, signs]).astype(f),
        "sel": selector,
    }


def build(nc, dram):
    dram["v_scratch"] = nc.dram_tensor("v_scratch", (B, R * R), F32, kind="Internal").ap()
    dram["gate_scratch"] = nc.dram_tensor("gate_scratch", (L, B, 2 * C), F32, kind="Internal").ap()
    dram["qk_scratch"] = nc.dram_tensor("qk_scratch", (2, 2, H // 2, 2, HD, T), F32, kind="Internal").ap()
    with ExitStack() as ctx:
        def sb(name, shape):
            return ctx.enter_context(nc.sbuf_tensor(name, shape, F32))

        keep = {"ident": sb("ident", [P, P]), "mods": sb("mods", [KC, 12, L * B])}
        with ExitStack() as inner:
            for name, shape in (("u_twice", [KC, NCH, P]), ("g_rot", [P, NPAIR, C])):
                keep[name] = inner.enter_context(nc.sbuf_tensor(name, shape, F32))
            rotation_setup(nc, dram, keep)
            apply_rotation(nc, dram, keep)
        layers(nc, dram, keep)


def kernel(**inputs):
    import numpy as _np
    import concourse.bacc as _bacc
    from concourse import mybir as _mybir
    from concourse.bass_utils import run_bass_kernel_spmd as _run

    nc = _bacc.Bacc("TRN2", target_bir_lowering=False, num_devices=1)
    arrays, dram = {}, {}
    for name, a in _layout(_np, inputs).items():
        arrays[f"in_{name}"] = _np.ascontiguousarray(a)
        dram[name] = nc.dram_tensor(f"in_{name}", a.shape, _mybir.dt.from_np(a.dtype), kind="ExternalInput").ap()
    dram["out"] = nc.dram_tensor("out_x", (B, P, 2, C), F32, kind="ExternalOutput").ap()
    build(nc, dram)
    r = _run(nc, [arrays], core_ids=[0])
    got = _np.asarray(r.results[0]["out_x"])
    return got.transpose(0, 2, 1, 3).reshape(B, T, C)
```

```python
from contextlib import ExitStack

import concourse.bass as bass
from concourse import mybir

F32 = mybir.dt.float32
F32R = mybir.dt.float32r
ALU = mybir.AluOpType
ACT = mybir.ActivationFunctionType
AX = mybir.AxisListType

P = 128
B, T, C = 16, 256, 288
R = 64
L = 3
H = 16
HD = C // H
KC, NCH = 96, 3
FF = 4 * C
NPAIR = B // 2
SQUARINGS = 8
EPS = 1e-6
MOD_KINDS = (0, 3, 1, 4)
STACK = KC + 2
STACK_LOW = slice(R, KC + 1)
MOD_WIDTH = 2 * P + KC
GATE_START = 4 * MOD_WIDTH
ADA = GATE_START + 2 * C
NG = H // 4
NF = FF // P
QK_ROWS, QK_TILES = 7 * HD, 5
QK_USES, UP_USES = 3, 5
SCALE = float(HD) ** -0.5


def rotation_setup(nc, dram, keep):
    mods, u_twice, g_rot = keep["mods"], keep["u_twice"], keep["g_rot"]
    ident = keep["ident"]
    with ExitStack() as ctx:
        def sb(name, shape, dt=F32):
            return ctx.enter_context(nc.sbuf_tensor(name, shape, dt))

        def sem(name):
            return ctx.enter_context(nc.semaphore(name))

        cond = sb("cond", [KC, NCH, B])
        silu_c = sb("silu_c", [KC + 1, NCH, B])
        w_ada = sb("w_ada", [KC + 1, L, NCH, ADA])
        gates = sb("gates", [B, L, 2 * C])
        w_rot = sb("w_rot", [KC + 1, NCH, R * R])
        v_rot = sb("v_rot", [B, R * R])
        a_raw = sb("a_rows", [P, NPAIR, R])
        skew_mask = sb("skew_mask", [P, R])
        a_pos = sb("a_pos", [P, NPAIR, P])
        a_neg = sb("a_neg", [P, NPAIR, P])
        a_sq = sb("a_sq", [P, NPAIR, P])
        a_4 = sb("a_4", [P, NPAIR, P])
        even = sb("even", [P, NPAIR, P])
        inner_odd = sb("inner_odd", [P, NPAIR, P])
        outer_odd = sb("outer_odd", [P, NPAIR, P])
        e_mat = sb("e_mat", [P, NPAIR, P])
        f_mat = sb("f_mat", [P, NPAIR, P])
        p_t = sb("p_t", [R, C])
        p_nat = sb("p_nat", [KC, NCH, R])
        ones = sb("ones", [R, P])
        lower = sb("lower", [R, 2, R])
        pivot = sb("pivot", [R, 2, P])
        top = sb("top", [R, R])
        gram = sb("gram", [R, 2 * R])
        col = sb("col", [R, 2, 8])
        root = sb("root", [R, 2, 2])
        beta_all = sb("beta_all", [R, R])
        beta_diag = sb("beta_diag", [R, R])
        beta_col = sb("beta_col", [R, 2])
        c_mat = sb("c_mat", [R, R])
        c_t = sb("c_t", [R, 2, R])
        u_t = sb("u_t", [P, C])
        qr_ps = ctx.enter_context(nc.psum_tensor("qr_ps", [P, 2, 512], F32))
        ps_a = ctx.enter_context(nc.psum_tensor("ps_a", [P, 2, 512], F32))
        ps_b = ctx.enter_context(nc.psum_tensor("ps_b", [P, 2, 512], F32))
        ada_ps = ctx.enter_context(nc.psum_tensor("ada_ps", [P, 2, 512], F32))

        s_cond = sem("s_cond")
        s_const = sem("s_const")
        s_p = sem("s_p")
        s_wada = [sem(f"s_wada{l}") for l in range(L)]
        s_wrot = [sem(f"s_wrot{n}") for n in range(4)]
        s_ones = sem("s_ones")
        s_silu = sem("s_silu")
        s_ada_ps = sem("s_ada_ps")
        s_ada_out = sem("s_ada_out")
        s_gates = sem("s_gates")
        s_gates_st = sem("s_gates_st")
        s_rot_ps = sem("s_rot_ps")
        s_rot_out = sem("s_rot_out")
        s_v_st = sem("s_v_st")
        s_a_ld = sem("s_a_ld")
        s_chain = sem("s_chain")
        s_exp_ps = sem("s_exp_ps")
        s_exp_sb = sem("s_exp_sb")
        s_sq_ps = sem("s_sq_ps")
        s_sq = sem("s_sq")
        s_g0 = sem("s_g0")
        s_qr_init = sem("s_qr_init")
        s_pivot = sem("s_pivot")
        s_row_g = sem("s_row_g")
        s_row_t = sem("s_row_t")
        s_pivot_g = sem("s_pivot_g")
        s_root = sem("s_root")
        s_gram = sem("s_gram")
        s_top = sem("s_top")
        s_beta = sem("s_beta")
        s_u_ps = sem("s_u_ps")
        s_u_sb = sem("s_u_sb")
        s_gr_ps = sem("s_gr_ps")
        s_gr_sb = sem("s_gr_sb")
        block = ctx.enter_context(nc.Block())
        EARLY, PER_ROUND = R - 6 * SQUARINGS, 6
        SQUARED = ((0,), (1, 2), (3,), (4,), (5, 6), (7,))

        def elimination(engine, step, square=None, skew=None):
            with engine.Fori(0, EARLY // 4) as r:
                for k in range(2):
                    step(2 * r + k, k, None, (), False)
            yield
            with engine.Fori(0, EARLY // 4) as r:
                for k in range(2):
                    step(2 * r + (EARLY // 2 + k), k, None, (), False)
                    if skew:
                        skew(2 * r + k, k)
            yield

            def squaring_round(r, final):
                for k in range(PER_ROUND):
                    step(r * PER_ROUND + (EARLY + k), k % 2, (lambda n: square(r, n)) if square else None, SQUARED[k],
                         final and k == PER_ROUND - 1)

            with engine.Fori(0, SQUARINGS - 1) as r:
                squaring_round(r, False)
            squaring_round(SQUARINGS - 1, True)
            yield

        @block.sync
        def _(sp):
            sp.dma_start(p_t[:, :], dram["p_t"]).then_inc(s_p, 16)
            sp.dma_start(p_nat[:, :, :], dram["p_nat"]).then_inc(s_p, 16)
            sp.dma_start(ident[:, :], dram["ident"]).then_inc(s_const, 16)
            sp.dma_start(lower[:, :, :], dram["lower"]).then_inc(s_const, 16)
            sp.dma_start(skew_mask[:, :], dram["skew_mask"]).then_inc(s_const, 16)
            sp.dma_start(cond[:, :, :], dram["cond_t"]).then_inc(s_cond, 16)
            for n in range(4):
                part = slice(n * 1024, (n + 1) * 1024)
                sp.dma_start(w_rot[:, :, part], dram["w_rot"][:, :, part]).then_inc(s_wrot[n], 16)
            for l in range(L):
                sp.dma_start(w_ada[:, l, :, :], dram["w_ada"][l]).then_inc(s_wada[l], 16)
            sp.wait_ge(s_rot_out, 8 + 2)
            sp.dma_start(dram["v_scratch"], v_rot[:, :]).then_inc(s_v_st, 16)
            sp.wait_ge(s_v_st, 16)
            a_view = dram["v_scratch"].rearrange("(n two) (i j) -> two i n j", two=2, i=R)
            for half in range(2):
                sp.dma_start(a_raw[half * R:(half + 1) * R, :, :], a_view[half]).then_inc(s_a_ld, 16)
            sp.wait_ge(s_gates, 2 * L)
            sp.dma_start(dram["gate_scratch"].rearrange("l b c -> b l c"), gates[:, :, :]).then_inc(s_gates_st, 16)
            sp.wait_ge(s_gates_st, 16)

        @block.scalar
        def _(act):
            act.wait_ge(s_cond, 16)
            nc.scalar.activation(silu_c[0:KC, :, :], cond[:, :, :], ACT.Silu).then_inc(s_silu, 1)
            act.wait_ge(s_ones, 1)
            nc.scalar.activation(root[0:1, 0, 0:1], ones[0:1, 0:1], ACT.Sqrt).then_inc(s_root, 1)
            act.wait_ge(s_const, 48)
            for j in range(2):
                nc.scalar.activation(pivot[:, j, :], ones[:, :], ACT.Copy, scale=ident[0:R, j:j + 1])\
                    .then_inc(s_pivot, 1)

            def norms(j, parity):
                act.wait_ge(s_pivot_g, j + 1)
                for n, scale in enumerate((1.0, 4.0)):
                    nc.scalar.activation(root[:, parity, n:n + 1], col[:, parity, 0:1], ACT.Sqrt,
                                         scale=scale).then_inc(s_root, 1)

            def step(j, parity, square, pairs, last):
                if last:
                    return
                norms(j + 1, 1 - parity)
                act.wait_ge(s_row_t, j + 1)
                nc.scalar.activation(pivot[:, parity, :], ones[:, :], ACT.Copy,
                                     scale=ident[0:R, bass.ds(j + 2, 1)]).then_inc(s_pivot, 1)

            norms(0, 0)
            act.sem_inc(s_rot_out, 2)
            def skew(n, parity):
                act.wait_ge(s_rot_ps, n + 1)
                nc.scalar.activation(v_rot[:, bass.ds(n * 512, 512)], ps_b[0:B, parity, :],
                                     ACT.Copy).then_inc(s_rot_out, 1)

            for _ in elimination(act, step, skew=skew):
                pass

        @block.tensor
        def _(pe):
            mm = nc.tensor.matmul
            pe.wait_ge(s_p, 32)
            for c in range(NCH):
                last = mm(ps_a[0:R, 0, 0:R], p_nat[:, c, :], p_nat[:, c, :], start=c == 0, stop=c == NCH - 1)
            last.then_inc(s_g0, 1)
            pe.wait_ge(s_qr_init, 3)

            def gram_row(j, parity):
                pe.wait_ge(s_pivot, j + 1)
                pe.wait_ge(s_gram, 3 * j + 1)
                mm(qr_ps[:, 0, 0:2 * R], pivot[:, parity, :], gram[:, :], start=True, stop=True).then_inc(s_row_g, 1)

            def step(j, parity, square, pairs, last):
                pe.wait_ge(s_top, 7 * j + 1)
                mm(qr_ps[:, 1, 0:R], pivot[:, parity, :], top[:, :], start=True, stop=True).then_inc(s_row_t, 1)
                if not last:
                    gram_row(j + 1, 1 - parity)
                for n in pairs:
                    square(n)

            gram_row(0, 0)

            def square(r, n):
                pe.wait_ge(s_sq, 2 * NPAIR * r + 2 * n + 14)
                bank = ps_a[:, n % 2, :]
                mm(bank[:, 0:P], f_mat[:, n, :], e_mat[:, n, :], start=True, stop=True)
                mm(bank[:, P:2 * P], e_mat[:, n, :], f_mat[:, n, :], start=True, stop=True).then_inc(s_sq_ps, 1)

            def skew(n, parity):
                pe.wait_ge(s_rot_out, n + 1)
                for c in range(NCH):
                    k = KC + (c == NCH - 1)
                    last = mm(ps_b[0:B, parity, :], silu_c[0:k, c, :], w_rot[0:k, c, bass.ds(n * 512, 512)],
                              start=c == 0, stop=c == NCH - 1)
                last.then_inc(s_rot_ps, 1)

            steps = elimination(pe, step, square, skew)
            next(steps)
            pe.wait_ge(s_silu, 3)
            for sm in s_wrot:
                pe.wait_ge(sm, 16)
            next(steps)

            def modulation(l, outputs):
                if 0 in outputs:
                    pe.wait_ge(s_wada[l], 16)
                    if l:
                        pe.wait_ge(s_ada_out, 8 * l)
                        pe.wait_ge(s_gates, 2 * l)
                for n in outputs:
                    src, width = n // 3 * MOD_WIDTH + n % 3 * P, (P, P, KC)[n % 3]
                    for c in range(NCH):
                        k = KC + (c == NCH - 1)
                        mm(ada_ps[0:width, 0, n * B:(n + 1) * B], w_ada[0:k, l, c, src:src + width],
                           silu_c[0:k, c, :], start=c == 0, stop=c == NCH - 1)

            def gate_rows(l):
                for n in range(2):
                    src = GATE_START + n * C
                    for c in range(NCH):
                        k = KC + (c == NCH - 1)
                        last = mm(ada_ps[0:B, n, 192:192 + C], silu_c[0:k, c, :], w_ada[0:k, l, c, src:src + C],
                                  start=c == 0, stop=c == NCH - 1)
                last.then_inc(s_ada_ps, 1)

            modulation(0, range(12))
            gate_rows(0)

            def product(out, lhs, rhs):
                for n in range(NPAIR):
                    last = mm(out[:, n // 4, (n % 4) * P:(n % 4 + 1) * P], lhs[:, n, :], rhs[:, n, :],
                              start=True, stop=True)
                last.then_inc(s_exp_ps, 1)

            pe.wait_ge(s_exp_sb, 1)
            product(ps_a, a_neg, a_pos)
            modulation(1, range(0, 4))
            pe.wait_ge(s_exp_sb, 2)
            product(ps_b, a_sq, a_sq)
            modulation(1, range(4, 8))
            pe.wait_ge(s_exp_sb, 4)
            product(ps_a, a_4, inner_odd)
            pe.wait_ge(s_exp_sb, 5)
            product(ps_b, a_4, even)
            modulation(1, range(8, 12))
            pe.wait_ge(s_exp_sb, 6)
            product(ps_a, a_neg, outer_odd)
            gate_rows(1)
            modulation(2, range(12))
            gate_rows(2)
            next(steps)
            pe.wait_ge(s_u_sb, 1)
            nc.tensor.transpose(qr_ps[0:R, 0, 0:R], c_mat[:, :], ident[0:R, 0:R]).then_inc(s_u_ps, 1)
            pe.wait_ge(s_u_sb, 3)
            for c in range(NCH):
                last = mm(ps_a[0:KC, 0, c * R:(c + 1) * R], p_t[:, c * KC:(c + 1) * KC], c_t[:, 0, :],
                          start=True, stop=True)
            mm(ps_a[:, 1, 0:C], c_t[:, :, :], p_t[:, :], start=True, stop=True).then_inc(s_u_ps, 1)
            pe.wait_ge(s_u_sb, 6)
            for n in range(NPAIR):
                if n >= 2:
                    pe.wait_ge(s_gr_sb, n - 1)
                mm(ps_b[:, n % 2, 0:C], f_mat[:, n, :], u_t[:, :], start=True, stop=True)\
                    .then_inc(s_gr_ps, 1)

        @block.vector
        def _(dve):
            V = nc.vector
            V.memset(ones[:, :], 1.0).then_inc(s_ones, 1)
            V.memset(silu_c[KC:KC + 1, :, :], 1.0).then_inc(s_silu, 2)
            V.memset(a_pos[:, :, :], 0.0).then_inc(s_chain, 1)
            dve.wait_ge(s_p, 32)
            V.tensor_copy(top[:, :], p_t[:, 0:R]).then_inc(s_qr_init, 1)
            dve.wait_ge(s_const, 48)
            V.tensor_copy(gram[:, R:2 * R], ident[0:R, 0:R]).then_inc(s_qr_init, 1)
            dve.wait_ge(s_g0, 1)
            V.tensor_copy(gram[:, 0:R], ps_a[0:R, 0, 0:R]).then_inc(s_qr_init, 1)
            dve.sem_inc(s_gram, 1)
            dve.sem_inc(s_top, 1)
            dve.wait_ge(s_qr_init, 3)

            def gram_steps(j, parity):
                g = qr_ps[0:R, 0, :]
                c = [col[:, parity, n:n + 1] for n in range(3)]
                dve.wait_ge(s_row_g, j + 1)
                V.reciprocal(c[1], g[:, bass.ds(j, 1)]).then_inc(s_gram, 1)
                V.tensor_copy(c[0], g[:, bass.ds(j, 1)]).then_inc(s_pivot_g, 1)
                yield
                dve.wait_ge(s_gram, 3 * j + 2)
                V.tensor_scalar(c[2], gram[:, bass.ds(j, 1)], c[1], lower[:, 1, bass.ds(j, 1)],
                                ALU.mult, ALU.mult).then_inc(s_gram, 1)
                yield
                dve.wait_ge(s_gram, 3 * j + 3)
                V.scalar_tensor_tensor(out=gram[:, :], in0=g[:, 0:2 * R], scalar=c[2], in1=gram[:, :],
                                       op0=ALU.mult, op1=ALU.add).then_inc(s_gram, 1)
                yield

            def top_steps(j, parity):
                t = qr_ps[0:R, 1, :]
                c = [col[:, parity, n:n + 1] for n in range(8)]
                norm, twice = root[:, parity, 0:1], root[:, parity, 1:2]
                alpha, beta = t[:, bass.ds(j, 1)], beta_all[:, bass.ds(j, 1)]
                dve.wait_ge(s_row_t, j + 1)
                dve.wait_ge(s_root, 2 * j + 3)
                V.tensor_scalar(c[3], alpha, 0.0, twice, ALU.is_lt, ALU.mult).then_inc(s_top, 1)
                yield
                dve.wait_ge(s_top, 7 * j + 2)
                V.tensor_scalar(c[5], c[3], norm, alpha, ALU.subtract, ALU.subtract).then_inc(s_top, 1)
                V.tensor_scalar(beta, c[3], norm, None, ALU.subtract).then_inc(s_top, 1)
                yield
                dve.wait_ge(s_top, 7 * j + 3)
                V.reciprocal(c[6], c[5]).then_inc(s_top, 1)
                dve.wait_ge(s_top, 7 * j + 4)
                V.scalar_tensor_tensor(out=c[4], in0=c[2], scalar=beta, in1=top[:, bass.ds(j, 1)],
                                       op0=ALU.mult, op1=ALU.add).then_inc(s_top, 1)
                yield
                dve.wait_ge(s_top, 7 * j + 6)
                V.tensor_scalar(c[7], c[4], c[6], lower[:, 0, bass.ds(j, 1)], ALU.mult, ALU.mult).then_inc(s_top, 1)
                yield
                dve.wait_ge(s_top, 7 * j + 7)
                V.scalar_tensor_tensor(out=top[:, :], in0=t[:, 0:R], scalar=c[7], in1=top[:, :],
                                       op0=ALU.mult, op1=ALU.add).then_inc(s_top, 1)
                yield

            def step(j, parity, square, pairs, last):
                grams = iter(()) if last else gram_steps(j + 1, 1 - parity)
                tops = top_steps(j, parity)
                squares = (square(n) for n in pairs)
                for source in (tops, tops, grams, tops, grams, tops, tops, grams, squares, squares):
                    next(source, None)

            for _ in gram_steps(0, 0):
                pass

            def square(r, n):
                dve.wait_ge(s_sq_ps, NPAIR * r + n + 1)
                for m, part in ((e_mat, slice(0, P)), (f_mat, slice(P, 2 * P))):
                    V.scalar_tensor_tensor(out=m[:, n, :], in0=m[:, n, :], scalar=2.0, in1=ps_a[:, n % 2, part],
                                           op0=ALU.mult, op1=ALU.add).then_inc(s_sq, 1)

            steps = elimination(dve, step, square)
            next(steps)
            next(steps)

            def modulation_out(l):
                dve.wait_ge(s_ada_ps, l + 1)
                out = ada_ps[:, 0, 0:12 * B].rearrange("p (k c b) -> p k c b", c=3, b=B)
                here = slice(l * B, (l + 1) * B)
                for rows, c in ((slice(0, P), slice(0, 2)), (slice(0, KC), slice(2, 3))):
                    for k in range(2):
                        V.tensor_copy(mods[rows, k, c, here], out[rows, k, c, :]).then_inc(s_ada_out, 1)
                    for k in range(2, 4):
                        V.tensor_scalar(mods[rows, k, c, here], out[rows, k, c, :], 1.0, None,
                                        ALU.add).then_inc(s_ada_out, 1)
                for n in range(2):
                    V.tensor_copy(gates[:, l, n * C:(n + 1) * C], ada_ps[0:B, n, 192:192 + C]).then_inc(s_gates, 1)

            modulation_out(0)
            dve.wait_ge(s_a_ld, 32)
            dve.wait_ge(s_chain, 1)
            for half in range(2):
                h = slice(half * R, (half + 1) * R)
                V.tensor_tensor(a_pos[h, :, h], a_raw[h, :, :],
                                skew_mask[h, :].unsqueeze(1).to_broadcast([R, NPAIR, R]),
                                ALU.mult).then_inc(s_chain, 1)
            dve.wait_ge(s_chain, 3)
            V.tensor_scalar(a_neg[:, :, :], a_pos[:, :, :], -1.0, None, ALU.mult).then_inc(s_exp_sb, 1)
            unit = ident[:, :].unsqueeze(1).to_broadcast([P, NPAIR, P])

            def blocks(ps):
                return ps[:, :, :].rearrange("p h (n c) -> p (h n) c", c=P)

            def scaled_sum(out, in0, scalar, in1, op=ALU.add):
                return V.scalar_tensor_tensor(out=out[:, :, :], in0=in0, scalar=scalar, in1=in1, op0=ALU.mult, op1=op)

            dve.wait_ge(s_exp_ps, 1)
            V.tensor_copy(a_sq[:, :, :], blocks(ps_a)).then_inc(s_exp_sb, 1)
            dve.wait_ge(s_exp_sb, 2)
            scaled_sum(inner_odd, a_sq[:, :, :], 1 / 42, unit).then_inc(s_exp_sb, 1)
            scaled_sum(even, a_sq[:, :, :], 1 / 30, unit).then_inc(s_chain, 1)
            dve.wait_ge(s_exp_ps, 2)
            V.tensor_copy(a_4[:, :, :], blocks(ps_b)).then_inc(s_exp_sb, 1)
            dve.wait_ge(s_exp_sb, 4)
            dve.wait_ge(s_chain, 4)
            scaled_sum(even, a_4[:, :, :], 1 / 1680, even[:, :, :]).then_inc(s_exp_sb, 1)
            scaled_sum(outer_odd, a_sq[:, :, :], 1 / 6, unit).then_inc(s_chain, 1)
            dve.wait_ge(s_exp_ps, 3)
            dve.wait_ge(s_chain, 5)
            scaled_sum(outer_odd, blocks(ps_a), 1 / 120, outer_odd[:, :, :]).then_inc(s_exp_sb, 1)
            dve.wait_ge(s_exp_ps, 4)
            scaled_sum(even, blocks(ps_b), 1 / 12, a_sq[:, :, :]).then_inc(s_chain, 1)
            dve.wait_ge(s_exp_ps, 5)
            dve.wait_ge(s_chain, 6)
            scaled_sum(e_mat, even[:, :, :], 0.5, blocks(ps_a)).then_inc(s_chain, 1)
            scaled_sum(f_mat, even[:, :, :], 0.5, blocks(ps_a), ALU.subtract).then_inc(s_sq, 2 * NPAIR)
            modulation_out(1)
            modulation_out(2)
            dve.wait_ge(s_chain, 7)
            next(steps)
            dve.wait_ge(s_top, 7 * R + 1)
            V.tensor_tensor(beta_diag[:, :], beta_all[:, :], ident[0:R, 0:R], ALU.mult).then_inc(s_beta, 1)
            dve.wait_ge(s_beta, 1)
            V.tensor_reduce(out=beta_col[:, 0:1], in_=beta_diag[:, :], axis=AX.X, op=ALU.add).then_inc(s_beta, 1)
            dve.wait_ge(s_beta, 2)
            V.reciprocal(beta_col[:, 1:2], beta_col[:, 0:1]).then_inc(s_beta, 1)
            dve.wait_ge(s_beta, 3)
            dve.wait_ge(s_gram, 3 * R + 1)
            V.tensor_scalar(c_mat[:, :], gram[:, R:2 * R], beta_col[:, 1:2], None, ALU.mult).then_inc(s_u_sb, 1)
            dve.wait_ge(s_u_ps, 1)
            for n in range(2):
                V.tensor_copy(c_t[:, n, :], qr_ps[0:R, 0, 0:R]).then_inc(s_u_sb, 1)
            dve.wait_ge(s_u_ps, 2)
            u_ps = ps_a[0:KC, 0, 0:NCH * R].rearrange("p (c r) -> p c r", r=R)
            for n in range(2):
                V.tensor_copy(u_twice[:, :, n * R:(n + 1) * R], u_ps).then_inc(s_u_sb, 1)
            V.tensor_copy(u_t[:, :], ps_a[:, 1, 0:C]).then_inc(s_u_sb, 1)
            for n in range(NPAIR):
                dve.wait_ge(s_gr_ps, n + 1)
                V.tensor_copy(g_rot[:, n, :], ps_b[:, n % 2, 0:C]).then_inc(s_gr_sb, 1)


def apply_rotation(nc, dram, keep):
    ident, u_twice, g_rot = keep["ident"], keep["u_twice"], keep["g_rot"]
    with ExitStack() as ctx:
        def sb(name, shape, dt=F32):
            return ctx.enter_context(nc.sbuf_tensor(name, shape, dt))

        def sem(name):
            return ctx.enter_context(nc.semaphore(name))

        AHEAD = 4
        x_in = sb("r_x", [P, AHEAD, 2, C])
        x_t = sb("r_xt", [KC, 2, NCH, T])
        z_t = sb("r_zt", [P, 2, T])
        g_now = sb("r_g", [P, 2, C])
        x_out = sb("r_out", [P, 2, 2, C])
        xt_ps = [ctx.enter_context(nc.psum_tensor(f"xt_ps{i}", [P, 2, 512], F32)) for i in range(2)]
        z_ps = ctx.enter_context(nc.psum_tensor("z_ps", [P, 2, 512], F32))
        d_ps = ctx.enter_context(nc.psum_tensor("d_ps", [P, 2, 512], F32))
        s_x = [sem(f"r_x{n}") for n in range(AHEAD)]
        s_xt_ps = sem("r_xt_ps")
        s_xt = sem("r_xt")
        s_z_ps = sem("r_z_ps")
        s_z = sem("r_z")
        s_g = sem("r_g")
        s_d_ps = sem("r_d_ps")
        s_out = sem("r_out")
        s_st = [sem("r_st0"), sem("r_st1")]
        s_tick = sem("r_tick")
        block = ctx.enter_context(nc.Block())
        PRE_D, PRE_OUT, PRE_Z = 2, 2, 1

        def batches(engine, step):
            with engine.Fori(0, B // AHEAD - 1) as m:
                for k in range(AHEAD):
                    step(m, k)
            for k in range(AHEAD):
                step(B // AHEAD - 1, k)

        def follows(m, k, n):
            return not isinstance(m, int) or AHEAD * m + k + n < B

        @block.sync
        def _(sp):
            for k in range(AHEAD):
                sp.dma_start(x_in[:, k, :, :], dram["x"][k]).then_inc(s_x[k], 16)

            def step(m, k):
                sp.wait_ge(s_out, 2 * (AHEAD * m + k) + 2 + PRE_OUT)
                sp.sem_inc(s_tick, 1)
                sp.dma_start(dram["out"][AHEAD * m + k], x_out[:, k % 2, :, :]).then_inc(s_st[k % 2], 16)
                if follows(m, k, AHEAD):
                    sp.dma_start(x_in[:, k, :, :], dram["x"][AHEAD * m + (k + AHEAD)]).then_inc(s_x[k], 16)

            batches(sp, step)
            for h in range(2):
                sp.wait_ge(s_st[h], 16 * (B // 2) + 16)

        @block.scalar
        def _(act):
            def copy_xt(i, k):
                act.wait_ge(s_xt_ps, i + 1)
                bank = xt_ps[k % 2]
                nc.scalar.activation(x_t[:, k % 2, 0:2, :], bank[0:KC, 0, :].rearrange("p (c t) -> p c t", t=T),
                                     ACT.Copy).then_inc(s_xt, 1)
                nc.scalar.activation(x_t[:, k % 2, 2, :], bank[0:KC, 1, 0:T], ACT.Copy).then_inc(s_xt, 1)

            def copy_z(i, k):
                act.wait_ge(s_z_ps, i + 1)
                nc.scalar.activation(z_t[:, k % 2, :], z_ps[:, k % 2, 0:T], ACT.Copy).then_inc(s_z, 1)

            act.sem_inc(s_z, PRE_Z)
            copy_xt(0, 0)
            copy_xt(1, 1)
            copy_z(0, 0)

            def step(m, k):
                i = AHEAD * m + k
                if follows(m, k, 2):
                    act.wait_ge(s_z_ps, i + 1)
                    copy_xt(i + 2, k)
                if follows(m, k, 1):
                    act.wait_ge(s_d_ps, 2 * i + PRE_D)
                    copy_z(i + 1, k + 1)

            batches(act, step)

        @block.tensor
        def _(pe):
            pe.sem_inc(s_d_ps, PRE_D)

            def transposes(m, k, ahead):
                slot, turn = (k + ahead) % AHEAD, (k + ahead) // AHEAD
                pe.wait_ge(s_x[slot], 16 * (m + turn) + 16)
                for c in range(NCH):
                    for t in range(2):
                        last = nc.tensor.transpose(
                            xt_ps[slot % 2][0:KC, c // 2, (c % 2) * T + t * P:(c % 2) * T + (t + 1) * P],
                            x_in[:, slot, t, c * KC:(c + 1) * KC], ident[:, :])
                last.then_inc(s_xt_ps, 1)

            def into_subspace(i, k):
                pe.wait_ge(s_xt, 2 * i + 2)
                for c in range(NCH):
                    last = nc.tensor.matmul(z_ps[:, k % 2, 0:T], u_twice[:, c, :], x_t[:, k % 2, c, :],
                                            start=c == 0, stop=c == NCH - 1)
                last.then_inc(s_z_ps, 1)

            transposes(0, 0, 0)
            transposes(0, 1, 0)
            into_subspace(0, 0)

            def step(m, k):
                i = AHEAD * m + k
                if follows(m, k, 2):
                    pe.wait_ge(s_xt, 2 * i + 2)
                    transposes(m, k, 2)
                if follows(m, k, 1):
                    pe.wait_ge(s_z, i + PRE_Z)
                    into_subspace(i + 1, k + 1)
                pe.wait_ge(s_z, i + 1 + PRE_Z)
                pe.wait_ge(s_g, 2 * m + k // 2 + 1)
                h = k % 2
                for t in range(2):
                    pe.wait_ge(s_out, 2 * i - 1 + t + PRE_OUT)
                    nc.tensor.matmul(d_ps[:, t, 0:C], z_t[h * R:(h + 1) * R, h, t * P:(t + 1) * P],
                                     g_now[h * R:(h + 1) * R, k // 2, :], start=True, stop=True).then_inc(s_d_ps, 1)

            batches(pe, step)

        @block.vector
        def _(dve):
            for h in range(2):
                dve.sem_inc(s_st[h], 16)
            dve.sem_inc(s_out, PRE_OUT)
            nc.vector.tensor_copy(g_now[:, 0, :], g_rot[:, 0, :]).then_inc(s_g, 1)

            def step(m, k):
                i = AHEAD * m + k
                if k % 2 == 0 and follows(m, k, 2):
                    nc.vector.tensor_copy(g_now[:, (k // 2 + 1) % 2, :].unsqueeze(1),
                                          g_rot[:, bass.ds(2 * m + k // 2 + 1, 1), :]).then_inc(s_g, 1)
                for t in range(2):
                    dve.wait_ge(s_d_ps, 2 * i + t + 1 + PRE_D)
                    if t == 0:
                        dve.wait_ge(s_st[k % 2], 16 * (2 * m + k // 2) + 16)
                    nc.vector.tensor_tensor(x_out[:, k % 2, t, :], d_ps[:, t, 0:C], x_in[:, k, t, :],
                                            ALU.add).then_inc(s_out, 1)

            batches(dve, step)


def layers(nc, dram, keep):
    ident, mods = keep["ident"], keep["mods"]
    with ExitStack() as ctx:
        def sb(name, shape, dt=F32):
            return ctx.enter_context(nc.sbuf_tensor(name, shape, dt))

        def sem(name):
            return ctx.enter_context(nc.semaphore(name))

        SLOTS = 3
        w_in = [sb(f"w_in{i}", [P, 3 - i, 3 * C], F32R) for i in range(2)]
        w_out = [sb(f"w_out{i}", [P, NG, C], F32R) for i in range(2)]
        w_up = [sb(f"w_up{i}", [P, 3 - i, FF], F32R) for i in range(2)]
        w_down = [sb(f"w_down{i}", [P, NF, C], F32R) for i in range(2)]
        b_down = sb("b_down", [R // 2 + 1, C], F32R)
        staging = sb("staging", [P, SLOTS, 3 * C])
        ones = sb("ones_l", [R // 2 + 1, P], F32R)
        x_in = sb("x_in", [P, 2, C])
        x_mid = sb("x_mid", [P, 2, C])
        x_one = sb("x_one", [P, 2, C])
        x_out = sb("x_out", [P, 2, C])
        gated = sb("gated", [P, 2, C])
        gate_a = sb("gate_a", [P, C])
        gate_f = sb("gate_f", [P, C])
        stats = sb("stats", [P, 2, 6])
        mean_var = sb("mean_var", [P, 2, 2])
        rstd = sb("rstd", [P, 2, 2])
        minus_half = sb("minus_half", [P, 2])
        x_hat = sb("x_hat", [P, 2, MOD_WIDTH])
        h_full = sb("h_full", [P, 3, T])
        h_att = [sb(f"h_att{i}", [P, 3 - i, T], F32R) for i in range(2)]
        h_mlp = [sb(f"h_mlp{i}", [P, 3 - i, T], F32R) for i in range(2)]
        qk = [sb(f"qk{i}", [QK_ROWS, QK_TILES, T], F32R) for i in range(2)]
        q_stack = sb("q_stack", [P, H // 2, T], F32R)
        k_stack = sb("k_stack", [P, H // 2, T], F32R)
        v_sb = sb("v_sb", [P, 2, H, 32])
        maxima = sb("maxima", [P, 2, 2, H // 2])
        neg_max = sb("neg_max", [H, T], F32R)
        probs = sb("probs", [P, 4, 2, 2, T])
        o_full = sb("o_full", [P, 2, 512])
        sums = sb("sums", [P, 32])
        inv_few = sb("inv_few", [P, 32])
        inv_sum = sb("inv_sum", [P, 2, 512])
        o_att = [sb(f"o_att{i}", [P, 2, 512], F32R) for i in range(2)]
        g_full = sb("g_full", [P, 2, 512])
        hidden = [sb(f"hidden{i}", [P, NF, T], F32R) for i in range(2)]

        scores = [ctx.enter_context(nc.psum_tensor(f"scores{i}", [P, 2, 2, T], F32)) for i in range(2)]
        pv_ps = ctx.enter_context(nc.psum_tensor("pv_ps", [P, 512], F32))
        mlp2_ps = ctx.enter_context(nc.psum_tensor("mlp2_ps", [P, 512], F32))
        att_ps = ctx.enter_context(nc.psum_tensor("att_ps", [P, 512], F32))
        mlp_ps = ctx.enter_context(nc.psum_tensor("mlp_ps", [P, 512], F32))
        qk_bank = (att_ps, mlp_ps, att_ps)
        token_bank = (mlp_ps, mlp2_ps)
        up_bank = (mlp_ps, mlp2_ps)

        s_init = sem("s_init")
        s_kinit = sem("s_kinit")
        s_half = sem("s_half")
        s_stage = [sem(f"s_stage{n}") for n in range(SLOTS)]
        s_w_high = sem("s_w_high")
        s_w_low = sem("s_w_low")
        s_xin = sem("s_xin")
        s_xmid = sem("s_xmid")
        s_gate_a = sem("s_gate_a")
        s_gate_f = sem("s_gate_f")
        s_stats = [sem("s_stats_a"), sem("s_stats_m")]
        s_var = [sem("s_var_a"), sem("s_var_m")]
        s_rstd = [sem("s_rstd_a"), sem("s_rstd_m")]
        s_pow = [sem("s_pow_a"), sem("s_pow_m")]
        s_xhat_a = sem("s_xhat_a")
        s_xhat_m = sem("s_xhat_m")
        s_tr_a = sem("s_tr_a")
        s_tr_m = sem("s_tr_m")
        s_h_a = sem("s_h_a")
        s_h_m = sem("s_h_m")
        s_hhi_a = sem("s_hhi_a")
        s_hhi_m = sem("s_hhi_m")
        s_hlo_a = sem("s_hlo_a")
        s_hlo_m = sem("s_hlo_m")
        s_qk_ps = sem("s_qk_ps")
        s_qk_hi = sem("s_qk_hi")
        s_qk_lo = sem("s_qk_lo")
        s_qk_st = sem("s_qk_st")
        s_stack = sem("s_stack")
        s_v_ps = sem("s_v_ps")
        s_v = sem("s_v")
        s_score = sem("s_score")
        s_max = sem("s_max")
        s_max_ps = sem("s_max_ps")
        s_neg = sem("s_neg")
        s_neg_st = sem("s_neg_st")
        s_st = sem("s_st")
        s_exp = sem("s_exp")
        s_pv = sem("s_pv")
        s_o_full = sem("s_o_full")
        s_sum = sem("s_sum")
        s_inv = sem("s_inv")
        s_inv_st = sem("s_inv_st")
        s_inv_ld = sem("s_inv_ld")
        s_o = sem("s_o")
        s_o_lo = sem("s_o_lo")
        s_proj = sem("s_proj")
        s_proj_gated = sem("s_proj_gated")
        s_x_one = sem("s_x_one")
        s_up = sem("s_up")
        s_gelu = sem("s_gelu")
        s_g_lo = sem("s_g_lo")
        s_down = sem("s_down")
        s_down_gated = sem("s_down_gated")
        s_x_out = sem("s_x_out")
        s_x_st = sem("s_x_st")
        s_tick = [sem("s_tick_sp"), sem("s_tick_pool"), sem("s_tick_dve")]

        block = ctx.enter_context(nc.Block())

        PRE_EXP, PRE_PV, G_PRE, PRE2, PRE = 2, 2, 2, 2, 1
        TRS = 2

        def piece(name, high, low, low_rows, view, rows, cols):
            return dict(name=name, high=high, low=low, low_rows=low_rows, view=view, rows=rows, cols=cols)

        def chunks(name, pair, c, cols):
            if c < 2:
                return piece(name, pair[0][:, c, cols], pair[1][:, c, cols], slice(0, P), (slice(0, P), c, cols), P,
                             cols.stop - cols.start)
            stack = pair[0][0:STACK, 2, cols]
            return piece(name, stack, stack, STACK_LOW, (slice(0, STACK), 2, cols), STACK, cols.stop - cols.start)

        def groups(name, pair, n, size):
            g = slice(size * n, size * n + size)
            return piece(name, pair[0][:, g, :], pair[1][:, g, :], slice(0, P), (slice(0, P), g, slice(0, C)), P, size * C)

        pieces = [chunks("w_in", w_in, c, slice(0, 3 * C)) for c in range(NCH)]
        pieces += [groups("w_out", w_out, n, 2) for n in range(2)]
        pieces += [chunks("w_up", w_up, c, slice(n * 576, n * 576 + 576)) for c in range(NCH) for n in range(2)]
        pieces += [groups("w_down", w_down, n, 3) for n in range(3)]
        pieces += [piece("b_down", b_down[:, :], b_down[:, :], slice(R // 2, R // 2 + 1), None, R // 2 + 1, C)]
        NP = len(pieces)
        OF = {name: range(a, b) for name, a, b in (("w_in", 0, 3), ("w_out", 3, 5), ("w_up", 5, 11), ("w_down", 11, 15))}

        def staged(n):
            p = pieces[n]
            part = staging[0:p["rows"], n % SLOTS, 0:p["cols"]]
            return part.rearrange("p (a c) -> p a c", c=C) if p["name"] in ("w_out", "w_down") else part

        def whole_run(engine, prologue, half_step, epilogue):
            prologue()
            half_step(0, 0)
            with engine.Fori(0, L - 1) as l:
                half_step(l, 1)
                with engine.Fori(2, B - 2) as b:
                    half_step(l, b)
                half_step(l, B - 2)
                half_step(l, B - 1)
                half_step(l + 1, 0)
            half_step(L - 1, 1)
            with engine.Fori(2, B - 2) as b:
                half_step(L - 1, b)
            half_step(L - 1, B - 2)
            half_step(L - 1, B - 1)
            epilogue()

        def neighbours(l, b):
            start = isinstance(l, int) and isinstance(b, int) and l == 0 and b == 0
            final = isinstance(l, int) and isinstance(b, int) and l == L - 1
            return not start, not (final and b >= B - 1), not (final and b >= B - 2)

        def at(b, n):
            return isinstance(b, int) and b == n

        @block.sync
        def _(sp):
            def hold(semaphore, value):
                sp.wait_ge(semaphore, value)
                sp.sem_inc(s_tick[0], 1)

            sp.sem_inc(s_x_st, 16 * B)
            sp.sem_inc(s_qk_st, 16)
            sp.sem_inc(s_stack, 16)
            sp.dma_start(x_in[:, :, :], dram["out"][0]).then_inc(s_xin, 16)
            qk_rows = dram["qk_scratch"].rearrange("s a b c d t -> s (a b c d) t")
            gate_rows = dram["gate_scratch"].rearrange("l b c -> (l b) c")
            FULL = QK_ROWS * (QK_TILES - 1)

            def load_x_in(it, b):
                hold(s_xhat_a, 4 * it)
                hold(s_x_st, 16 * it + 16)
                sp.dma_start(x_in[:, :, :], dram["out"][b]).then_inc(s_xin, 16)

            def stacks(it):
                for i, made in enumerate((s_qk_hi, s_qk_lo)):
                    hold(made, 3 * it + 3)
                    if i == 0:
                        hold(s_stack, 192 * it + 16)
                    sp.dma_start(qk_rows[i, 0:FULL, :].rearrange("(m p) t -> p m t", p=QK_ROWS),
                                 qk[i][:, 0:QK_TILES - 1, :].bitcast(F32)).then_inc(s_qk_st, 16)
                    sp.dma_start(qk_rows[i, FULL:2 * C, :],
                                 qk[i][0:2 * C - FULL, QK_TILES - 1, :].bitcast(F32)).then_inc(s_qk_st, 16)
                hold(s_qk_st, 64 * it + 80)
                hold(s_st, 8 * it + PRE)
                for n, (stack, order) in enumerate(((q_stack, (0, 1, 0)), (k_stack, (0, 0, 1)))):
                    for par in range(2):
                        for j, part in enumerate(order):
                            row = R * par + HD * j
                            sp.dma_start(stack[row:row + HD, :, :].bitcast(F32),
                                         dram["qk_scratch"][part, n, :, par].rearrange("b d t -> d b t"))\
                              .then_inc(s_stack, 16)

            def negated_maxima(it):
                hold(s_neg, it + 1 + PRE)
                for par in range(2):
                    row = R * par + 3 * HD
                    sp.dma_start(q_stack[row:row + 1, :, :].bitcast(F32),
                                 neg_max[par * 8:par * 8 + 8, :].bitcast(F32)).then_inc(s_neg_st, 16)

            def inverse_sums(it):
                hold(s_o_full, 2 * it + 2 + PRE)
                for i in range(4):
                    sp.dma_start(sums[32 * i:32 * i + 32, :],
                                 o_full[32 * i + HD:32 * i + HD + 1, :, :].rearrange("i h (j e) -> i (h j) e", e=32))\
                      .then_inc(s_sum, 16)
                hold(s_inv, it + 1)
                sp.dma_start(dram["inv_scratch"].rearrange("i (j e) -> (i j) e", e=32), inv_few[:, :])\
                  .then_inc(s_inv_st, 16)
                hold(s_inv_st, 16 * it + 16)
                for i in range(4):
                    sp.dma_start(inv_sum[32 * i:32 * i + 32, :, :].rearrange("d h t -> d (h t)"),
                                 dram["inv_scratch"][i].partition_broadcast(32)).then_inc(s_inv_ld, 16)

            def store(it, b):
                hold(s_x_out, 2 * it + 2 + PRE2)
                sp.dma_start(dram["out"][b], x_out[:, :, :]).then_inc(s_x_st, 16)

            def gate(it, tile, which, signal, free, count):
                hold(free, count)
                row = gate_rows[bass.ds(it, 1), which * C:(which + 1) * C]
                sp.dma_start(tile[:, :], row.rearrange("a c -> (a c)").partition_broadcast(P)).then_inc(signal, 16)

            def prologue():
                load_x_in(1, 1)
                sp.wait_ge(s_kinit, 1)
                stacks(0)

            def half_step(l, b):
                it = l * B + b
                before, after, after_next = neighbours(l, b)
                negated_maxima(it)
                hold(s_x_one, 2 * it + PRE)
                sp.dma_start(x_mid[:, :, :], dram["out"][b]).then_inc(s_xmid, 16)
                gate(it, gate_a, 0, s_gate_a, s_proj_gated, 2 * it + PRE)
                if after_next:
                    load_x_in(it + 2, (b + 2) % B if isinstance(b, int) else b + 2)
                if after:
                    stacks(it + 1)
                inverse_sums(it)
                gate(it, gate_f, 1, s_gate_f, s_down_gated, 2 * it + PRE2)
                if before:
                    store(it - 1, (b - 1) % B if isinstance(b, int) else b - 1)

            def epilogue():
                store(L * B - 1, B - 1)

            whole_run(sp, prologue, half_step, epilogue)
            sp.wait_ge(s_x_st, 16 * B * (L + 1))

        @block.gpsimd
        def _(pool):
            tt = nc.gpsimd.tensor_tensor
            nc.gpsimd.memset(minus_half[:, :], -0.5).then_inc(s_half, 1)
            for sm in (s_x_one, s_o_lo, s_hlo_m):
                pool.sem_inc(sm, PRE)
            pool.sem_inc(s_x_out, PRE2)
            pool.sem_inc(s_g_lo, G_PRE)
            pool.wait_ge(s_half, 1)

            def inverse_deviation(order, it):
                pool.wait_ge(s_var[order], 2 * it + 2)
                pool.sem_inc(s_tick[1], 1)
                nc.gpsimd.tensor_scalar(rstd[:, 0, :], mean_var[:, :, 1], EPS, None, ALU.add).then_inc(s_pow[order], 1)
                pool.wait_ge(s_pow[order], it + 1)
                tt(rstd[:, 1, :], rstd[:, 0, :], minus_half[:, :], ALU.pow).then_inc(s_rstd[order], 1)

            def low(out, full, high, signal):
                tt(out, full, high.bitcast(F32), ALU.subtract).then_inc(signal, 1)

            def stage(l, n):
                src = dram[pieces[n]["name"]][bass.ds(l, 1)]
                if pieces[n]["name"] == "b_down":
                    src = src.rearrange("l p c -> (l p) c")
                else:
                    src = src.rearrange("l p a c -> (l p) a c")[pieces[n]["view"]]
                pool.dma_start(staged(n), src).then_inc(s_stage[n % SLOTS], 16)

            def low_weights(name, l, which=None, last_layer=False):
                for n in OF[name] if which is None else [OF[name][k] for k in which]:
                    p = pieces[n]
                    rows = p["low_rows"]
                    pool.wait_ge(s_w_high, NP * l + n + 1)
                    low(p["low"][rows], staged(n)[rows], p["high"][rows], s_w_low)
                    follower = (l, n + SLOTS) if n + SLOTS < NP else (l + 1, n % SLOTS)
                    pool.wait_ge(s_w_low, NP * l + n + 1)
                    if n + SLOTS < NP or not last_layer:
                        stage(*follower)

            def attention_low(it):
                pool.wait_ge(s_hhi_a, 3 * it + 2)
                low(h_att[1][:, :, :], h_full[:, 0:2, :], h_att[0][:, 0:2, :], s_hlo_a)

            def prologue():
                for n in range(SLOTS):
                    stage(0, n)
                inverse_deviation(0, 0)
                low_weights("w_in", 0)
                attention_low(0)
                inverse_deviation(0, 1)
                low_weights("w_out", 0)
                attention_low(1)

            def half_step(l, b):
                it = l * B + b
                before, after, after_next = neighbours(l, b)
                if before:
                    add_attention(it - 1)
                    inverse_deviation(1, it - 1)
                if at(b, 0) and before:
                    low_weights("w_out", l)
                if at(b, 1):
                    low_weights("w_up", l)
                if before:
                    mlp_low(it - 1)
                if after_next:
                    inverse_deviation(0, it + 2)
                if at(b, 1):
                    low_weights("w_down", l, (0,))
                if before:
                    for n in range(UP_USES):
                        if at(b, 1) and n in (1, 2):
                            low_weights("w_down", l, (1,) if n == 1 else (2, 3), last_layer=isinstance(l, int) and l == L - 1)
                        hidden_low(it - 1, n)
                for half in range(2):
                    pool.wait_ge(s_o, 2 * it + half + 1)
                    low(o_att[1][:, half, :], o_full[:, half, :], o_att[0][:, half, :], s_o_lo)
                if after_next:
                    attention_low(it + 2)
                if at(b, B - 2) and after_next:
                    low_weights("w_in", l + 1)
                if before:
                    add_mlp(it - 1)

            def add_attention(it):
                pool.wait_ge(s_xmid, 16 * it + 16)
                for t in range(2):
                    pool.wait_ge(s_proj_gated, 2 * it + t + 1 + PRE)
                    tt(x_one[:, t, :], x_mid[:, t, :], gated[:, t, :], ALU.add).then_inc(s_x_one, 1)

            def mlp_low(it):
                pool.wait_ge(s_hhi_m, 3 * it + 2)
                low(h_mlp[1][:, :, :], h_full[:, 0:2, :], h_mlp[0][:, 0:2, :], s_hlo_m)

            def hidden_low(it, n):
                tiles = slice(2 * n, min(2 * n + 2, NF))
                width = (tiles.stop - tiles.start) * T
                pool.wait_ge(s_gelu, 2 * (UP_USES * it + n + 1))
                low(hidden[1][:, tiles, :].rearrange("p a t -> p (a t)"), g_full[:, n % 2, 0:width],
                    hidden[0][:, tiles, :].rearrange("p a t -> p (a t)"), s_g_lo)

            def add_mlp(it):
                for t in range(2):
                    pool.wait_ge(s_down_gated, 2 * it + t + 1 + PRE2)
                    if t == 0:
                        pool.wait_ge(s_x_st, 16 * it + 16 * B)
                    tt(x_out[:, t, :], x_one[:, t, :], gated[:, t, :], ALU.add).then_inc(s_x_out, 1)

            def epilogue():
                it = L * B - 1
                add_attention(it)
                inverse_deviation(1, it)
                mlp_low(it)
                for n in range(UP_USES):
                    hidden_low(it, n)
                add_mlp(it)

            whole_run(pool, prologue, half_step, epilogue)

        @block.scalar
        def _(act):
            act.sem_inc(s_exp, PRE_EXP)
            act.sem_inc(s_neg, PRE)
            act.sem_inc(s_neg_st, 16)
            act.sem_inc(s_v, PRE)
            act.sem_inc(s_o_full, PRE)
            evict = nc.scalar.activation

            def high_weights(name, l, which=None):
                for n in OF[name] if which is None else [OF[name][k] for k in which]:
                    act.wait_ge(s_stage[n % SLOTS], 16 * (l * (NP // SLOTS) + n // SLOTS + 1))
                    evict(pieces[n]["high"], staged(n), ACT.Copy).then_inc(s_w_high, 1)

            def attention_modulate(it, chunks, a_before, m_before):
                if 0 in chunks:
                    if a_before is not None:
                        act.wait_ge(s_hlo_a, a_before)
                        act.wait_ge(s_hhi_a, 3 * a_before)
                    if m_before is not None:
                        act.wait_ge(s_hlo_m, m_before + PRE)
                        act.wait_ge(s_hhi_m, 3 * m_before)
                for c in chunks:
                    act.wait_ge(s_tr_a, TRS * it + c // 2 + 1)
                    rows = P if c < 2 else KC
                    evict(h_full[0:rows, c, :], att_ps[0:rows, (c % 2) * T:(c % 2 + 1) * T], ACT.Identity,
                          scale=mods[0:rows, 2, c, bass.ds(it, 1)], bias=mods[0:rows, 0, c, bass.ds(it, 1)])\
                        .then_inc(s_h_a, 1)

            def qk_high(it, n):
                act.wait_ge(s_qk_ps, QK_USES * it + n + 1)
                if n == 0:
                    act.wait_ge(s_qk_st, 64 * it + 16)
                tiles = slice(2 * n, min(2 * n + 2, QK_TILES))
                rows = QK_ROWS if tiles.stop < QK_TILES else 2 * C - QK_ROWS * (QK_TILES - 1)
                width = (tiles.stop - tiles.start) * T
                evict(qk[0][0:rows, tiles, :].rearrange("p a t -> p (a t)"), qk_bank[n][0:rows, 0:width], ACT.Copy)\
                    .then_inc(s_qk_hi, 1)

            def v_evict(it, kt):
                act.wait_ge(s_v_ps, 2 * it + kt + 1 + PRE)
                if kt == 0:
                    act.wait_ge(s_pv, NG * it + PRE_PV)
                evict(v_sb[:, kt, :, 0:HD], att_ps[:, 0:C].rearrange("p (h d) -> p h d", d=HD), ACT.Copy)\
                    .then_inc(s_v, 1)

            def negate_maxima(it):
                act.wait_ge(s_max_ps, it + 1 + PRE)
                act.wait_ge(s_neg_st, 32 * it + 16)
                evict(neg_max[:, :], att_ps[0:H, 0:T], ACT.Copy, scale=-1.0).then_inc(s_neg, 1)

            def exponentials(it, u):
                act.wait_ge(s_st, 8 * it + u + 1 + PRE)
                products = max((u - 4) // 2 + 1, 0)
                act.wait_ge(s_pv, NG * it + products + PRE_PV)
                evict(probs[:, u % 4, :, :, :], scores[u % 2][:, :, :, :], ACT.Exp, scale=SCALE)\
                    .then_inc(s_exp, 1)

            def copy_o(it, half):
                act.wait_ge(s_pv, NG * it + 2 * half + 2 + PRE_PV)
                act.wait_ge(s_o_lo, 2 * it + PRE)
                evict(o_full[:, half, :], pv_ps[:, :], ACT.Copy).then_inc(s_o_full, 1)

            def gelu(it, n):
                act.wait_ge(s_up, UP_USES * it + n + 1 + PRE)
                act.wait_ge(s_g_lo, UP_USES * it + max(n - 1, 0) + G_PRE)
                if n == 0:
                    act.wait_ge(s_down, 2 * it + PRE)
                tiles = slice(2 * n, min(2 * n + 2, NF))
                width = (tiles.stop - tiles.start) * T
                bank = up_bank[n % 2]
                evict(g_full[:, n % 2, 0:width], bank[:, 0:width], ACT.Gelu_apprx_tanh).then_inc(s_gelu, 1)
                evict(hidden[0][:, tiles, :].rearrange("p a t -> p (a t)"), bank[:, 0:width], ACT.Gelu_apprx_tanh)\
                    .then_inc(s_gelu, 1)

            def prologue():
                high_weights("w_in", 0)
                attention_modulate(0, (0, 1, 2), None, None)
                for n in range(QK_USES):
                    qk_high(0, n)
                act.wait_ge(s_init, 4)
                for kt in range(2):
                    v_evict(0, kt)
                attention_modulate(1, (0, 1, 2), 1, None)
                high_weights("w_out", 0)

            def half_step(l, b):
                it = l * B + b
                before, after, after_next = neighbours(l, b)
                negate_maxima(it)
                for n in range(3):
                    if after:
                        qk_high(it + 1, n)
                    if n < 2:
                        if at(b, 1):
                            high_weights("w_up", l, (n + 1,))
                        exponentials(it, n)
                for u in range(2, 5):
                    exponentials(it, u)
                    if at(b, 0) and before and u == 3:
                        act.wait_ge(s_proj, 2 * it + PRE)
                        high_weights("w_out", l)
                    if at(b, 1):
                        high_weights("w_up", l, (u + 1,))
                exponentials(it, 5)
                copy_o(it, 0)
                exponentials(it, 6)
                if at(b, 1):
                    act.wait_ge(s_down, 2 * it - 2 + PRE)
                    high_weights("w_down", l, (0,))
                exponentials(it, 7)
                copy_o(it, 1)
                if after:
                    v_evict(it + 1, 0)
                if before:
                    gelu(it - 1, 0)
                if after:
                    v_evict(it + 1, 1)
                if before:
                    for n in range(1, UP_USES):
                        if at(b, 1) and n in (1, 2):
                            high_weights("w_down", l, (1,) if n == 1 else (2, 3))
                        gelu(it - 1, n)
                if after_next:
                    attention_modulate(it + 2, (0, 1, 2), None if before else it + 2, it if before else None)
                if at(b, B - 2) and after_next:
                    high_weights("w_in", l + 1)
                if at(b, 0):
                    high_weights("w_up", l, (0,))

            def epilogue():
                it = L * B - 1
                for n in range(UP_USES):
                    gelu(it, n)

            whole_run(act, prologue, half_step, epilogue)

        @block.tensor
        def _(pe):
            mm = nc.tensor.matmul
            pe.sem_inc(s_st, PRE)
            pe.sem_inc(s_down, PRE)
            pe.sem_inc(s_pv, PRE_PV)
            for sm in (s_v_ps, s_up, s_max_ps, s_proj):
                pe.sem_inc(sm, PRE)
            pe.sem_inc(s_tr_m, PRE)
            pe.wait_ge(s_init, 3)

            def split(out, high, low_part, weights, steps, start=True, stop=True):
                n, total = 0, 3 * len(steps)
                for s in steps:
                    a, c = s
                    for left, w in ((high, 0), (high, 1), (low_part, 0)):
                        last = mm(out, a(left), c(weights[w]), start=start and n == 0, stop=stop and n == total - 1)
                        n += 1
                return last

            def channel_steps(w, h):
                for c in range(2):
                    for i, j in ((0, 0), (0, 1), (1, 0)):
                        yield w[i][:, c, :], h[j][:, c, :]
                yield w[0][0:STACK, 2, :], h[0][0:STACK, 2, :]

            def transposes(it, bank, chunks, done):
                for c in chunks:
                    for t in range(2):
                        width = P if c < 2 else KC
                        last = nc.tensor.transpose(bank[0:width, (c % 2) * T + t * P:(c % 2) * T + (t + 1) * P],
                                                   x_hat[:, t, c * P:c * P + width], ident[:, :])
                last.then_inc(done, 1)

            def attention_transposes(it, use, v_before=True):
                if use == 0:
                    pe.wait_ge(s_xhat_a, 4 * it + 4)
                    if v_before:
                        pe.wait_ge(s_v, 2 * it + PRE)
                    transposes(it, att_ps, (0, 1), s_tr_a)
                else:
                    pe.wait_ge(s_h_a, NCH * it + 2)
                    transposes(it, att_ps, (2,), s_tr_a)

            def mlp_transposes(it, use, qk_between):
                if use == 0:
                    pe.wait_ge(s_xhat_m, 4 * it + 4)
                    if qk_between:
                        pe.wait_ge(s_qk_lo, QK_USES * (it + 2) + 2)
                    else:
                        pe.wait_ge(s_proj_gated, 2 * it + 2 + PRE)
                    transposes(it, mlp_ps, (0, 1), s_tr_m)
                else:
                    pe.wait_ge(s_h_m, NCH * it + 2)
                    transposes(it, mlp_ps, (2,), s_tr_m)

            def qk_tiles(it, n, m_between=True):
                if n == 0:
                    pe.wait_ge(s_hlo_a, it + 1)
                    pe.wait_ge(s_hhi_a, 3 * it + 3)
                    pe.wait_ge(s_neg, it + PRE)
                    pe.wait_ge(s_h_a, NCH * it + NCH)
                elif n == 1:
                    if m_between:
                        pe.wait_ge(s_proj_gated, 2 * it - 3 + PRE)
                    elif it > 0:
                        pe.wait_ge(s_qk_lo, QK_USES * it)
                else:
                    pe.wait_ge(s_qk_lo, QK_USES * it + 1)
                for m in range(2 * n, min(2 * n + 2, QK_TILES)):
                    cols = slice(m * QK_ROWS, min((m + 1) * QK_ROWS, 2 * C))
                    for count, (w, h) in enumerate(channel_steps(w_in, h_att)):
                        last = mm(qk_bank[n][0:cols.stop - cols.start, (m % 2) * T:(m % 2 + 1) * T], w[:, cols], h,
                                  start=count == 0, stop=count == 6)
                last.then_inc(s_qk_ps, 1)

            def values(it, kt):
                if kt == 0:
                    pe.wait_ge(s_qk_lo, QK_USES * it + QK_USES)
                else:
                    pe.wait_ge(s_v, 2 * it + 1 + PRE)
                for count, (w, h) in enumerate(channel_steps(w_in, h_att)):
                    last = mm(att_ps[:, 0:C], h[:, kt * P:(kt + 1) * P], w[:, 2 * C:3 * C],
                              start=count == 0, stop=count == 6)
                last.then_inc(s_v_ps, 1)

            def score_unit(it, u):
                if u == 0:
                    pe.wait_ge(s_stack, 192 * it + 192 + 16)
                if u < 2:
                    pe.wait_ge(s_exp, 8 * it - 1 + u + PRE_EXP)
                else:
                    pe.wait_ge(s_max, 8 * it + u - 1)
                for par in range(2):
                    r = slice(R * par, R * par + 3 * HD)
                    for qt in range(2):
                        last = mm(scores[u % 2][:, par, qt, :], q_stack[r, u, qt * P:(qt + 1) * P],
                                  k_stack[r, u, :], start=True, stop=True)
                last.then_inc(s_score, 1)

            def maxima_transposes(it, after):
                pe.wait_ge(s_max, 8 * it + 8)
                pe.wait_ge(s_h_a, NCH * (it + 2 if after else it + 1))
                pe.wait_ge(s_v, 2 * it + 2 + PRE)
                for qt in range(2):
                    last = nc.tensor.transpose(att_ps[0:H, qt * P:(qt + 1) * P],
                                               maxima[:, qt, :, :].rearrange("p a b -> p (a b)"), ident[:, :])
                last.then_inc(s_max_ps, 1)

            def shifted_unit(it, u):
                if u == 0:
                    pe.wait_ge(s_neg_st, 32 * it + 32 + 16)
                if u >= 2:
                    pe.wait_ge(s_exp, 8 * it + u - 1 + PRE_EXP)
                for par in range(2):
                    r = slice(R * par, R * par + 3 * HD + 1)
                    for kt in range(2):
                        last = mm(scores[u % 2][:, par, kt, :], k_stack[r, u, kt * P:(kt + 1) * P],
                                  q_stack[r, u, :], start=True, stop=True)
                last.then_inc(s_st, 1)

            def weighted_values(it, g):
                pe.wait_ge(s_exp, 8 * it + 2 * g + 2 + PRE_EXP)
                if g == 0:
                    pe.wait_ge(s_v, 2 * it + 2 + PRE)
                pe.wait_ge(s_o_full, 2 * it + g // 2 + PRE)
                for kt in range(2):
                    for i in range(4):
                        u = 2 * g + i // 2
                        last = mm(pv_ps[32 * i:32 * i + 32, (g % 2) * T:(g % 2 + 1) * T], v_sb[:, kt, 4 * g + i, :],
                                  probs[:, u % 4, i % 2, kt, :], start=kt == 0, stop=kt == 1, tile_position=(0, 32 * i))
                last.then_inc(s_pv, 1)

            def projection(it, t):
                if t == 0:
                    pe.wait_ge(s_o_lo, 2 * it + 2 + PRE)
                pe.wait_ge(s_down_gated, 2 * it - 1 + t + PRE2)
                split(token_bank[t][:, 0:C], o_att[0], o_att[1], w_out,
                      [(lambda o, g=g: o[:, g // 2, (g % 2) * T + t * P:(g % 2) * T + (t + 1) * P],
                        lambda w, g=g: w[:, g, :]) for g in range(NG)]).then_inc(s_proj, 1)

            def up(it, n):
                if n == 0:
                    pe.wait_ge(s_hlo_m, it + 1 + PRE)
                    pe.wait_ge(s_hhi_m, 3 * it + 3)
                    pe.wait_ge(s_h_m, NCH * it + NCH)
                elif n == 1:
                    pe.wait_ge(s_proj_gated, 2 * it + 2 + PRE)
                else:
                    pe.wait_ge(s_gelu, 2 * (UP_USES * it + n - 1))
                for m in range(2 * n, min(2 * n + 2, NF)):
                    for count, (w, h) in enumerate(channel_steps(w_up, h_mlp)):
                        last = mm(up_bank[n % 2][:, (m % 2) * T:(m % 2 + 1) * T], w[:, m * P:(m + 1) * P], h,
                                  start=count == 0, stop=count == 6)
                last.then_inc(s_up, 1)

            def down(it, t, part):
                tiles = range(0, 6) if part == 0 else range(6, NF)
                if part == 0:
                    pe.wait_ge(s_gelu, 2 * (UP_USES * it + UP_USES))
                    pe.wait_ge(s_g_lo, UP_USES * it + 3 + G_PRE)
                    mm(token_bank[t][:, 0:C], ones[:, :], b_down[:, :], start=True, stop=False)
                else:
                    pe.wait_ge(s_g_lo, UP_USES * it + UP_USES + G_PRE)
                last = split(token_bank[t][:, 0:C], hidden[0], hidden[1], w_down,
                             [(lambda h, m=m: h[:, m, t * P:(t + 1) * P], lambda w, m=m: w[:, m, :]) for m in tiles],
                             start=False, stop=part == 1)
                if part == 1:
                    last.then_inc(s_down, 1)

            def weights_ready(name, l):
                pe.wait_ge(s_w_low, NP * l + OF[name].stop)

            def prologue():
                weights_ready("w_in", 0)
                attention_transposes(0, 0, v_before=False)
                attention_transposes(0, 1)
                for n in range(QK_USES):
                    qk_tiles(0, n, m_between=False)
                values(0, 0)
                values(0, 1)
                attention_transposes(1, 0)
                attention_transposes(1, 1)
                for u in range(8):
                    score_unit(0, u)

            def half_step(l, b):
                it = l * B + b
                before, after, after_next = neighbours(l, b)
                if before:
                    if at(b, 1):
                        weights_ready("w_out", l)
                    projection(it - 1, 0)
                maxima_transposes(it, after)
                if before:
                    projection(it - 1, 1)
                if after and at(b, B - 1):
                    weights_ready("w_in", l + 1)
                for n in range(3):
                    if after:
                        qk_tiles(it + 1, n, m_between=before)
                    shifted_unit(it, n)
                shifted_unit(it, 3)
                weighted_values(it, 0)
                shifted_unit(it, 4)
                shifted_unit(it, 5)
                weighted_values(it, 1)
                if before:
                    mlp_transposes(it - 1, 0, after)
                shifted_unit(it, 6)
                if after:
                    values(it + 1, 0)
                shifted_unit(it, 7)
                if before:
                    mlp_transposes(it - 1, 1, after)
                weighted_values(it, 2)
                weighted_values(it, 3)
                m = it - 1
                if before:
                    if at(b, 1):
                        weights_ready("w_up", l)
                    up(m, 0)
                if after:
                    values(it + 1, 1)
                work = []
                if before:
                    work = [lambda: None, lambda: up(m, 1), lambda: up(m, 2), lambda: up(m, 3), lambda: up(m, 4)]
                for n, w in enumerate(work):
                    w()
                    if n >= 1 and after:
                        score_unit(it + 1, n - 1)
                if after and not before:
                    for u in range(4):
                        score_unit(it + 1, u)
                if before and at(b, 1):
                    weights_ready("w_down", l)
                if after_next:
                    attention_transposes(it + 2, 0)
                if after:
                    score_unit(it + 1, 4)
                if before:
                    down(m, 0, 0)
                if after:
                    score_unit(it + 1, 5)
                if after_next:
                    attention_transposes(it + 2, 1)
                if before:
                    down(m, 0, 1)
                if after:
                    score_unit(it + 1, 6)
                if before:
                    down(m, 1, 0)
                if after:
                    score_unit(it + 1, 7)
                if before:
                    down(m, 1, 1)

            def epilogue():
                it = L * B - 1
                projection(it, 0)
                projection(it, 1)
                mlp_transposes(it, 0, False)
                mlp_transposes(it, 1, False)
                for n in range(UP_USES):
                    up(it, n)
                for t in range(2):
                    down(it, t, 0)
                    down(it, t, 1)

            whole_run(pe, prologue, half_step, epilogue)

        @block.vector
        def _(dve):
            tt = nc.vector.tensor_tensor
            nc.vector.memset(ones[:, :].bitcast(F32), 1.0).then_inc(s_init, 1)
            nc.vector.memset(h_att[0][:, 2, :].bitcast(F32), 1.0).then_inc(s_init, 1)
            nc.vector.memset(h_mlp[0][:, 2, :].bitcast(F32), 1.0).then_inc(s_init, 1)
            dve.sem_inc(s_proj_gated, PRE)
            dve.sem_inc(s_down_gated, PRE2)

            def norm(order, it, x_tile, ready, done):
                for t in range(2):
                    if ready:
                        ready(t)
                    nc.vector.bn_stats(out=stats[:, t, :], in_=x_tile[:, t, :]).then_inc(s_stats[order], 1)
                for t in range(2):
                    dve.wait_ge(s_stats[order], 2 * it + t + 1)
                    dve.sem_inc(s_tick[2], 1)
                    nc.vector.bn_aggr(out=mean_var[:, t, :], in_=stats[:, t, :]).then_inc(s_var[order], 1)

            def x_hats(order, it, x_tile, done):
                dve.wait_ge(s_var[order], 2 * it + 2)
                dve.wait_ge(s_rstd[order], it + 1)
                for t in range(2):
                    for out, part in ((x_hat[:, t, 0:C], x_tile[:, t, :]),
                                      (x_hat[:, t, C:MOD_WIDTH].rearrange("p (n c) -> p n c", n=2),
                                       x_tile[:, t, 2 * P:C].unsqueeze(1).to_broadcast([P, 2, C - 2 * P]))):
                        nc.vector.tensor_scalar(out, part, mean_var[:, t, 0:1], rstd[:, 1, t:t + 1],
                                                ALU.subtract, ALU.mult).then_inc(done, 1)

            def attention_norm(it):
                def ready(t):
                    if t == 0:
                        dve.wait_ge(s_xin, 16 * it + 16)
                norm(0, it, x_in, ready, s_xhat_a)

            def high(h, it, done):
                low_rows = slice(C - 2 * P, 2 * (C - 2 * P))
                nc.vector.tensor_copy(h[0:KC, 2, :], h_full[0:KC, 2, :]).then_inc(done, 1)
                nc.vector.tensor_copy(h[:, 0:2, :], h_full[:, 0:2, :]).then_inc(done, 1)
                dve.wait_ge(done, 3 * it + 1)
                tt(h[low_rows, 2, :], h_full[low_rows, 2, :], h[low_rows, 2, :].bitcast(F32), ALU.subtract)\
                    .then_inc(done, 1)

            def attention_high(it):
                dve.wait_ge(s_h_a, NCH * it + NCH)
                dve.wait_ge(s_v_ps, 2 * it + PRE)
                high(h_att[0], it, s_hhi_a)

            def qk_low(it, n):
                dve.wait_ge(s_qk_hi, QK_USES * it + n + 1)
                tiles = slice(2 * n, min(2 * n + 2, QK_TILES))
                rows = QK_ROWS if tiles.stop < QK_TILES else 2 * C - QK_ROWS * (QK_TILES - 1)
                width = (tiles.stop - tiles.start) * T
                tt(qk[1][0:rows, tiles, :].rearrange("p a t -> p (a t)"), qk_bank[n][0:rows, 0:width],
                   qk[0][0:rows, tiles, :].rearrange("p a t -> p (a t)").bitcast(F32), ALU.subtract)\
                    .then_inc(s_qk_lo, 1)

            def unit_max(it, u):
                dve.wait_ge(s_score, 8 * it + u + 1)
                if u == 0:
                    dve.wait_ge(s_max_ps, it + PRE)
                nc.vector.tensor_reduce(out=maxima[:, :, :, u].rearrange("p q r -> p r q"), in_=scores[u % 2][:, :, :, :],
                                        axis=AX.X, op=ALU.max).then_inc(s_max, 1)

            def inverse(it):
                dve.wait_ge(s_sum, 64 * it + 64)
                nc.vector.reciprocal(inv_few[:, :], sums[:, :]).then_inc(s_inv, 1)

            def normalise(it):
                dve.wait_ge(s_inv_ld, 64 * it + 64)
                dve.wait_ge(s_proj, 2 * it + PRE)
                for half in range(2):
                    for out in (o_att[0], o_full):
                        last = tt(out[:, half, :], o_full[:, half, :], inv_sum[:, half, :], ALU.mult)
                    last.then_inc(s_o, 1)

            def gate_projection(it):
                dve.wait_ge(s_gate_a, 16 * it + 16)
                for t in range(2):
                    dve.wait_ge(s_proj, 2 * it + t + 1 + PRE)
                    dve.wait_ge(s_x_out, 2 * it - 1 + t + PRE2)
                    tt(gated[:, t, :], token_bank[t][:, 0:C], gate_a[:, :], ALU.mult).then_inc(s_proj_gated, 1)

            def mlp_norm(it):
                norm(1, it, x_one, lambda t: dve.wait_ge(s_x_one, 2 * it + t + 1 + PRE), s_xhat_m)

            def mlp_modulate(it, h_before):
                dve.wait_ge(s_hlo_a, h_before)
                for c in range(NCH):
                    dve.wait_ge(s_tr_m, TRS * it + c // 2 + 1 + PRE)
                    rows = P if c < 2 else KC
                    dve.sem_inc(s_tick[2], 1)
                    nc.vector.tensor_scalar(h_full[0:rows, c, :], mlp_ps[0:rows, (c % 2) * T:(c % 2 + 1) * T],
                                            mods[0:rows, 3, c, bass.ds(it, 1)], mods[0:rows, 1, c, bass.ds(it, 1)],
                                            ALU.mult, ALU.add).then_inc(s_h_m, 1)

            def mlp_high(it):
                dve.wait_ge(s_h_m, NCH * it + NCH)
                dve.wait_ge(s_up, UP_USES * it + PRE)
                high(h_mlp[0], it, s_hhi_m)

            def gate_down(it, t):
                if t == 0:
                    dve.wait_ge(s_gate_f, 16 * it + 16)
                dve.wait_ge(s_down, 2 * it + t + 1 + PRE)
                tt(gated[:, t, :], token_bank[t][:, 0:C], gate_f[:, :], ALU.mult).then_inc(s_down_gated, 1)

            def prologue():
                attention_norm(0)
                x_hats(0, 0, x_in, s_xhat_a)
                nc.vector.memset(v_sb[:, :, :, :], 1.0).then_inc(s_init, 1)
                nc.vector.memset(k_stack[:, :, :].bitcast(F32), 1.0).then_inc(s_kinit, 1)
                attention_high(0)
                for n in range(QK_USES):
                    qk_low(0, n)
                attention_norm(1)
                dve.wait_ge(s_tr_a, TRS)
                x_hats(0, 1, x_in, s_xhat_a)
                attention_high(1)
                for u in range(8):
                    unit_max(0, u)

            def half_step(l, b):
                it = l * B + b
                before, after, after_next = neighbours(l, b)
                if before:
                    gate_projection(it - 1)
                    mlp_norm(it - 1)
                if after:
                    qk_low(it + 1, 0)
                if before:
                    dve.wait_ge(s_tr_a, TRS * (it + 2 if after else it + 1))
                    x_hats(1, it - 1, x_one, s_xhat_m)
                if after:
                    qk_low(it + 1, 1)
                    qk_low(it + 1, 2)
                if before:
                    mlp_modulate(it - 1, it + 2 if after else it + 1)
                    mlp_high(it - 1)
                if after_next:
                    attention_norm(it + 2)
                if after_next:
                    dve.wait_ge(s_tr_a, TRS * (it + 2))
                    dve.wait_ge(s_tr_m, TRS * it + PRE)
                    x_hats(0, it + 2, x_in, s_xhat_a)
                inverse(it)
                for u in range(8):
                    if u == 5:
                        normalise(it)
                    if u == 7 and after_next:
                        attention_high(it + 2)
                    if u == 7 and before:
                        gate_down(it - 1, 0)
                    if after:
                        unit_max(it + 1, u)
                if before:
                    gate_down(it - 1, 1)

            def epilogue():
                it = L * B - 1
                gate_projection(it)
                mlp_norm(it)
                dve.wait_ge(s_tr_a, TRS * (it + 1))
                x_hats(1, it, x_one, s_xhat_m)
                mlp_modulate(it, it + 1)
                mlp_high(it)
                gate_down(it, 0)
                gate_down(it, 1)

            whole_run(dve, prologue, half_step, epilogue)


def _in_chunks(np, weight, bias):
    n = weight.shape[1]
    out = np.zeros((KC + 1, NCH, n), weight.dtype)
    out[0:KC] = weight.reshape(NCH, KC, n).transpose(1, 0, 2)
    out[KC, NCH - 1] = bias
    return out


def _stacked(np, weight, bias):
    tail = weight[2 * P:]
    out = np.zeros((P, 3, weight.shape[1]), weight.dtype)
    out[:, 0], out[:, 1] = weight[0:P], weight[P:2 * P]
    out[0:STACK, 2] = np.concatenate([tail, tail, tail, bias[None], bias[None]])
    return out


def _modulation(np, weight, bias):
    columns = []
    for k in MOD_KINDS:
        columns += list(range(k * C, k * C + 2 * P)) + 3 * list(range(k * C + 2 * P, (k + 1) * C))
    columns += list(range(2 * C, 3 * C)) + list(range(5 * C, 6 * C))
    return _in_chunks(np, weight[:, columns], bias[columns])


def _by_head(np, weight, bias):
    out = np.zeros((P, NG, C), weight.dtype)
    for g in range(NG):
        for i in range(4):
            out[32 * i:32 * i + HD, g] = weight[(4 * g + i) * HD:(4 * g + i + 1) * HD]
    out[HD, 0] = bias
    return out


_LAYERS = [
    dict(qkv=("L1_cond_W_qkv", "L1_cond_b_qkv"), out=("L1_cond_W_proj", "L1_cond_b_proj"),
         up=("L1_cond_W_fc1", "L1_cond_b_fc1"), down=("L1_cond_W_fc2", "L1_cond_b_fc2"),
         ada=("L1_cond_W_ada", "L1_cond_b_ada")),
    dict(qkv=("L2_cond_qkv_w", "L2_cond_qkv_b"), out=("L2_cond_out_w", "L2_cond_out_b"),
         up=("L2_cond_w1", "L2_cond_b1"), down=("L2_cond_w2", "L2_cond_b2"),
         ada=("L2_cond_ada_w", "L2_cond_ada_b")),
    dict(qkv=("L3_cond_w_qkv", "L3_cond_b_qkv"), out=("L3_cond_w_proj", "L3_cond_b_proj"),
         up=("L3_cond_w_fc1", "L3_cond_b_fc1"), down=("L3_cond_w_fc2", "L3_cond_b_fc2"),
         ada=("L3_cond_w_ada", "L3_cond_b_ada")),
]


def _layout(np, inputs):
    a = {k: np.asarray(v) for k, v in inputs.items()}
    f = np.float32
    upper = np.triu_indices(R, k=1)
    index = np.zeros((R, R), np.int64)
    index[upper] = np.arange(len(upper[0]))
    index = index + index.T
    signs = (np.triu(np.ones((R, R)), 1) - np.tril(np.ones((R, R)), -1)) * 2.0 ** -SQUARINGS
    b_down = np.zeros((L, R // 2 + 1, C), f)
    for n, w in enumerate(_LAYERS):
        b_down[n, [0, R // 2]] = a[w["down"][1]]
    pick = lambda key, lay: np.stack([lay(np, a[w[key][0]], a[w[key][1]]) for w in _LAYERS])
    return {
        "x": a["x"].reshape(B, 2, P, C).transpose(0, 2, 1, 3),
        "cond_t": a["cond_1152"].T.reshape(NCH, KC, B).transpose(1, 0, 2),
        "p_t": a["L0_cond_P"].T,
        "p_nat": a["L0_cond_P"].reshape(NCH, KC, R).transpose(1, 0, 2),
        "w_rot": _in_chunks(np, a["L0_cond_W"].T[:, index.reshape(-1)], a["L0_cond_b"][index.reshape(-1)]),
        "w_ada": pick("ada", _modulation),
        "w_in": pick("qkv", _stacked),
        "w_out": pick("out", _by_head),
        "w_up": pick("up", _stacked),
        "w_down": np.stack([a[w["down"][0]].reshape(NF, P, C).transpose(1, 0, 2) for w in _LAYERS]),
        "b_down": b_down,
        "ident": np.eye(P, dtype=f),
        "lower": np.stack([np.tril(np.ones((R, R), f), -1), -np.tril(np.ones((R, R), f), -1)], axis=1),
        "skew_mask": np.concatenate([signs, signs]).astype(f),
    }


def build(nc, dram):
    dram["v_scratch"] = nc.dram_tensor("v_scratch", (B, R * R), F32, kind="Internal").ap()
    dram["gate_scratch"] = nc.dram_tensor("gate_scratch", (L, B, 2 * C), F32, kind="Internal").ap()
    dram["qk_scratch"] = nc.dram_tensor("qk_scratch", (2, 2, H // 2, 2, HD, T), F32, kind="Internal").ap()
    dram["inv_scratch"] = nc.dram_tensor("inv_scratch", (4, 2 * 512), F32, kind="Internal").ap()
    with ExitStack() as ctx:
        def sb(name, shape):
            return ctx.enter_context(nc.sbuf_tensor(name, shape, F32))

        keep = {"ident": sb("ident", [P, P]), "mods": sb("mods", [P, 4, 3, L * B])}
        with ExitStack() as inner:
            for name, shape in (("u_twice", [KC, NCH, P]), ("g_rot", [P, NPAIR, C])):
                keep[name] = inner.enter_context(nc.sbuf_tensor(name, shape, F32))
            rotation_setup(nc, dram, keep)
            apply_rotation(nc, dram, keep)
        layers(nc, dram, keep)


def kernel(**inputs):
    import numpy as _np
    import concourse.bacc as _bacc
    from concourse import mybir as _mybir
    from concourse.bass_utils import run_bass_kernel_spmd as _run

    nc = _bacc.Bacc("TRN2", target_bir_lowering=False, num_devices=1)
    arrays, dram = {}, {}
    for name, a in _layout(_np, inputs).items():
        arrays[f"in_{name}"] = _np.ascontiguousarray(a)
        dram[name] = nc.dram_tensor(f"in_{name}", a.shape, _mybir.dt.from_np(a.dtype), kind="ExternalInput").ap()
    dram["out"] = nc.dram_tensor("out_x", (B, P, 2, C), F32, kind="ExternalOutput").ap()
    build(nc, dram)
    r = _run(nc, [arrays], core_ids=[0])
    got = _np.asarray(r.results[0]["out_x"])
    return got.transpose(0, 2, 1, 3).reshape(B, T, C)
```
